# Optimizing a Trainium2 kernel written in Bass

```python
import numpy as np
import jax
import jax.numpy as jnp

def _softmax(x, axis=-1):
    return jax.nn.softmax(x, axis=axis)

def _gelu(x):
    return jax.nn.gelu(x, approximate=True)

def _silu(x):
    return jax.nn.silu(x)

def _sigmoid(x):
    return jax.nn.sigmoid(x)

def _layernorm(x, axis=-1, eps=1e-05):
    m = jnp.mean(x, axis=axis, keepdims=True)
    v = jnp.var(x, axis=axis, keepdims=True)
    return (x - m) / jnp.sqrt(v + eps)

def _scatter_add(tgt, idx, src, axis=0):
    return tgt.at[idx].add(src)

def _segment_sum(src, seg, n):
    return jax.ops.segment_sum(src, seg, n)
kernel_name = 'mk_decoder_preln_d1_seqx_r4_86ef7a'

def setup_inputs(seed: int=0):
    np.random.seed(seed)
    _w = jnp.asarray

    def _rec_inputs():
        import jax
        import jax.numpy as jnp
        _rk = jax.random.key(seed)
        x = 7.22e-05 + 1 * jax.random.normal(jax.random.fold_in(_rk, 1), (16, 128, 1024), jnp.float32)
        _lenS = 128 - jax.random.randint(jax.random.fold_in(_rk, 7), (16,), 0, max(1, 128 // 4) + 1, jnp.int32)
        _lenS2 = 128 - jax.random.randint(jax.random.fold_in(_rk, 8), (16,), 0, max(1, 128 // 4) + 1, jnp.int32)
        _ctx_4096P = jax.random.normal(jax.random.fold_in(_rk, 11), (16, 16, 1024), jnp.float32)
        _ctx_4096c = jax.random.dirichlet(jax.random.fold_in(_rk, 511), 0.3 * jnp.ones((16,), jnp.float32), (16, 128))
        _ctx_4096t = jnp.einsum('bsk,bkd->bsd', _ctx_4096c, _ctx_4096P)
        _ctx_4096t = _ctx_4096t * jax.lax.rsqrt(jnp.mean(jnp.square(_ctx_4096t)) + 1e-12) * 0.953939
        ctx_4096 = 4.13588e-05 + 0.999923 * (_ctx_4096t + 0.3 * jax.random.normal(jax.random.fold_in(_rk, 611), (16, 128, 1024), jnp.float32))
        return (x, ctx_4096)
    x, ctx_4096 = _rec_inputs()

    def _L0_attn_setup():
        import jax, jax.numpy as jnp
        import numpy as np
        SEQ, BATCH, HIDDEN = (512, 1, 1024)
        NUM_HEADS, NUM_KV_HEADS, HEAD_DIM = (32, 8, 128)
        Q_PER_GROUP = NUM_HEADS // NUM_KV_HEADS
        TOTAL_PROJ = NUM_KV_HEADS * (Q_PER_GROUP + 2) * HEAD_DIM
        key = jax.random.key(seed)
        k1, k2, k3 = jax.random.split(key, 3)
        tokens = jax.random.normal(k1, (SEQ, BATCH, HIDDEN), dtype=jnp.float32)
        weight_qkv = jax.random.normal(k2, (TOTAL_PROJ, HIDDEN), dtype=jnp.float32) * (2.0 / (TOTAL_PROJ + HIDDEN)) ** 0.5
        weight_proj = jax.random.normal(k3, (HIDDEN, NUM_HEADS * HEAD_DIM), dtype=jnp.float32) * (2.0 / (HIDDEN + NUM_HEADS * HEAD_DIM)) ** 0.5
        return {'tokens': tokens, 'weight_qkv': weight_qkv, 'weight_proj': weight_proj}
    _L0_attn_all = _L0_attn_setup()
    _L0_attn_in = {k: v for k, v in _L0_attn_all.items() if k in ('weight_qkv', 'weight_proj')}
    del _L0_attn_all

    def _L0_xattn_setup():
        import jax, jax.numpy as jnp
        import numpy as np
        import math
        D_MODEL = 256
        NHEAD = 16
        MAX_SUP = 4
        DK = D_MODEL // NHEAD
        DM = D_MODEL * MAX_SUP
        B, S = (2, 256)
        key = jax.random.key(seed)
        ks = jax.random.split(key, 12)
        std = 0.02
        inp = {'q': jax.random.normal(ks[0], (B, S, DM), jnp.float32), 'k': jax.random.normal(ks[1], (B, S, DM), jnp.float32), 'v': jax.random.normal(ks[2], (B, S, DM), jnp.float32), 'Wq': jax.random.normal(ks[3], (DM, DM), jnp.float32) * std, 'bq': jnp.zeros((DM,), jnp.float32), 'Wk': jax.random.normal(ks[4], (DM, DM), jnp.float32) * std, 'bk': jnp.zeros((DM,), jnp.float32), 'Wv': jax.random.normal(ks[5], (DM, DM), jnp.float32) * std, 'bv': jnp.zeros((DM,), jnp.float32), 'interference': jax.random.normal(ks[6], (NHEAD, MAX_SUP, MAX_SUP), jnp.float32), 'amp': jnp.ones((1,), jnp.float32), 'Wo': jax.random.normal(ks[7], (DM, DM), jnp.float32) * std, 'bo': jnp.zeros((DM,), jnp.float32)}
        return inp
    _L0_xattn_all = _L0_xattn_setup()
    _L0_xattn_in = {k: v for k, v in _L0_xattn_all.items() if k in ('Wq', 'bq', 'Wk', 'bk', 'Wv', 'bv', 'interference', 'amp', 'Wo', 'bo')}
    del _L0_xattn_all

    def _L0_ffn_setup():
        import jax, jax.numpy as jnp
        import numpy as np
        IN, OUT = (1024, 1024)
        R_TOP, R_INT = (64, 4)
        R_TAIL = min(IN, OUT) - R_TOP
        B, S = (4, 256)
        key = jax.random.key(seed)
        ks = jax.random.split(key, 10)
        sc = 1.0 / np.sqrt(OUT)
        x = jax.random.normal(ks[0], (B, S, IN), jnp.float32)
        U_top = jax.random.normal(ks[1], (OUT, R_TOP), jnp.float32) * sc
        Vh_top = jax.random.normal(ks[2], (R_TOP, IN), jnp.float32) * sc
        U_tail = jax.random.normal(ks[3], (OUT, R_TAIL), jnp.float32) * sc
        Vh_tail = jax.random.normal(ks[4], (R_TAIL, IN), jnp.float32) * sc
        S_top = jnp.sort(jax.random.uniform(ks[5], (R_TOP,), jnp.float32, 1.0, 10.0))[::-1]
        S_tail = jnp.sort(jax.random.uniform(ks[6], (R_TAIL,), jnp.float32, 0.01, 1.0))[::-1]
        U_tail_r = U_tail[:, :R_INT]
        S_tail_r = S_tail[:R_INT]
        Vh_tail_r = Vh_tail[:R_INT, :]
        alpha = jnp.ones((R_TOP,), jnp.float32)
        beta = jnp.zeros((R_TOP,), jnp.float32)
        D = jnp.ones((R_INT,), jnp.float32)
        R = jnp.eye(R_INT, dtype=jnp.float32) + 0.01 * jax.random.normal(ks[7], (R_INT, R_INT), jnp.float32)
        bias = jax.random.normal(ks[8], (OUT,), jnp.float32) * 0.02
        return dict(x=x, U_top=U_top, S_top=S_top, Vh_top=Vh_top, U_tail=U_tail, S_tail=S_tail, Vh_tail=Vh_tail, U_tail_r=U_tail_r, S_tail_r=S_tail_r, Vh_tail_r=Vh_tail_r, alpha=alpha, beta=beta, D=D, R=R, bias=bias)
    _L0_ffn_all = _L0_ffn_setup()
    _L0_ffn_in = {k: v for k, v in _L0_ffn_all.items() if k in ('U_top', 'S_top', 'Vh_top', 'U_tail', 'S_tail', 'Vh_tail', 'U_tail_r', 'S_tail_r', 'Vh_tail_r', 'alpha', 'beta', 'D', 'R', 'bias')}
    del _L0_ffn_all
    return {'x': x, 'ctx_4096': ctx_4096, 'L0_attn_weight_qkv': _L0_attn_in['weight_qkv'], 'L0_attn_weight_proj': _L0_attn_in['weight_proj'], 'L0_xattn_Wq': _L0_xattn_in['Wq'], 'L0_xattn_bq': _L0_xattn_in['bq'], 'L0_xattn_Wk': _L0_xattn_in['Wk'], 'L0_xattn_bk': _L0_xattn_in['bk'], 'L0_xattn_Wv': _L0_xattn_in['Wv'], 'L0_xattn_bv': _L0_xattn_in['bv'], 'L0_xattn_interference': _L0_xattn_in['interference'], 'L0_xattn_amp': _L0_xattn_in['amp'], 'L0_xattn_Wo': _L0_xattn_in['Wo'], 'L0_xattn_bo': _L0_xattn_in['bo'], 'L0_ffn_U_top': _L0_ffn_in['U_top'], 'L0_ffn_S_top': _L0_ffn_in['S_top'], 'L0_ffn_Vh_top': _L0_ffn_in['Vh_top'], 'L0_ffn_U_tail': _L0_ffn_in['U_tail'], 'L0_ffn_S_tail': _L0_ffn_in['S_tail'], 'L0_ffn_Vh_tail': _L0_ffn_in['Vh_tail'], 'L0_ffn_U_tail_r': _L0_ffn_in['U_tail_r'], 'L0_ffn_S_tail_r': _L0_ffn_in['S_tail_r'], 'L0_ffn_Vh_tail_r': _L0_ffn_in['Vh_tail_r'], 'L0_ffn_alpha': _L0_ffn_in['alpha'], 'L0_ffn_beta': _L0_ffn_in['beta'], 'L0_ffn_D': _L0_ffn_in['D'], 'L0_ffn_R': _L0_ffn_in['R'], 'L0_ffn_bias': _L0_ffn_in['bias']}

def reference(x, ctx_4096, L0_attn_weight_qkv, L0_attn_weight_proj, L0_xattn_Wq, L0_xattn_bq, L0_xattn_Wk, L0_xattn_bk, L0_xattn_Wv, L0_xattn_bv, L0_xattn_interference, L0_xattn_amp, L0_xattn_Wo, L0_xattn_bo, L0_ffn_U_top, L0_ffn_S_top, L0_ffn_Vh_top, L0_ffn_U_tail, L0_ffn_S_tail, L0_ffn_Vh_tail, L0_ffn_U_tail_r, L0_ffn_S_tail_r, L0_ffn_Vh_tail_r, L0_ffn_alpha, L0_ffn_beta, L0_ffn_D, L0_ffn_R, L0_ffn_bias):
    import jax
    import jax.numpy as jnp

    def _L0_attn_ref(tokens, weight_qkv, weight_proj):
        import jax, jax.numpy as jnp
        import numpy as np
        SEQ, BATCH, HIDDEN = (512, 1, 1024)
        NUM_HEADS, NUM_KV_HEADS, HEAD_DIM = (32, 8, 128)
        Q_PER_GROUP = NUM_HEADS // NUM_KV_HEADS
        TOTAL_PROJ = NUM_KV_HEADS * (Q_PER_GROUP + 2) * HEAD_DIM
        S, B, H = tokens.shape
        scale = 1.0 / HEAD_DIM ** 0.5
        qkv = jnp.einsum('sbh,ph->sbp', tokens, weight_qkv)
        qkv = qkv.reshape(S, B, NUM_KV_HEADS, Q_PER_GROUP + 2, HEAD_DIM)
        q = qkv[:, :, :, :Q_PER_GROUP, :].reshape(S, B, NUM_HEADS, HEAD_DIM)
        k = qkv[:, :, :, Q_PER_GROUP, :]
        v = qkv[:, :, :, Q_PER_GROUP + 1, :]
        k = jnp.repeat(k, Q_PER_GROUP, axis=2)
        v = jnp.repeat(v, Q_PER_GROUP, axis=2)
        q = q.transpose(1, 2, 0, 3)
        k = k.transpose(1, 2, 0, 3)
        v = v.transpose(1, 2, 0, 3)
        scores = jnp.einsum('bhsd,bhtd->bhst', q, k) * scale
        causal = jnp.tril(jnp.ones((S, S), dtype=bool))
        scores = jnp.where(causal, scores, jnp.finfo(scores.dtype).min)
        attn = jax.nn.softmax(scores, axis=-1)
        out = jnp.einsum('bhst,bhtd->bhsd', attn, v)
        out = out.transpose(2, 0, 1, 3).reshape(S, B, NUM_HEADS * HEAD_DIM)
        return jnp.einsum('sbe,he->sbh', out, weight_proj)

    def _L0_xattn_ref(q, k, v, Wq, bq, Wk, bk, Wv, bv, interference, amp, Wo, bo):
        import jax, jax.numpy as jnp
        import numpy as np
        import math
        D_MODEL = 256
        NHEAD = 16
        MAX_SUP = 4
        DK = D_MODEL // NHEAD
        DM = D_MODEL * MAX_SUP
        B, S = (2, 256)
        b, s, dm = q.shape
        H, M = (interference.shape[0], interference.shape[1])
        dk = dm // (H * M)

        def proj(x, W, bias):
            y = x @ W.T + bias
            y = y.reshape(b, s, H, dk, M)
            return jnp.transpose(y, (0, 2, 1, 3, 4))
        qh = proj(q, Wq, bq)
        kh = proj(k, Wk, bk)
        vh = proj(v, Wv, bv)

        def interfere(x):
            return x + 0.1 * amp[0] * jnp.einsum('bhsdi,hij->bhsdj', x, interference)
        qh, kh, vh = (interfere(qh), interfere(kh), interfere(vh))
        scores = jnp.einsum('bhqdm,bhkdm->bhqkm', qh, kh) / math.sqrt(dk)
        weights = jax.nn.softmax(scores, axis=3)
        out = jnp.einsum('bhqkm,bhkdm->bhqdm', weights, vh)
        out = jnp.transpose(out, (0, 2, 1, 3, 4)).reshape(b, s, dm)
        return out @ Wo.T + bo

    def _L0_ffn_ref(x, U_top, S_top, Vh_top, U_tail, S_tail, Vh_tail, U_tail_r, S_tail_r, Vh_tail_r, alpha, beta, D, R, bias):
        import jax, jax.numpy as jnp
        import numpy as np
        IN, OUT = (1024, 1024)
        R_TOP, R_INT = (64, 4)
        R_TAIL = min(IN, OUT) - R_TOP
        B, S = (4, 256)
        s_head = jax.nn.relu(S_top * alpha + beta)
        W_head = U_top * s_head[None, :] @ Vh_top
        W_tail = U_tail * S_tail[None, :] @ Vh_tail
        Bm = U_tail_r * S_tail_r[None, :]
        delta = Bm * jax.nn.relu(D)[None, :] @ R @ Vh_tail_r
        W_eff = W_head + W_tail + delta
        return jnp.einsum('bsi,oi->bso', x, W_eff) + bias
    x = x + _L0_attn_ref(_layernorm(x, axis=-1), L0_attn_weight_qkv, L0_attn_weight_proj)
    x = x + _L0_xattn_ref(_layernorm(x, axis=-1), ctx_4096, ctx_4096, L0_xattn_Wq, L0_xattn_bq, L0_xattn_Wk, L0_xattn_bk, L0_xattn_Wv, L0_xattn_bv, L0_xattn_interference, L0_xattn_amp, L0_xattn_Wo, L0_xattn_bo)
    x = x + _L0_ffn_ref(_layernorm(x, axis=-1), L0_ffn_U_top, L0_ffn_S_top, L0_ffn_Vh_top, L0_ffn_U_tail, L0_ffn_S_tail, L0_ffn_Vh_tail, L0_ffn_U_tail_r, L0_ffn_S_tail_r, L0_ffn_Vh_tail_r, L0_ffn_alpha, L0_ffn_beta, L0_ffn_D, L0_ffn_R, L0_ffn_bias)
    return x

_drawn_inputs = setup_inputs


def setup_inputs(seed=0):
    import zlib

    import numpy as np

    out = dict(_drawn_inputs(seed))
    spreads = {'L0_xattn_bq': (0.0, 0.8),
     'L0_xattn_bk': (0.0, 0.8),
     'L0_xattn_bv': (0.0, 0.1),
     'L0_xattn_bo': (0.0, 0.1),
     'L0_ffn_alpha': (1.0, 0.2),
     'L0_ffn_beta': (0.0, 0.644),
     'L0_ffn_D': (1.0, 0.6)}
    factors = {'L0_ffn_S_tail_r': 8.0, 'L0_ffn_bias': 6.322}
    for name, (base, spread) in spreads.items():
        noise = np.random.default_rng([zlib.crc32(name.encode()), seed]).standard_normal(out[name].shape)
        drawn = base * np.exp(spread * noise) if base else spread * noise
        out[name] = jnp.asarray(drawn.astype(out[name].dtype))
    for name, factor in factors.items():
        out[name] = (out[name] * factor).astype(out[name].dtype)
    return out
```

```python
import numpy as np
import concourse.bass as bass
from concourse import mybir
from contextlib import ExitStack

F32 = mybir.dt.float32
F32R = mybir.dt.float32r
ALU = mybir.AluOpType
ACT = mybir.ActivationFunctionType
AX = mybir.AxisListType

P = 128
D = 1024
KC = D // P
HALF = 512
TOKENS = 2048
TILES = 4
BT = TILES * P
BLOCKS = TOKENS // BT
EPS = 1e-5
MASKED = -1e30

SEQ = 16
KVH = 8
QPG = 4
HD = 128
SELF_SCALE = 1.0 / HD ** 0.5

CH = D // P
SLOTS = 8
DK = 16
MS = 4
CROSS_SCALE = 1.0 / DK ** 0.5
VW = DK + 1

R_TOP = 64
R_INT = 4


def f32(ap):
    return ap.bitcast(F32)


def three_passes(nc, out, parts, first=True, last=True):
    for i, (ah, al, bh, bl) in enumerate(parts):
        nc.tensor.matmul(out, ah, bh, start=(first and i == 0), stop=False)
        nc.tensor.matmul(out, ah, bl, start=False, stop=False)
        ins = nc.tensor.matmul(out, al, bh, start=False, stop=(last and i == len(parts) - 1))
    return ins



def tile_of(array, index):
    return array[bass.ds(index, 1)].rearrange("a p n -> (a p) n")



def setup_phase(nc, sems, ident, causal, slotmask, bias_qkv, w_nat, b_nat, inter_rows, amp_col, w_folded):
    NW = 3 * CH
    with ExitStack() as ctx:
        def sb(name, shape, dt=F32):
            return ctx.enter_context(nc.sbuf_tensor(name, shape, dt))

        def sem(name):
            return sems.enter_context(nc.semaphore(name))

        inter = sb("inter", [P, CH, MS])
        amp = sb("amp", [P, 1])
        amp01 = sb("amp01", [P, 1])
        same_hd = sb("same_hd", [P, 2 * DK])
        same_m = sb("same_m", [P, MS])
        mix_rows = sb("mix_rows", [P, CH, MS])
        mix = sb("mix", [P, CH, 2 * MS * DK])
        bias_raw = sb("bias_raw", [P, CH, 3])
        wraw = sb("set_wraw", [P, 2, D])
        wfold = sb("set_wfold", [P, 2, D])
        fold_ps = [ctx.enter_context(nc.psum_tensor(f"fold_ps{i}", [P, D], F32)) for i in range(2)]
        bias_ps = ctx.enter_context(nc.psum_tensor("bias_ps", [P, HALF], F32))

        small_loaded = sem("set_small_loaded")
        masks_built = sem("set_masks_built")
        mix_steps = sem("set_mix_steps")
        mix_ready = sem("set_mix_ready")
        wraw_loaded = [sem(f"set_wraw_loaded{i}") for i in range(2)]
        folded = sem("set_folded")
        fold_copied = sem("set_fold_copied")
        stored = [sem(f"set_stored{i}") for i in range(2)]
        bias_mixed = sem("set_bias_mixed")
        bias_done = sem("set_bias_done")

        block = ctx.enter_context(nc.Block())

        @block.sync
        def _(sp):
            sp.dma_start(inter[:], inter_rows).then_inc(small_loaded, 16)
            sp.dma_start(amp[:], amp_col).then_inc(small_loaded, 16)
            sp.dma_start(bias_raw[:], b_nat).then_inc(small_loaded, 16)
            for i in range(2):
                sp.dma_start(wraw[:, i], w_nat[i]).then_inc(wraw_loaded[i], 16)
            with sp.Fori(0, NW // 2 - 1) as m:
                for i in range(2):
                    sp.wait_ge(fold_copied, m * 2 + (i + 3))
                    sp.dma_start(tile_of(w_folded, m * 2 + i), wfold[:, i]).then_inc(stored[i], 16)
                    sp.dma_start(wraw[:, i], tile_of(w_nat, m * 2 + (i + 2))).then_inc(wraw_loaded[i], 16)
            for i in range(2):
                sp.wait_ge(fold_copied, NW + 1 + i)
                sp.dma_start(w_folded[NW - 2 + i], wfold[:, i]).then_inc(stored[i], 16)
            for i in range(2):
                sp.wait_ge(stored[i], 16 * (NW // 2 + 1))

        @block.gpsimd
        def _(pool):
            pool.memset(ident[:], 0.0).then_inc(masks_built, 1)
            pool.memset(causal[:], 0.0).then_inc(masks_built, 1)
            pool.memset(same_hd[:], 1.0).then_inc(masks_built, 1)
            pool.memset(slotmask[:], 1.0).then_inc(masks_built, 1)
            pool.wait_ge(masks_built, 4)
            pool.affine_select(out=ident[:], in_=ident[:], compare_op=ALU.not_equal, fill=1.0, base=0,
                               pattern=[[-1, P]], channel_multiplier=1).then_inc(masks_built, 1)
            pool.affine_select(out=causal[:], in_=causal[:], compare_op=ALU.is_ge, fill=MASKED, base=0,
                               pattern=[[-1, P]], channel_multiplier=1).then_inc(masks_built, 1)
            pool.affine_select(out=same_hd[:], in_=same_hd[:], compare_op=ALU.is_ge, fill=0.0, base=0,
                               pattern=[[-MS, 2 * DK]], channel_multiplier=1).then_inc(masks_built, 1)
            pool.affine_select(out=slotmask[:], in_=slotmask[:], compare_op=ALU.is_ge, fill=0.0, base=0,
                               pattern=[[-DK, SLOTS]], channel_multiplier=1).then_inc(masks_built, 1)
            pool.wait_ge(masks_built, 8)
            cv = causal[:].rearrange("p (j i) -> p j i", i=SEQ)
            pool.affine_select(out=cv, in_=cv, compare_op=ALU.is_ge, fill=MASKED, base=SEQ - 1,
                               pattern=[[SEQ, P // SEQ], [0, SEQ]], channel_multiplier=-1).then_inc(masks_built, 1)
            pool.affine_select(out=same_hd[:], in_=same_hd[:], compare_op=ALU.is_ge, fill=0.0, base=MS - 1,
                               pattern=[[MS, 2 * DK]], channel_multiplier=-1).then_inc(masks_built, 1)
            pool.affine_select(out=slotmask[:], in_=slotmask[:], compare_op=ALU.is_ge, fill=0.0, base=DK - 1,
                               pattern=[[DK, SLOTS]], channel_multiplier=-1).then_inc(masks_built, 1)

        @block.vector
        def _(dve):
            dve.wait_ge(masks_built, 11)
            nc.vector.tensor_reduce(same_m[:], ident[:].rearrange("p (k j) -> p j k", j=MS), AX.X,
                                    ALU.add).then_inc(mix_steps, 1)
            dve.wait_ge(small_loaded, 48)
            nc.vector.tensor_scalar(amp01[:], amp[:], 0.1, None, ALU.mult).then_inc(mix_steps, 1)
            dve.wait_ge(mix_steps, 2)
            for c in range(CH):
                ins = nc.vector.scalar_tensor_tensor(mix_rows[:, c], inter[:, c], amp01[:], same_m[:],
                                                     ALU.mult, ALU.add)
            ins.then_inc(mix_steps, 1)
            dve.wait_ge(mix_steps, 3)
            hd = same_hd[:].rearrange("p (h d) -> p h d", h=2)
            mv = mix[:].rearrange("p c (h j d) -> p c h j d", h=2, j=MS)
            for c in range(CH):
                for h in range(2):
                    ins = nc.vector.tensor_tensor(
                        mv[:, c, h], hd[:, h].unsqueeze(1).broadcast_to([P, MS, DK]),
                        mix_rows[:, c].unsqueeze(2).broadcast_to([P, MS, DK]), ALU.mult)
            ins.then_inc(mix_ready, 1)
            dve.wait_ge(bias_mixed, 1)
            nc.vector.tensor_copy(bias_qkv[:].rearrange("p c w -> p (c w)"),
                                  bias_ps[:, 0:CH * 3]).then_inc(bias_done, 1)

        @block.tensor
        def _(pe):
            pe.wait_ge(mix_ready, 1)
            pe.wait_ge(small_loaded, 48)
            for c in range(CH):
                ins = nc.tensor.matmul(bias_ps[:, c * 3:c * 3 + 3], mix[:, c], bias_raw[:, c],
                                       start=True, stop=True)
            ins.then_inc(bias_mixed, 1)
            with pe.Fori(0, 3) as w:
                for c in range(CH):
                    i = c % 2
                    pe.wait_ge(wraw_loaded[i], w * (16 * CH // 2) + 16 * (c // 2 + 1))
                    pe.wait_ge(fold_copied, w * CH + (c + 1))
                    for k in range(KC):
                        ins = nc.tensor.matmul(fold_ps[i][:, k * P:(k + 1) * P], wraw[:, i, k * P:(k + 1) * P],
                                               mix[:, c], start=True, stop=True)
                    ins.then_inc(folded, 1)

        @block.scalar
        def _(act):
            act.sem_inc(fold_copied, 2)
            for i in range(2):
                act.sem_inc(stored[i], 16)
            with act.Fori(0, NW // 2) as m:
                for i in range(2):
                    act.wait_ge(folded, m * 2 + (i + 1))
                    act.wait_ge(stored[i], m * 16 + 16)
                    nc.scalar.activation(wfold[:, i], fold_ps[i][:], ACT.Copy).then_inc(fold_copied, 1)



class NormBuffers:

    def __init__(self, nc, ctx, sems, tag, eps):
        self.nc, self.eps = nc, eps

        def sb(name, shape, dt=F32):
            return ctx.enter_context(nc.sbuf_tensor(f"{tag}_{name}", shape, dt))

        def sem(name):
            return sems.enter_context(nc.semaphore(f"{tag}_{name}"))

        self.stats = sb("stats", [P, TILES, 12])
        self.mv = sb("mv", [P, TILES, 2])
        self.std = sb("std", [P, TILES])
        self.idle = sb("idle", [P, 1])
        self.rstd = sb("rstd", [P, TILES])
        self.xn = sb("xn", [P, 2, D])
        self.xh = sb("xh", [P, KC, BT], F32R)
        self.xl = sb("xl", [P, KC, BT], F32R)
        self.stats_done = sem("stats_done")
        self.moments_done = sem("moments_done")
        self.std_done = sem("std_done")
        self.rstd_done = sem("rstd_done")
        self.xn_ready = sem("xn_ready")
        self.turned = sem("turned")
        self.hi_done = sem("hi_done")

    def moments(self, dve, b, x_tile, loaded, loads):
        nc = self.nc
        for t in range(TILES):
            dve.wait_ge(loaded[t], loads * 16)
            nc.vector.bn_stats(self.stats[:, t, 0:6], x_tile(t)[:, 0:HALF])
            nc.vector.bn_stats(self.stats[:, t, 6:12], x_tile(t)[:, HALF:D]).then_inc(self.stats_done, 1)
            dve.wait_ge(self.stats_done, b * TILES + (t + 1))
            nc.vector.memset(self.idle[:], 0.0)
            nc.vector.bn_aggr(self.mv[:, t], self.stats[:, t]).then_inc(self.moments_done, 1)
        dve.wait_ge(self.std_done, b + 1)
        nc.vector.reciprocal(self.rstd[:], self.std[:]).then_inc(self.rstd_done, 1)
        dve.wait_ge(self.rstd_done, b + 1)

    def normalise(self, dve, b, t, x_tile):
        if t >= 2:
            dve.wait_ge(self.turned, b * 8 + (2 * t - 2))
        self.nc.vector.tensor_scalar(self.xn[:, t % 2], x_tile(t), self.mv[:, t, 0:1], self.rstd[:, t:t + 1],
                                     ALU.subtract, ALU.mult).then_inc(self.xn_ready, 1)

    def deviations(self, act, b):
        act.wait_ge(self.moments_done, b * TILES + TILES)
        self.nc.scalar.activation(self.std[:], self.mv[:, :, 1], ACT.Sqrt, bias=self.eps[:]
                                  ).then_inc(self.std_done, 1)

    def turn(self, pe, b, t, ident, bank, bank_free, count):
        pe.wait_ge(self.xn_ready, b * TILES + (t + 1))
        for q in range(2):
            pe.wait_ge(bank_free, count + (2 * t + q + 1))
            for k in range(4):
                ins = self.nc.tensor.transpose(bank[q][:, k * P:(k + 1) * P],
                                               self.xn[:, t % 2, (4 * q + k) * P:(4 * q + k + 1) * P], ident[:])
            ins.then_inc(self.turned, 1)

    def high(self, act, b, t, bank):
        for q in range(2):
            act.wait_ge(self.turned, b * 8 + (2 * t + q + 1))
            self.nc.scalar.activation(self.xh[:, 4 * q:4 * q + 4, t * P:(t + 1) * P],
                                      bank[q][:].rearrange("p (k n) -> p k n", k=4), ACT.Copy
                                      ).then_inc(self.hi_done, 1)

    def low(self, dve, b, t, bank, bank_free):
        for q in range(2):
            dve.wait_ge(self.hi_done, b * 8 + (2 * t + q + 1))
            self.nc.vector.tensor_tensor(self.xl[:, 4 * q:4 * q + 4, t * P:(t + 1) * P],
                                         bank[q][:].rearrange("p (k n) -> p k n", k=4),
                                         f32(self.xh[:, 4 * q:4 * q + 4, t * P:(t + 1) * P]), ALU.subtract
                                         ).then_inc(bank_free, 1)



def self_attention_phase(nc, sems, ident, causal, eps, x_rows, wqkv, wproj, x1):
    U = 2 + QPG
    PR = TILES * 2
    PR_BLOCK = 8 + KVH * PR
    with ExitStack() as ctx:
        def sb(name, shape, dt=F32):
            return ctx.enter_context(nc.sbuf_tensor(name, shape, dt))

        def bank(name):
            return ctx.enter_context(nc.psum_tensor(name, [P, HALF], F32))

        def sem(name):
            return sems.enter_context(nc.semaphore(name))

        ln = NormBuffers(nc, ctx, sems, "sa_ln", eps)
        xin = sb("sa_xin", [P, TILES, D])
        acc = sb("sa_acc", [P, TILES, D])
        wraw = sb("sa_wraw", [P, 3, D])
        wh = sb("sa_wh", [P, 3, D], F32R)
        wl = sb("sa_wl", [P, 3, D], F32R)
        praw = sb("sa_praw", [P, 2, D])
        ph = sb("sa_ph", [P, QPG, D], F32R)
        pl = sb("sa_pl", [P, QPG, D], F32R)
        kT = sb("sa_kT", [P, 2, BT])
        qT = sb("sa_qT", [P, 2, QPG, BT])
        vT = sb("sa_vT", [P, BT])
        v = sb("sa_v", [P, 2, TILES, HD])
        probs = sb("sa_probs", [P, QPG, P])
        probsT = sb("sa_probsT", [P, QPG * P])
        top = sb("sa_top", [P, QPG])
        total = sb("sa_total", [P, QPG])
        inv = sb("sa_inv", [P, QPG])
        oh = sb("sa_oh", [P, QPG * P], F32R)
        ol = sb("sa_ol", [P, QPG * P], F32R)

        u_ps = [bank(f"sa_u{i}") for i in range(2)]
        pr_ps = [bank(f"sa_pr{i}") for i in range(2)]
        s_ps, t_ps, o_ps, v_ps = bank("sa_s"), bank("sa_t"), bank("sa_o"), bank("sa_vt")

        xin_loaded = [sem(f"sa_xin_loaded{t}") for t in range(TILES)]
        wraw_loaded = [sem(f"sa_wraw_loaded{i}") for i in range(3)]
        praw_loaded = [sem(f"sa_praw_loaded{i}") for i in range(2)]
        x1_stored = [sem(f"sa_x1_stored{t}") for t in range(TILES)]
        acc_loaded = sem("sa_acc_loaded")
        w_hi = sem("sa_w_hi")
        w_split = sem("sa_w_split")
        p_hi = sem("sa_p_hi")
        p_split = sem("sa_p_split")
        u_done = sem("sa_u_done")
        u_copied = sem("sa_u_copied")
        v_turned = sem("sa_v_turned")
        v_copied = sem("sa_v_copied")
        s_done = sem("sa_s_done")
        s_masked = sem("sa_s_masked")
        s_top = sem("sa_s_top")
        s_shifted = sem("sa_s_shifted")
        exp_done = sem("sa_exp_done")
        total_done = sem("sa_total_done")
        inv_done = sem("sa_inv_done")
        probs_ready = sem("sa_probs_ready")
        probs_turned = sem("sa_probs_turned")
        probsT_ready = sem("sa_probsT_ready")
        o_done = sem("sa_o_done")
        o_hi = sem("sa_o_hi")
        o_split = sem("sa_o_split")
        pr_done = sem("sa_pr_done")
        pr_free = sem("sa_pr_free")

        def whole_program(eng, start, step):
            with eng.Fori(0, BLOCKS) as b:
                start(b)
                step(b, 0, 0, True, False, True)
                with eng.Fori(0, KVH // 2 - 1) as i:
                    step(b, i * 2 + 1, 1, True, True, True)
                    step(b, i * 2 + 2, 0, True, True, True)
                step(b, KVH - 1, 1, True, True, False)
                step(b, KVH, 0, False, True, False)

        block = ctx.enter_context(nc.Block())

        @block.sync
        def _(sp):
            def start(b):
                for t in range(TILES):
                    sp.wait_ge(acc_loaded, b * TILES + (t + 1))
                    sp.dma_start(xin[:, t], tile_of(x_rows, b * TILES + t)).then_inc(xin_loaded[t], 16)
                for u in range(3):
                    weights(b, 0, u)

            def weights(b, g, u):
                sp.wait_ge(w_split, (b * KVH + g) * U + (u + 1))
                sp.dma_start(wraw[:, u % 3], tile_of(wqkv, g * U + u)).then_inc(wraw_loaded[u % 3], 16)

            def step(b, g, par, proj, attn, nxt):
                if attn:
                    for h in range(QPG):
                        sp.wait_ge(p_split, ((b * KVH + g) + (-1)) * QPG + (h + 1))
                        sp.dma_start(praw[:, h % 2], tile_of(wproj, (g + (-1)) * QPG + h)
                                     ).then_inc(praw_loaded[h % 2], 16)
                if proj:
                    for u in range(3, U):
                        weights(b, g, u)
                if nxt:
                    for u in range(3):
                        weights(b, g + 1, u)

            whole_program(sp, start, step)

        @block.gpsimd
        def _(pool):
            pool.sem_inc(w_split, 3)
            pool.sem_inc(p_split, 2)

            def weights(b, g, u):
                pool.wait_ge(w_hi, (b * KVH + g) * U + (u + 1))
                nc.gpsimd.tensor_tensor(wl[:, u % 3], wraw[:, u % 3], f32(wh[:, u % 3]), ALU.subtract
                                        ).then_inc(w_split, 1)

            def start(b):
                for u in range(3):
                    weights(b, 0, u)

            def step(b, g, par, proj, attn, nxt):
                if attn:
                    for h in range(QPG):
                        pool.wait_ge(p_hi, ((b * KVH + g) + (-1)) * QPG + (h + 1))
                        nc.gpsimd.tensor_tensor(pl[:, h], praw[:, h % 2], f32(ph[:, h]), ALU.subtract
                                                ).then_inc(p_split, 1)
                if proj:
                    for u in range(3, U):
                        weights(b, g, u)
                if nxt:
                    for u in range(3):
                        weights(b, g + 1, u)

            whole_program(pool, start, step)

        @block.tensor
        def _(pe):
            pe.sem_inc(pr_done, 1)

            def start(b):
                for t in range(TILES):
                    ln.turn(pe, b, t, ident, pr_ps, pr_free, b * PR_BLOCK)
                pe.wait_ge(pr_free, b * PR_BLOCK + 10)

            def step(b, g, par, proj, attn, nxt):
                n = b * KVH + g
                m = n + (-1)
                mp = 1 - par

                def unit(u):
                    if not proj:
                        return
                    pe.wait_ge(w_split, n * U + (u + 4))
                    pe.wait_ge(u_copied, n * U + (u + 1))
                    w = lambda a: [a[:, u % 3, k * P:(k + 1) * P] for k in range(KC)]
                    three_passes(nc, u_ps[u % 2][:], [(h, l, ln.xh[:, k], ln.xl[:, k]) for k, (h, l)
                                                      in enumerate(zip(w(wh), w(wl)))]).then_inc(u_done, 1)

                def turn_v():
                    if not proj:
                        return
                    pe.wait_ge(u_copied, n * U + 4)
                    pe.wait_ge(v_copied, n + 1)
                    for t in range(TILES):
                        ins = nc.tensor.transpose(v_ps[:, t * P:(t + 1) * P], vT[:, t * P:(t + 1) * P], ident[:])
                    ins.then_inc(v_turned, 1)

                def scores(t):
                    if not attn:
                        return
                    if t == 0:
                        pe.wait_ge(u_copied, n * U + 2)
                    pe.wait_ge(s_masked, m * TILES + (t + 1))
                    for h in range(QPG):
                        ins = nc.tensor.matmul(s_ps[:, h * P:(h + 1) * P], qT[:, mp, h, t * P:(t + 1) * P],
                                               kT[:, mp, t * P:(t + 1) * P], start=True, stop=True)
                    ins.then_inc(s_done, 1)

                def turn_probs(t):
                    if not attn:
                        return
                    pe.wait_ge(probs_ready, m * TILES + (t + 1))
                    pe.wait_ge(probsT_ready, m * TILES + (t + 1))
                    for h in range(QPG):
                        ins = nc.tensor.transpose(t_ps[:, h * P:(h + 1) * P], probs[:, h], ident[:])
                    ins.then_inc(probs_turned, 1)

                def mix_values(t):
                    if not attn:
                        return
                    if t == 0:
                        pe.wait_ge(v_copied, m + 2)
                    pe.wait_ge(probsT_ready, m * TILES + (t + 2))
                    pe.wait_ge(o_split, m * TILES + (t + 1))
                    nc.tensor.matmul(o_ps[:], v[:, mp, t], probsT[:], start=True, stop=True).then_inc(o_done, 1)

                def project(t):
                    if not attn:
                        return
                    if t == 0:
                        pe.wait_ge(p_split, m * QPG + (QPG + 2))
                    pe.wait_ge(o_split, m * TILES + (t + 2))
                    for half in range(2):
                        pe.wait_ge(pr_free, b * (PR_BLOCK - KVH * PR) + m * PR + (8 + 2 * t + half + 1))
                        cols = slice(half * HALF, (half + 1) * HALF)
                        ins = three_passes(nc, pr_ps[half][:],
                                           [(oh[:, h * P:(h + 1) * P], ol[:, h * P:(h + 1) * P],
                                             ph[:, h, cols], pl[:, h, cols]) for h in range(QPG)])
                        ins.then_inc(pr_done, 1)

                scores(0)
                unit(0)
                turn_probs(0)
                scores(1)
                unit(1)
                mix_values(0)
                turn_probs(1)
                scores(2)
                unit(2)
                turn_v()
                project(0)
                mix_values(1)
                turn_probs(2)
                scores(3)
                unit(3)
                project(1)
                mix_values(2)
                turn_probs(3)
                unit(4)
                project(2)
                mix_values(3)
                unit(5)
                project(3)

            whole_program(pe, start, step)

        @block.scalar
        def _(act):
            act.sem_inc(u_copied, 2)
            act.sem_inc(v_copied, 1)
            act.sem_inc(probsT_ready, 1)
            act.sem_inc(acc_loaded, TILES)
            for t in range(TILES):
                act.sem_inc(x1_stored[t], 16)

            def weights(b, g, u):
                act.wait_ge(wraw_loaded[u % 3], (b * KVH + g) * 32 + (16 * (u // 3) + 16))
                nc.scalar.activation(wh[:, u % 3], wraw[:, u % 3], ACT.Copy).then_inc(w_hi, 1)

            def start(b):
                for u in range(3):
                    weights(b, 0, u)
                ln.deviations(act, b)
                for t in range(TILES):
                    act.wait_ge(ln.xn_ready, b * TILES + (t + 1))
                    act.wait_ge(x1_stored[t], b * 16 + 16)
                    nc.scalar.activation(acc[:, t], xin[:, t], ACT.Copy).then_inc(acc_loaded, 1)
                    ln.high(act, b, t, pr_ps)

            def step(b, g, par, proj, attn, nxt):
                n = b * KVH + g
                m = n + (-1)
                dst = [kT[:, par], vT[:]] + [qT[:, par, h] for h in range(QPG)]

                def copy_unit(u):
                    if not proj:
                        return
                    act.wait_ge(u_done, n * U + (u + 1))
                    nc.scalar.activation(dst[u], u_ps[u % 2][:], ACT.Copy).then_inc(u_copied, 1)
                    if u < 3:
                        weights(b, g, u + 3)
                    elif nxt:
                        weights(b, g + 1, u - 3)

                def copy_v():
                    if not proj:
                        return
                    act.wait_ge(v_turned, n + 1)
                    nc.scalar.activation(v[:, par].rearrange("p t d -> p (t d)"), v_ps[:], ACT.Copy
                                         ).then_inc(v_copied, 1)

                def out_weights(hs):
                    if not attn:
                        return
                    act.wait_ge(pr_done, m * PR + 1)
                    for h in hs:
                        act.wait_ge(praw_loaded[h % 2], m * 32 + (16 * (h // 2) + 16))
                        nc.scalar.activation(ph[:, h], praw[:, h % 2], ACT.Copy).then_inc(p_hi, 1)

                def exps(t):
                    if not attn:
                        return
                    act.wait_ge(s_shifted, m * TILES + (t + 1))
                    nc.scalar.activation(probs[:], probs[:], ACT.Exp, scale=SELF_SCALE).then_inc(exp_done, 1)

                def copy_probs(t):
                    if not attn:
                        return
                    act.wait_ge(probs_turned, m * TILES + (t + 1))
                    nc.scalar.activation(probsT[:], t_ps[:], ACT.Copy).then_inc(probsT_ready, 1)

                def high_o(t):
                    if not attn:
                        return
                    act.wait_ge(o_done, m * TILES + (t + 1))
                    nc.scalar.activation(oh[:], o_ps[:], ACT.Copy).then_inc(o_hi, 1)

                out_weights([0, 1])
                exps(0)
                copy_unit(0)
                out_weights([2, 3])
                copy_probs(0)
                exps(1)
                copy_unit(1)
                high_o(0)
                copy_probs(1)
                exps(2)
                copy_unit(2)
                copy_v()
                high_o(1)
                copy_probs(2)
                exps(3)
                copy_unit(3)
                high_o(2)
                copy_probs(3)
                copy_unit(4)
                high_o(3)
                copy_unit(5)
                if not proj:
                    for t in range(TILES):
                        act.wait_ge(pr_free, b * PR_BLOCK + (PR_BLOCK - PR + 2 * t + 4))
                        act.dma_start(tile_of(x1, b * TILES + t), acc[:, t]).then_inc(x1_stored[t], 16)

            whole_program(act, start, step)
            for t in range(TILES):
                act.wait_ge(x1_stored[t], 16 * (BLOCKS + 1))

        @block.vector
        def _(dve):
            dve.sem_inc(s_masked, 1)
            dve.sem_inc(o_split, 1)
            dve.sem_inc(pr_free, 2)

            def start(b):
                x_tile = lambda t: xin[:, t]
                ln.moments(dve, b, x_tile, xin_loaded, b + 1)
                ln.normalise(dve, b, 0, x_tile)
                for t in range(TILES):
                    if t + 1 < TILES:
                        ln.normalise(dve, b, t + 1, x_tile)
                    ln.low(dve, b, t, pr_ps, pr_free)
            def step(b, g, par, proj, attn, nxt):
                if not attn:
                    return
                m = b * KVH + g + (-1)
                dve.wait_ge(acc_loaded, b * TILES + 2 * TILES)

                def softmax(t):
                    i = m * TILES + (t + 1)
                    dve.wait_ge(s_done, i)
                    nc.vector.tensor_tensor(probs[:], s_ps[:].rearrange("p (h n) -> p h n", h=QPG),
                                            causal[:].unsqueeze(1).broadcast_to([P, QPG, P]), ALU.add
                                            ).then_inc(s_masked, 1)
                    dve.wait_ge(s_masked, i + 1)
                    nc.vector.tensor_reduce(top[:], probs[:], AX.X, ALU.max).then_inc(s_top, 1)
                    dve.wait_ge(s_top, i)
                    nc.vector.tensor_tensor(probs[:], probs[:], top[:].unsqueeze(2).broadcast_to([P, QPG, P]),
                                            ALU.subtract).then_inc(s_shifted, 1)
                    dve.wait_ge(exp_done, i)
                    nc.vector.tensor_reduce(total[:], probs[:], AX.X, ALU.add).then_inc(total_done, 1)
                    dve.wait_ge(total_done, i)
                    nc.vector.reciprocal(inv[:], total[:]).then_inc(inv_done, 1)
                    dve.wait_ge(inv_done, i)
                    nc.vector.tensor_tensor(probs[:], probs[:], inv[:].unsqueeze(2).broadcast_to([P, QPG, P]),
                                            ALU.mult).then_inc(probs_ready, 1)

                def low_o(t):
                    dve.wait_ge(o_hi, m * TILES + (t + 1))
                    nc.vector.tensor_tensor(ol[:], o_ps[:], f32(oh[:]), ALU.subtract).then_inc(o_split, 1)

                def add_projected(t):
                    for half in range(2):
                        dve.wait_ge(pr_done, m * PR + (2 * t + half + 2))
                        part = acc[:, t, half * HALF:(half + 1) * HALF]
                        nc.vector.tensor_tensor(part, pr_ps[half][:], part, ALU.add).then_inc(pr_free, 1)

                softmax(0)
                softmax(1)
                low_o(0)
                softmax(2)
                add_projected(0)
                low_o(1)
                softmax(3)
                add_projected(1)
                low_o(2)
                add_projected(2)
                low_o(3)
                add_projected(3)

            whole_program(dve, start, step)



def cross_attention_phase(nc, sems, ident, slotmask, bias_qkv, eps, x1, ctxT, w_folded, wo, bo, x2):
    KV_PIECES = 2
    PR = TILES * 2
    U = 3
    WHICH = [1, 2, 0]
    U_BLOCK = 8 + U * CH
    X_BLOCK = (1 + PR) * CH
    with ExitStack() as ctx:
        def sb(name, shape, dt=F32):
            return ctx.enter_context(nc.sbuf_tensor(name, shape, dt))

        def psum(name, cols=HALF):
            return ctx.enter_context(nc.psum_tensor(name, [P, cols], F32))

        def sem(name):
            return sems.enter_context(nc.semaphore(name))

        ln = NormBuffers(nc, ctx, sems, "ca_ln", eps)
        acc = sb("ca_acc", [P, TILES, D])
        bo_all = sb("ca_bo", [P, D])
        craw = sb("ca_craw", [P, 2, 2, BT])
        ch = sb("ca_ch", [P, KC, BT], F32R)
        cl = sb("ca_cl", [P, KC, BT], F32R)
        wraw = sb("ca_wraw", [P, U, D])
        wh = sb("ca_wh", [P, U, D], F32R)
        wl = sb("ca_wl", [P, U, D], F32R)
        oraw = sb("ca_oraw", [P, D])
        owh = sb("ca_owh", [P, D], F32R)
        owl = sb("ca_owl", [P, D], F32R)
        kh = sb("ca_kh", [P, 2, BT], F32R)
        kl = sb("ca_kl", [P, 2, BT], F32R)
        qh = sb("ca_qh", [P, 2, BT], F32R)
        ql = sb("ca_ql", [P, 2, BT], F32R)
        vT = sb("ca_vT", [P, BT])
        v = sb("ca_v", [P, 2, TILES * SLOTS, VW])
        kmh = sb("ca_kmh", [P, 2, SLOTS, P], F32R)
        kml = sb("ca_kml", [P, 2, SLOTS, P], F32R)
        probs = sb("ca_probs", [P, SLOTS, P])
        probsT = sb("ca_probsT", [P, SLOTS * P])
        bias_now = sb("ca_bias_now", [P, 2, 3])
        top = sb("ca_top", [P, SLOTS])
        inv = sb("ca_inv", [P, SLOTS])
        o = sb("ca_o", [P, P])
        oh = sb("ca_oh", [P, P], F32R)
        ol = sb("ca_ol", [P, P], F32R)

        u_ps = [psum(f"ca_u{i}") for i in range(2)]
        s_ps = psum("ca_s", 2 * HALF)
        t_ps = psum("ca_t", 2 * HALF)
        o_ps = psum("ca_o_ps")
        x_ps = psum("ca_x")

        acc_in = [sem(f"ca_acc_in{t}") for t in range(TILES)]
        bo_loaded = sem("ca_bo_loaded")
        acc_ready = sem("ca_acc_ready")
        craw_loaded = [sem(f"ca_craw_loaded{i}") for i in range(2)]
        c_hi = sem("ca_c_hi")
        c_split = sem("ca_c_split")
        wraw_loaded = [sem(f"ca_wraw_loaded{u}") for u in range(U)]
        w_hi = sem("ca_w_hi")
        w_split = sem("ca_w_split")
        oraw_loaded = sem("ca_oraw_loaded")
        ow_hi = sem("ca_ow_hi")
        ow_split = sem("ca_ow_split")
        u_done = sem("ca_u_done")
        u_hi = sem("ca_u_hi")
        u_free = sem("ca_u_free")
        v_turned = sem("ca_v_turned")
        km_hi = sem("ca_km_hi")
        km_ready = sem("ca_km_ready")
        s_done = sem("ca_s_done")
        s_top = sem("ca_s_top")
        s_shifted = sem("ca_s_shifted")
        probs_ready = sem("ca_probs_ready")
        probs_turned = sem("ca_probs_turned")
        probsT_ready = sem("ca_probsT_ready")
        pv_done = sem("ca_pv_done")
        inv_done = sem("ca_inv_done")
        o_ready = sem("ca_o_ready")
        o_turned = sem("ca_o_turned")
        o_hi = sem("ca_o_hi")
        o_split = sem("ca_o_split")
        pr_done = sem("ca_pr_done")
        x_free = sem("ca_x_free")
        x2_stored = [sem(f"ca_x2_stored{t}") for t in range(TILES)]
        v_ones = sem("ca_v_ones")
        bias_ready = sem("ca_bias_ready")

        x1_by_i = x1.rearrange("t p n -> (t p) n").rearrange("(j i) n -> i j n", i=SEQ)

        def shared_before(n, attn):
            return n * (1 + PR) + (-PR if attn else 0)

        def whole_program(eng, start, step):
            with eng.Fori(0, BLOCKS) as b:
                start(b)
                step(b, 0, 0, True, False, True)
                with eng.Fori(0, CH // 2 - 1) as i:
                    step(b, i * 2 + 1, 1, True, True, True)
                    step(b, i * 2 + 2, 0, True, True, True)
                step(b, CH - 1, 1, True, True, False)
                step(b, CH, 0, False, True, False)

        block = ctx.enter_context(nc.Block())

        @block.sync
        def _(sp):
            sp.dma_start(bo_all[:], bo).then_inc(bo_loaded, 16)

            def weights(b, c, u):
                sp.wait_ge(w_split, (b * CH + c) * U + (u + 1))
                sp.dma_start(wraw[:, u], tile_of(w_folded, c + WHICH[u] * CH)).then_inc(wraw_loaded[u], 16)

            def start(b):
                for t in range(TILES):
                    sp.wait_ge(x2_stored[t], b * 16 + 16)
                    sp.dma_start(acc[:, t], tile_of(x1_by_i, b * TILES + t)).then_inc(acc_in[t], 16)
                for q in range(4):
                    sp.wait_ge(c_split, b * 4 + (q + 1))
                    sp.dma_start(craw[:, q % 2], tile_of(ctxT, b * 4 + q)
                                 .rearrange("p (k n) -> p k n", k=2)).then_inc(craw_loaded[q % 2], 16)
                for u in range(U):
                    weights(b, 0, u)

            def step(b, c, par, proj, attn, nxt):
                if attn:
                    sp.wait_ge(ow_split, (b * CH + c))
                    sp.dma_start(oraw[:], tile_of(wo, c + (-1))).then_inc(oraw_loaded, 16)
                if nxt:
                    for u in range(U):
                        weights(b, c + 1, u)

            whole_program(sp, start, step)

        @block.gpsimd
        def _(pool):
            pool.sem_inc(c_split, 2)
            pool.sem_inc(w_split, 3)
            pool.sem_inc(ow_split, 1)
            nc.gpsimd.memset(v[:, :, :, DK:VW], 1.0).then_inc(v_ones, 1)

            def weights(b, c, u):
                pool.wait_ge(w_hi, (b * CH + c) * U + (u + 1))
                nc.gpsimd.tensor_tensor(wl[:, u], wraw[:, u], f32(wh[:, u]), ALU.subtract).then_inc(w_split, 1)

            def masked_k(n, par, t):
                i = n * TILES + (t + 1)
                pool.wait_ge(s_done, i)
                mask = slotmask[:].unsqueeze(2).broadcast_to([P, SLOTS, P])
                for dst, src in ((kmh, kh), (kml, kl)):
                    ins = nc.gpsimd.tensor_tensor(
                        dst[:, t % 2], f32(src[:, par, t * P:(t + 1) * P]).unsqueeze(1).broadcast_to([P, SLOTS, P]),
                        mask, ALU.mult)
                ins.then_inc(km_ready, 1)

            def start(b):
                for q in range(4):
                    pool.wait_ge(c_hi, b * 4 + (q + 1))
                    nc.gpsimd.tensor_tensor(cl[:, 2 * q:2 * q + 2], craw[:, q % 2], f32(ch[:, 2 * q:2 * q + 2]),
                                            ALU.subtract).then_inc(c_split, 1)
                for u in range(U):
                    weights(b, 0, u)

            def step(b, c, par, proj, attn, nxt):
                n = b * CH + c
                if attn:
                    pool.wait_ge(ow_hi, n)
                    nc.gpsimd.tensor_tensor(owl[:], oraw[:], f32(owh[:]), ALU.subtract).then_inc(ow_split, 1)
                    masked_k(n + (-1), 1 - par, 2)
                    masked_k(n + (-1), 1 - par, 3)
                if nxt:
                    weights(b, c + 1, 0)
                if proj:
                    pool.wait_ge(u_free, b * 8 + n * U + (8 + 1 + 2))
                    masked_k(n, par, 0)
                    masked_k(n, par, 1)
                if nxt:
                    weights(b, c + 1, 1)
                    weights(b, c + 1, 2)

            whole_program(pool, start, step)

        @block.tensor
        def _(pe):
            pe.sem_inc(s_done, 2)
            pe.sem_inc(pr_done, 1)

            def start(b):
                for t in range(TILES):
                    ln.turn(pe, b, t, ident, u_ps, u_free, b * U_BLOCK)
                pe.wait_ge(u_free, b * U_BLOCK + 10)

            def step(b, c, par, proj, attn, nxt):
                n = b * CH + c
                m = n + (-1)
                mp = 1 - par
                x0 = shared_before(n, attn)

                def unit(u, *pieces):
                    if not proj:
                        return
                    if pieces[0] == 0:
                        pe.wait_ge(w_split, n * U + (u + 4))
                        if u == 0:
                            pe.wait_ge(c_split, b * 4 + 6)
                        pe.wait_ge(u_free, b * 8 + n * U + (8 + u + 1))
                    bh, bl = (ln.xh, ln.xl) if u == 2 else (ch, cl)
                    for q in pieces:
                        ks = range(q * KV_PIECES, (q + 1) * KV_PIECES)
                        ins = three_passes(nc, u_ps[(par * U + u) % 2][:],
                                           [(wh[:, u, k * P:(k + 1) * P], wl[:, u, k * P:(k + 1) * P],
                                             bh[:, k], bl[:, k]) for k in ks], first=q == 0, last=q == 3)
                    if q == 3:
                        ins.then_inc(u_done, 1)

                def turn_v():
                    if not proj:
                        return
                    pe.wait_ge(u_free, b * 8 + n * U + (8 + 2 + 2))
                    pe.wait_ge(x_free, x0 + (3 if attn else 1))
                    for t in range(TILES):
                        ins = nc.tensor.transpose(x_ps[:, t * P:(t + 1) * P], vT[:, t * P:(t + 1) * P], ident[:])
                    ins.then_inc(v_turned, 1)

                def scores(t):
                    if not attn:
                        return
                    if t == 0:
                        pe.wait_ge(u_free, b * 8 + n * U + (8 + 2))
                    pe.wait_ge(km_ready, m * TILES + (t + 1))
                    pe.wait_ge(s_shifted, m * TILES + (t + 1))
                    for half in range(2):
                        sl = slice(4 * half, 4 * half + 4)
                        ins = three_passes(nc, s_ps[:, half * HALF:(half + 1) * HALF],
                                           [(qh[:, mp, t * P:(t + 1) * P], ql[:, mp, t * P:(t + 1) * P],
                                             kmh[:, t % 2, sl], kml[:, t % 2, sl])])
                    ins.then_inc(s_done, 1)

                def turn_probs(t):
                    if not attn:
                        return
                    pe.wait_ge(probs_ready, m * TILES + (t + 1))
                    pe.wait_ge(probsT_ready, m * TILES + (t + 1))
                    for s in range(SLOTS):
                        ins = nc.tensor.transpose(t_ps[:, s * P:(s + 1) * P], probs[:, s], ident[:])
                    ins.then_inc(probs_turned, 1)

                def mix_values(t):
                    if not attn:
                        return
                    if t == 0:
                        pe.wait_ge(x_free, x0 + 1)
                        pe.wait_ge(v_ones, 1)
                    pe.wait_ge(probsT_ready, m * TILES + (t + 2))
                    pe.wait_ge(o_ready, m * TILES + (t + 1))
                    if t:
                        pe.wait_ge(o_split, m * TILES + t)
                    for s in range(SLOTS):
                        ins = nc.tensor.matmul(o_ps[:, s * VW:(s + 1) * VW], probsT[:, s * P:(s + 1) * P],
                                               v[:, mp, t * SLOTS + s], start=True, stop=True)
                    ins.then_inc(pv_done, 1)

                def turn_o(t):
                    if not attn:
                        return
                    pe.wait_ge(o_ready, m * TILES + (t + 2))
                    nc.tensor.transpose(o_ps[:, 256:256 + P], o[:], ident[:]).then_inc(o_turned, 1)

                def project(t, half):
                    if not attn:
                        return
                    if t == 0 and half == 0:
                        pe.wait_ge(ow_split, m + 2)
                    if half == 0:
                        pe.wait_ge(o_split, m * TILES + (t + 1))
                    use = 2 * t + half
                    pe.wait_ge(x_free, x0 + (use + (1 if proj and use >= 2 else 0) + 1))
                    cols = slice(half * HALF, (half + 1) * HALF)
                    three_passes(nc, x_ps[:], [(oh[:], ol[:], owh[:, cols], owl[:, cols])]).then_inc(pr_done, 1)

                scores(0)
                unit(0, 0, 1)
                turn_probs(0)
                scores(1)
                unit(0, 2, 3)
                unit(1, 0)
                mix_values(0)
                turn_probs(1)
                scores(2)
                unit(1, 1)
                turn_o(0)
                unit(1, 2, 3)
                mix_values(1)
                turn_probs(2)
                scores(3)
                project(0, 0)
                unit(2, 0)
                project(0, 1)
                turn_o(1)
                unit(2, 1)
                turn_v()
                mix_values(2)
                turn_probs(3)
                project(1, 0)
                unit(2, 2)
                project(1, 1)
                turn_o(2)
                unit(2, 3)
                mix_values(3)
                project(2, 0)
                project(2, 1)
                turn_o(3)
                project(3, 0)
                project(3, 1)

            whole_program(pe, start, step)

        @block.scalar
        def _(act):
            act.sem_inc(probsT_ready, 1)
            for t in range(TILES):
                act.sem_inc(x2_stored[t], 16)

            def weights(b, c, u):
                act.wait_ge(wraw_loaded[u], (b * CH + c) * 16 + 16)
                nc.scalar.activation(wh[:, u], wraw[:, u], ACT.Copy).then_inc(w_hi, 1)

            def start(b):
                for q in range(4):
                    act.wait_ge(craw_loaded[q % 2], b * 32 + (16 * (q // 2) + 16))
                    nc.scalar.activation(ch[:, 2 * q:2 * q + 2], craw[:, q % 2], ACT.Copy).then_inc(c_hi, 1)
                for u in range(U):
                    weights(b, 0, u)
                ln.deviations(act, b)
                for t in range(TILES):
                    ln.high(act, b, t, u_ps)

            def step(b, c, par, proj, attn, nxt):
                n = b * CH + c
                m = n + (-1)

                def set_bias():
                    if not proj:
                        return
                    src = bias_qkv[:, bass.ds(c, 1)].rearrange("p a w -> p (a w)")
                    nc.scalar.activation(bias_now[:, par], src, ACT.Copy).then_inc(bias_ready, 1)
                    act.wait_ge(bias_ready, n + 1)

                def high_unit(u, dst):
                    if not proj:
                        return
                    act.wait_ge(u_done, n * U + (u + 1))
                    w = WHICH[u]
                    nc.scalar.activation(dst[:, par], u_ps[(par * U + u) % 2][:], ACT.Identity,
                                         bias=bias_now[:, par, w:w + 1]).then_inc(u_hi, 1)

                def next_weights(u):
                    if nxt:
                        act.wait_ge(u_done, n * U + (u + 1))
                        weights(b, c + 1, u)

                def out_weights():
                    if not attn:
                        return
                    act.wait_ge(pr_done, m * PR + 1)
                    act.wait_ge(oraw_loaded, n * 16)
                    nc.scalar.activation(owh[:], oraw[:], ACT.Copy).then_inc(ow_hi, 1)

                def exps(t):
                    if not attn:
                        return
                    act.wait_ge(s_shifted, m * TILES + (t + 2))
                    nc.scalar.activation(probs[:], probs[:], ACT.Exp, scale=CROSS_SCALE).then_inc(probs_ready, 1)

                def copy_probs(t):
                    if not attn:
                        return
                    act.wait_ge(probs_turned, m * TILES + (t + 1))
                    nc.scalar.activation(probsT[:], t_ps[:], ACT.Copy).then_inc(probsT_ready, 1)

                def high_o(t):
                    if not attn:
                        return
                    act.wait_ge(o_turned, m * TILES + (t + 1))
                    nc.scalar.activation(oh[:], o_ps[:, 256:256 + P], ACT.Copy).then_inc(o_hi, 1)

                set_bias()
                out_weights()
                exps(0)
                copy_probs(0)
                exps(1)
                high_unit(0, kh)
                next_weights(0)
                copy_probs(1)
                exps(2)
                high_o(0)
                copy_probs(2)
                exps(3)
                next_weights(1)
                high_o(1)
                copy_probs(3)
                high_o(2)
                high_unit(2, qh)
                next_weights(2)
                high_o(3)
                if not proj:
                    for t in range(TILES):
                        act.wait_ge(x_free, b * X_BLOCK + (X_BLOCK - PR + 2 * t + 3))
                        act.dma_start(tile_of(x2, b * TILES + t), acc[:, t]).then_inc(x2_stored[t], 16)

            whole_program(act, start, step)
            for t in range(TILES):
                act.wait_ge(x2_stored[t], 16 * (BLOCKS + 1))

        @block.vector
        def _(dve):
            dve.sem_inc(u_free, 2)
            dve.sem_inc(s_shifted, 1)
            dve.sem_inc(o_ready, 1)
            dve.sem_inc(x_free, 1)
            dve.wait_ge(bo_loaded, 16)

            def start(b):
                x_tile = lambda t: acc[:, t]

                def add_bias(t):
                    dve.wait_ge(ln.xn_ready, b * TILES + (t + 1))
                    nc.vector.tensor_tensor(acc[:, t], acc[:, t], bo_all[:], ALU.add).then_inc(acc_ready, 1)

                ln.moments(dve, b, x_tile, acc_in, b + 1)
                ln.normalise(dve, b, 0, x_tile)
                for t in range(TILES):
                    if t + 1 < TILES:
                        ln.normalise(dve, b, t + 1, x_tile)
                    ln.low(dve, b, t, u_ps, u_free)
                for t in range(TILES):
                    add_bias(t)
                dve.wait_ge(acc_ready, b * TILES + TILES)

            def step(b, c, par, proj, attn, nxt):
                n = b * CH + c
                m = n + (-1)

                def low_unit(u, dst, hi, number):
                    if not proj:
                        return
                    dve.wait_ge(u_hi, n * 2 + number)
                    w = WHICH[u]
                    nc.vector.scalar_tensor_tensor(dst[:, par], u_ps[(par * U + u) % 2][:],
                                                   bias_now[:, par, w:w + 1], f32(hi[:, par]),
                                                   ALU.add, ALU.subtract).then_inc(u_free, 1)

                def copy_v():
                    if not proj:
                        return
                    dve.wait_ge(bias_ready, n + 1)
                    dve.wait_ge(u_done, n * U + 2)
                    nc.vector.tensor_scalar(vT[:], u_ps[(par * U + 1) % 2][:], bias_now[:, par, 2:3], None,
                                            ALU.add).then_inc(u_free, 1)

                def place_v():
                    if not proj:
                        return
                    dve.wait_ge(v_turned, n + 1)
                    nc.vector.tensor_copy(v[:, par, :, 0:DK], x_ps[:].rearrange("p (s d) -> p s d", d=DK)
                                          ).then_inc(x_free, 1)

                def shift(t):
                    if not attn:
                        return
                    i = m * TILES + (t + 1)
                    sv = s_ps[:].rearrange("p (s n) -> p s n", s=SLOTS)
                    dve.wait_ge(s_done, m * TILES + (t + 3))
                    nc.vector.tensor_reduce(top[:], sv, AX.X, ALU.max).then_inc(s_top, 1)
                    dve.wait_ge(s_top, i)
                    nc.vector.tensor_tensor(probs[:], sv, top[:].unsqueeze(2).broadcast_to([P, SLOTS, P]),
                                            ALU.subtract).then_inc(s_shifted, 1)

                def scale_o(t):
                    if not attn:
                        return
                    ov = o_ps[:, 0:SLOTS * VW].rearrange("p (s w) -> p s w", w=VW)
                    dve.wait_ge(pv_done, m * TILES + (t + 1))
                    nc.vector.reciprocal(inv[:], ov[:, :, DK]).then_inc(inv_done, 1)
                    dve.wait_ge(inv_done, m * TILES + (t + 1))
                    nc.vector.tensor_tensor(o[:].rearrange("p (s d) -> p s d", d=DK), ov[:, :, 0:DK],
                                            inv[:].unsqueeze(2).broadcast_to([P, SLOTS, DK]), ALU.mult
                                            ).then_inc(o_ready, 1)

                def low_o(t):
                    if not attn:
                        return
                    dve.wait_ge(o_hi, m * TILES + (t + 1))
                    nc.vector.tensor_tensor(ol[:], o_ps[:, 256:256 + P], f32(oh[:]), ALU.subtract
                                            ).then_inc(o_split, 1)

                def add_projected(t, half):
                    if not attn:
                        return
                    dve.wait_ge(pr_done, m * PR + (2 * t + half + 2))
                    part = acc[:, t, half * HALF:(half + 1) * HALF]
                    nc.vector.tensor_tensor(part, x_ps[:], part, ALU.add).then_inc(x_free, 1)

                shift(0)
                shift(1)
                low_unit(0, kl, kh, 1)
                scale_o(0)
                shift(2)
                low_o(0)
                copy_v()
                scale_o(1)
                shift(3)
                add_projected(0, 0)
                add_projected(0, 1)
                low_o(1)
                place_v()
                scale_o(2)
                add_projected(1, 0)
                add_projected(1, 1)
                low_o(2)
                low_unit(2, ql, qh, 2)
                scale_o(3)
                add_projected(2, 0)
                add_projected(2, 1)
                low_o(3)
                add_projected(3, 0)
                add_projected(3, 1)

            whole_program(dve, start, step)



def ffn_phase(nc, sems, ident, eps, x2, vh, uT, s_all, alpha, beta, u_rT, vh_r, s_r, d_r, r_mat, bias, out):
    with ExitStack() as ctx:
        def sb(name, shape, dt=F32):
            return ctx.enter_context(nc.sbuf_tensor(name, shape, dt))

        def bank(name):
            return ctx.enter_context(nc.psum_tensor(name, [P, HALF], F32))

        def sem(name):
            return sems.enter_context(nc.semaphore(name))

        ln = NormBuffers(nc, ctx, sems, "ff_ln", eps)
        acc = sb("ff_acc", [P, 2, TILES, D])
        vh_sb = sb("ff_vh", [P, KC, D])
        uT_sb = sb("ff_uT", [P, KC, D])
        s_sb = sb("ff_s", [P, KC])
        ab = sb("ff_ab", [R_TOP, 2])
        small = sb("ff_small", [R_INT, 2])
        urT_sb = sb("ff_urT", [R_INT, D])
        vhr_sb = sb("ff_vhr", [R_INT, D])
        r_sb = sb("ff_r", [R_INT, R_INT])
        delta = sb("ff_delta", [R_INT, D])
        bias_sb = sb("ff_bias", [P, D])
        weh = sb("ff_weh", [P, KC, D], F32R)
        wel = sb("ff_wel", [P, KC, D], F32R)
        t_ps = [bank(f"ff_t{i}") for i in range(2)]
        y_ps = [bank(f"ff_y{i}") for i in range(4)]
        d_ps = [bank(f"ff_d{i}") for i in range(2)]

        small_loaded = sem("ff_small_loaded")
        bias_loaded = sem("ff_bias_loaded")
        factors_loaded = [sem(f"ff_factors_loaded{k}") for k in range(KC)]
        acc_in = [[sem(f"ff_acc_in{p}{t}") for t in range(TILES)] for p in range(2)]
        s_steps = sem("ff_s_steps")
        u_scaled = sem("ff_u_scaled")
        delta_mm = sem("ff_delta_mm")
        delta_ready = sem("ff_delta_ready")
        we_done = sem("ff_we_done")
        we_hi = sem("ff_we_hi")
        t_free = sem("ff_t_free")
        acc_ready = sem("ff_acc_ready")
        y_done = sem("ff_y_done")
        y_free = sem("ff_y_free")
        stored = [[sem(f"ff_stored{p}{t}") for t in range(TILES)] for p in range(2)]
        NWE = 2 * KC
        YB = 2 * TILES

        block = ctx.enter_context(nc.Block())

        @block.sync
        def _(sp):
            sp.dma_start(s_sb[:], s_all).then_inc(small_loaded, 16)
            sp.dma_start(ab[:, 0:1], alpha).then_inc(small_loaded, 16)
            sp.dma_start(ab[:, 1:2], beta).then_inc(small_loaded, 16)
            sp.dma_start(small[:, 0:1], s_r).then_inc(small_loaded, 16)
            sp.dma_start(small[:, 1:2], d_r).then_inc(small_loaded, 16)
            sp.dma_start(urT_sb[:], u_rT).then_inc(small_loaded, 16)
            sp.dma_start(vhr_sb[:], vh_r).then_inc(small_loaded, 16)
            sp.dma_start(r_sb[:], r_mat).then_inc(small_loaded, 16)
            for k in range(KC):
                sp.dma_start(uT_sb[:, k], uT[k]).then_inc(factors_loaded[k], 16)
                sp.dma_start(vh_sb[:, k], vh[k]).then_inc(factors_loaded[k], 16)
            sp.dma_start(bias_sb[:], bias).then_inc(bias_loaded, 16)
            with sp.Fori(0, BLOCKS // 2) as bb:
                for p in range(2):
                    for t in range(TILES):
                        sp.wait_ge(stored[p][t], bb * 16 + 16)
                        sp.dma_start(acc[:, p, t], tile_of(x2, bb * (2 * TILES) + (p * TILES + t))
                                     ).then_inc(acc_in[p][t], 16)

        @block.tensor
        def _(pe):
            pe.wait_ge(s_steps, 5)
            for half in range(2):
                ins = nc.tensor.matmul(d_ps[half][0:R_INT, :], r_sb[:], urT_sb[:, half * HALF:(half + 1) * HALF],
                                       start=True, stop=True)
            ins.then_inc(delta_mm, 1)
            pe.wait_ge(delta_ready, 1)
            for ic in range(KC):
                for half in range(2):
                    w = 2 * ic + half
                    pe.wait_ge(y_free, w + 1)
                    cols = slice(half * HALF, (half + 1) * HALF)
                    for k in range(KC):
                        if w == 0:
                            pe.wait_ge(u_scaled, k + 1)
                        nc.tensor.matmul(y_ps[w % 4][:], vh_sb[:, k, ic * P:(ic + 1) * P], uT_sb[:, k, cols],
                                         start=(k == 0), stop=False)
                    nc.tensor.matmul(y_ps[w % 4][:], vhr_sb[:, ic * P:(ic + 1) * P], delta[:, cols],
                                     start=False, stop=True).then_inc(we_done, 1)
            pe.wait_ge(y_free, NWE + 4)
            with pe.Fori(0, BLOCKS // 2) as bb:
                for p in range(2):
                    b = bb * 2 + p
                    for t in range(TILES):
                        ln.turn(pe, b, t, ident, t_ps, t_free, b * 8)
                    for t in range(TILES):
                        pe.wait_ge(t_free, b * 8 + (2 * t + 4))
                        for half in range(2):
                            use = 2 * t + half
                            pe.wait_ge(y_free, b * YB + (NWE + use + 1))
                            cols = slice(half * HALF, (half + 1) * HALF)
                            three_passes(nc, y_ps[use % 4][:],
                                         [(ln.xh[:, k, t * P:(t + 1) * P], ln.xl[:, k, t * P:(t + 1) * P],
                                           weh[:, k, cols], wel[:, k, cols]) for k in range(KC)]
                                         ).then_inc(y_done, 1)

        @block.scalar
        def _(act):
            for p in range(2):
                for t in range(TILES):
                    act.sem_inc(stored[p][t], 16)
            for w in range(NWE):
                act.wait_ge(we_done, w + 1)
                nc.scalar.activation(weh[:, w // 2, (w % 2) * HALF:(w % 2 + 1) * HALF], y_ps[w % 4][:],
                                     ACT.Copy).then_inc(we_hi, 1)
            with act.Fori(0, BLOCKS // 2) as bb:
                for p in range(2):
                    b = bb * 2 + p
                    ln.deviations(act, b)
                    for t in range(TILES):
                        ln.high(act, b, t, t_ps)
                    for t in range(TILES):
                        act.wait_ge(y_free, b * YB + (NWE + 2 * t + 2 + 4))
                        act.dma_start(tile_of(out, b * TILES + t), acc[:, p, t]).then_inc(stored[p][t], 16)
            for p in range(2):
                for t in range(TILES):
                    act.wait_ge(stored[p][t], 16 + 16 * (BLOCKS // 2))

        @block.vector
        def _(dve):
            dve.sem_inc(t_free, 2)
            dve.sem_inc(y_free, 4)
            dve.wait_ge(small_loaded, 8 * 16)
            top = s_sb[0:R_TOP, 0:1]
            nc.vector.tensor_scalar(top, top, ab[:, 0:1], ab[:, 1:2], ALU.mult, ALU.add).then_inc(s_steps, 1)
            dve.wait_ge(s_steps, 1)
            nc.vector.tensor_scalar(top, top, 0.0, None, ALU.max).then_inc(s_steps, 1)
            nc.vector.tensor_scalar(small[:, 1:2], small[:, 1:2], 0.0, None, ALU.max).then_inc(s_steps, 1)
            dve.wait_ge(s_steps, 3)
            nc.vector.tensor_scalar(urT_sb[:], urT_sb[:], small[:, 0:1], None, ALU.mult).then_inc(s_steps, 1)
            dve.wait_ge(s_steps, 4)
            nc.vector.tensor_scalar(urT_sb[:], urT_sb[:], small[:, 1:2], None, ALU.mult).then_inc(s_steps, 1)
            dve.wait_ge(delta_mm, 1)
            for half in range(2):
                ins = nc.vector.tensor_copy(delta[:, half * HALF:(half + 1) * HALF], d_ps[half][0:R_INT, :])
            ins.then_inc(delta_ready, 1)
            for k in range(KC):
                dve.wait_ge(factors_loaded[k], 32)
                nc.vector.tensor_scalar(uT_sb[:, k], uT_sb[:, k], s_sb[:, k:k + 1], None, ALU.mult
                                        ).then_inc(u_scaled, 1)
            for w in range(NWE):
                dve.wait_ge(we_hi, w + 1)
                part = (slice(None), w // 2, slice((w % 2) * HALF, (w % 2 + 1) * HALF))
                nc.vector.tensor_tensor(wel[part], y_ps[w % 4][:], f32(weh[part]), ALU.subtract
                                        ).then_inc(y_free, 1)
            dve.wait_ge(bias_loaded, 16)
            with dve.Fori(0, BLOCKS // 2) as bb:
                for p in range(2):
                    b = bb * 2 + p
                    x_tile = lambda t: acc[:, p, t]
                    ln.moments(dve, b, x_tile, acc_in[p], bb + 1)
                    ln.normalise(dve, b, 0, x_tile)
                    for t in range(TILES):
                        if t + 1 < TILES:
                            ln.normalise(dve, b, t + 1, x_tile)
                        ln.low(dve, b, t, t_ps, t_free)
                    for t in range(TILES):
                        nc.vector.tensor_tensor(acc[:, p, t], acc[:, p, t], bias_sb[:], ALU.add
                                                ).then_inc(acc_ready, 1)
                    dve.wait_ge(acc_ready, b * TILES + TILES)
                    for t in range(TILES):
                        for half in range(2):
                            use = 2 * t + half
                            dve.wait_ge(y_done, b * YB + (use + 1))
                            part = acc[:, p, t, half * HALF:(half + 1) * HALF]
                            nc.vector.tensor_tensor(part, y_ps[use % 4][:], part, ALU.add).then_inc(y_free, 1)


def decoder_layer(nc, a, out):
    x1 = nc.dram_tensor("x1", (TOKENS // P, P, D), F32, kind="Internal").ap()
    x2 = nc.dram_tensor("x2", (TOKENS // P, P, D), F32, kind="Internal").ap()
    w_folded = nc.dram_tensor("w_folded", (3 * CH, P, D), F32, kind="Internal").ap()
    with ExitStack() as sems, ExitStack() as ctx:
        def sb(name, shape):
            return ctx.enter_context(nc.sbuf_tensor(name, shape, F32))

        ident = sb("ident", [P, P])
        causal = sb("causal", [P, P])
        slotmask = sb("slotmask", [P, SLOTS])
        bias_qkv = sb("bias_qkv", [P, CH, 3])
        eps = sb("eps", [P, 1])
        eps_set = ctx.enter_context(nc.semaphore("eps_set"))
        with nc.Block() as block:
            @block.vector
            def _(dve):
                nc.vector.memset(eps[:], EPS).then_inc(eps_set, 1)
        setup_phase(nc, sems, ident, causal, slotmask, bias_qkv, a["w_nat"], a["b_nat"], a["inter_rows"],
                    a["amp_col"], w_folded)
        self_attention_phase(nc, sems, ident, causal, eps, a["x_rows"], a["wqkv"], a["wproj"], x1)
        cross_attention_phase(nc, sems, ident, slotmask, bias_qkv, eps, x1, a["ctxT"], w_folded, a["wo"],
                              a["bo"], x2)
        ffn_phase(nc, sems, ident, eps, x2, a["vh"], a["uT"], a["s_all"], a["alpha"], a["beta"], a["u_rT"],
                  a["vh_r"], a["s_r"], a["d_r"], a["r_mat"], a["ffn_bias"], out)


def layouts(i):
    c = np.ascontiguousarray
    g = {}
    g["x_rows"] = c(np.transpose(i["x"], (1, 0, 2))).reshape(TOKENS // P, P, D)
    w = i["L0_attn_weight_qkv"].reshape(KVH, QPG + 2, HD, KC, P)[:, [QPG, QPG + 1] + list(range(QPG))]
    g["wqkv"] = c(np.transpose(w, (0, 1, 4, 3, 2))).reshape(KVH * (QPG + 2), P, D)
    g["wproj"] = c(i["L0_attn_weight_proj"].T).reshape(KVH * QPG, P, D)
    g["w_nat"] = c(np.concatenate([i["L0_xattn_W" + n] for n in "qkv"])).reshape(3 * CH, P, D)
    g["b_nat"] = c(np.stack([i["L0_xattn_b" + n].reshape(CH, P) for n in "qkv"], 2).transpose(1, 0, 2))
    inter = np.repeat(i["L0_xattn_interference"][:, None], DK, axis=1).reshape(CH, P, MS)
    g["inter_rows"] = c(np.transpose(inter, (1, 0, 2)))
    g["amp_col"] = c(np.broadcast_to(i["L0_xattn_amp"].reshape(1, 1), (P, 1)))
    ctx = np.transpose(i["ctx_4096"].reshape(BLOCKS, BT, KC // 2, 2, P), (0, 2, 4, 3, 1))
    g["ctxT"] = c(ctx).reshape(BLOCKS * KC // 2, P, 2 * BT)
    wo = i["L0_xattn_Wo"].T.reshape(CH, 2, DK, MS, D)
    g["wo"] = c(np.transpose(wo, (0, 1, 3, 2, 4))).reshape(CH, P, D)
    g["bo"] = c(np.broadcast_to(i["L0_xattn_bo"][None], (P, D)))
    g["vh"] = c(np.concatenate([i["L0_ffn_Vh_top"], i["L0_ffn_Vh_tail"]])).reshape(KC, P, D)
    g["uT"] = c(np.concatenate([i["L0_ffn_U_top"].T, i["L0_ffn_U_tail"].T])).reshape(KC, P, D)
    g["s_all"] = c(np.concatenate([i["L0_ffn_S_top"], i["L0_ffn_S_tail"]]).reshape(KC, P).T)
    g["alpha"] = c(i["L0_ffn_alpha"].reshape(R_TOP, 1))
    g["beta"] = c(i["L0_ffn_beta"].reshape(R_TOP, 1))
    g["u_rT"] = c(i["L0_ffn_U_tail_r"].T)
    g["vh_r"] = c(i["L0_ffn_Vh_tail_r"])
    g["s_r"] = c(i["L0_ffn_S_tail_r"].reshape(R_INT, 1))
    g["d_r"] = c(i["L0_ffn_D"].reshape(R_INT, 1))
    g["r_mat"] = c(i["L0_ffn_R"])
    g["ffn_bias"] = c(np.broadcast_to(i["L0_ffn_bias"][None], (P, D)))
    return g


def kernel(**inputs):
    import concourse.bacc as bacc
    from concourse.bass_utils import run_bass_kernel_spmd

    given = layouts({name: np.asarray(a) for name, a in inputs.items()})
    nc = bacc.Bacc("TRN2", target_bir_lowering=False, num_devices=1, dynamic_dma_scratch_size=1024)
    aps = {name: nc.dram_tensor(f"in_{name}", a.shape, F32, kind="ExternalInput").ap()
           for name, a in given.items()}
    out = nc.dram_tensor("out_x", (TOKENS // P, P, D), F32, kind="ExternalOutput").ap()
    decoder_layer(nc, aps, out)
    r = run_bass_kernel_spmd(nc, [{f"in_{name}": a for name, a in given.items()}], core_ids=[0])
    return r.results[0]["out_x"].reshape(SEQ, TOKENS // SEQ, D)
```

```python
import numpy as np
import concourse.bass as bass
from concourse import mybir
from contextlib import ExitStack

F32 = mybir.dt.float32
F32R = mybir.dt.float32r
ALU = mybir.AluOpType
ACT = mybir.ActivationFunctionType
AX = mybir.AxisListType

P = 128
D = 1024
KC = D // P
HALF = 512
TOKENS = 2048
TILES = 4
BT = TILES * P
BLOCKS = TOKENS // BT
EPS = 1e-5
MASKED = -1e30

SEQ = 16
KVH = 8
QPG = 4
HD = 128
SELF_SCALE = 1.0 / HD ** 0.5

CH = D // P
SLOTS = 8
DK = 16
MS = 4
CROSS_SCALE = 1.0 / DK ** 0.5
VW = DK + 1

R_TOP = 64
R_INT = 4


def f32(ap):
    return ap.bitcast(F32)


def three_passes(nc, out, parts, first=True, last=True):
    for i, (ah, al, bh, bl) in enumerate(parts):
        nc.tensor.matmul(out, ah, bh, start=(first and i == 0), stop=False)
        nc.tensor.matmul(out, ah, bl, start=False, stop=False)
        ins = nc.tensor.matmul(out, al, bh, start=False, stop=(last and i == len(parts) - 1))
    return ins



def tile_of(array, index):
    return array[bass.ds(index, 1)].rearrange("a p n -> (a p) n")



def constants_phase(nc, sems, ident, causal, slotmask, mix, bias_qkv, eps, b_nat, inter_rows, amp_col):
    with ExitStack() as ctx:
        def sb(name, shape, dt=F32):
            return ctx.enter_context(nc.sbuf_tensor(name, shape, dt))

        def sem(name):
            return sems.enter_context(nc.semaphore(name))

        inter = sb("inter", [P, CH, MS])
        amp = sb("amp", [P, 1])
        amp01 = sb("amp01", [P, 1])
        same_hd = sb("same_hd", [P, 2 * DK])
        same_m = sb("same_m", [P, MS])
        mix_rows = sb("mix_rows", [P, CH, MS])
        bias_raw = sb("bias_raw", [P, CH, 3])
        bias_ps = ctx.enter_context(nc.psum_tensor("bias_ps", [P, HALF], F32))

        small_loaded = sem("set_small_loaded")
        masks_built = sem("set_masks_built")
        mix_steps = sem("set_mix_steps")
        mix_ready = sem("set_mix_ready")
        bias_mixed = sem("set_bias_mixed")
        bias_done = sem("set_bias_done")

        block = ctx.enter_context(nc.Block())

        @block.sync
        def _(sp):
            sp.dma_start(inter[:], inter_rows).then_inc(small_loaded, 16)
            sp.dma_start(amp[:], amp_col).then_inc(small_loaded, 16)
            sp.dma_start(bias_raw[:], b_nat).then_inc(small_loaded, 16)

        @block.gpsimd
        def _(pool):
            pool.memset(ident[:], 0.0).then_inc(masks_built, 1)
            pool.memset(causal[:], 0.0).then_inc(masks_built, 1)
            pool.memset(same_hd[:], 1.0).then_inc(masks_built, 1)
            pool.memset(slotmask[:], 1.0).then_inc(masks_built, 1)
            pool.wait_ge(masks_built, 4)
            pool.affine_select(out=ident[:], in_=ident[:], compare_op=ALU.not_equal, fill=1.0, base=0,
                               pattern=[[-1, P]], channel_multiplier=1).then_inc(masks_built, 1)
            pool.affine_select(out=causal[:], in_=causal[:], compare_op=ALU.is_ge, fill=MASKED, base=0,
                               pattern=[[-1, P]], channel_multiplier=1).then_inc(masks_built, 1)
            pool.affine_select(out=same_hd[:], in_=same_hd[:], compare_op=ALU.is_ge, fill=0.0, base=0,
                               pattern=[[-MS, 2 * DK]], channel_multiplier=1).then_inc(masks_built, 1)
            pool.affine_select(out=slotmask[:], in_=slotmask[:], compare_op=ALU.is_ge, fill=0.0, base=0,
                               pattern=[[-DK, SLOTS]], channel_multiplier=1).then_inc(masks_built, 1)
            pool.wait_ge(masks_built, 8)
            cv = causal[:].rearrange("p (j i) -> p j i", i=SEQ)
            pool.affine_select(out=cv, in_=cv, compare_op=ALU.is_ge, fill=MASKED, base=SEQ - 1,
                               pattern=[[SEQ, P // SEQ], [0, SEQ]], channel_multiplier=-1).then_inc(masks_built, 1)
            pool.affine_select(out=same_hd[:], in_=same_hd[:], compare_op=ALU.is_ge, fill=0.0, base=MS - 1,
                               pattern=[[MS, 2 * DK]], channel_multiplier=-1).then_inc(masks_built, 1)
            pool.affine_select(out=slotmask[:], in_=slotmask[:], compare_op=ALU.is_ge, fill=0.0, base=DK - 1,
                               pattern=[[DK, SLOTS]], channel_multiplier=-1).then_inc(masks_built, 1)

        @block.vector
        def _(dve):
            nc.vector.memset(eps[:], EPS).then_inc(mix_steps, 1)
            dve.wait_ge(masks_built, 11)
            nc.vector.tensor_reduce(same_m[:], ident[:].rearrange("p (k j) -> p j k", j=MS), AX.X,
                                    ALU.add).then_inc(mix_steps, 1)
            dve.wait_ge(small_loaded, 48)
            nc.vector.tensor_scalar(amp01[:], amp[:], 0.1, None, ALU.mult).then_inc(mix_steps, 1)
            dve.wait_ge(mix_steps, 3)
            for c in range(CH):
                ins = nc.vector.scalar_tensor_tensor(mix_rows[:, c], inter[:, c], amp01[:], same_m[:],
                                                     ALU.mult, ALU.add)
            ins.then_inc(mix_steps, 1)
            dve.wait_ge(mix_steps, 4)
            hd = same_hd[:].rearrange("p (h d) -> p h d", h=2)
            mv = mix[:].rearrange("p c (h j d) -> p c h j d", h=2, j=MS)
            for c in range(CH):
                for h in range(2):
                    ins = nc.vector.tensor_tensor(
                        mv[:, c, h], hd[:, h].unsqueeze(1).broadcast_to([P, MS, DK]),
                        mix_rows[:, c].unsqueeze(2).broadcast_to([P, MS, DK]), ALU.mult)
            ins.then_inc(mix_ready, 1)
            dve.wait_ge(bias_mixed, 1)
            nc.vector.tensor_copy(bias_qkv[:].rearrange("p c w -> p (c w)"),
                                  bias_ps[:, 0:CH * 3]).then_inc(bias_done, 1)

        @block.tensor
        def _(pe):
            pe.wait_ge(mix_ready, 1)
            pe.wait_ge(small_loaded, 48)
            for c in range(CH):
                ins = nc.tensor.matmul(bias_ps[:, c * 3:c * 3 + 3], mix[:, c], bias_raw[:, c],
                                       start=True, stop=True)
            ins.then_inc(bias_mixed, 1)



class NormBuffers:
    GROUPS = 2 * TILES

    def __init__(self, nc, ctx, sems, tag, eps, offset=None):
        self.nc, self.eps, self.offset = nc, eps, offset

        def sb(name, shape, dt=F32):
            return ctx.enter_context(nc.sbuf_tensor(f"{tag}_{name}", shape, dt))

        def sem(name):
            return sems.enter_context(nc.semaphore(f"{tag}_{name}"))

        self.x = sb("x", [P, TILES, D])
        self.stats = sb("stats", [P, TILES, 12])
        self.mv = sb("mv", [P, TILES, 2])
        self.std = sb("std", [P, TILES])
        self.idle = sb("idle", [P, 1])
        self.rstd = sb("rstd", [P, TILES])
        self.xh = sb("xh", [P, KC, BT], F32R)
        self.xl = sb("xl", [P, KC, BT], F32R)
        self.loaded = [sem(f"x_loaded{t}") for t in range(TILES)]
        self.offset_added = sem("offset_added") if offset is not None else None
        self.stats_done = sem("stats_done")
        self.moments_done = sem("moments_done")
        self.std_done = sem("std_done")
        self.rstd_done = sem("rstd_done")
        self.normal = sem("normal")
        self.turned = sem("turned")
        self.hi_done = sem("hi_done")
        self.lo_done = sem("lo_done")

    def moments(self, dve, b):
        nc = self.nc
        for t in range(TILES):
            dve.wait_ge(self.loaded[t], b * 16 + 16)
            if self.offset is not None:
                nc.vector.tensor_tensor(self.x[:, t], self.x[:, t], self.offset[:], ALU.add
                                        ).then_inc(self.offset_added, 1)
                dve.wait_ge(self.offset_added, b * TILES + (t + 1))
            nc.vector.bn_stats(self.stats[:, t, 0:6], self.x[:, t, 0:HALF])
            nc.vector.bn_stats(self.stats[:, t, 6:12], self.x[:, t, HALF:D]).then_inc(self.stats_done, 1)
            dve.wait_ge(self.stats_done, b * TILES + (t + 1))
            nc.vector.memset(self.idle[:], 0.0)
            nc.vector.bn_aggr(self.mv[:, t], self.stats[:, t]).then_inc(self.moments_done, 1)

    def deviations(self, act, b):
        act.wait_ge(self.moments_done, b * TILES + TILES)
        self.nc.scalar.activation(self.std[:], self.mv[:, :, 1], ACT.Sqrt, bias=self.eps[:]
                                  ).then_inc(self.std_done, 1)

    def normalise(self, dve, b):
        nc = self.nc
        dve.wait_ge(self.std_done, b + 1)
        nc.vector.reciprocal(self.rstd[:], self.std[:]).then_inc(self.rstd_done, 1)
        dve.wait_ge(self.rstd_done, b + 1)
        for t in range(TILES):
            nc.vector.tensor_scalar(self.x[:, t], self.x[:, t], self.mv[:, t, 0:1], self.rstd[:, t:t + 1],
                                    ALU.subtract, ALU.mult).then_inc(self.normal, 1)

    def turn(self, pe, b, r, ident, bank):
        t, half = r // 2, r % 2
        pe.wait_ge(self.normal, b * TILES + (t + 1))
        for k in range(4):
            ins = self.nc.tensor.transpose(bank[:, k * P:(k + 1) * P],
                                           self.x[:, t, (4 * half + k) * P:(4 * half + k + 1) * P], ident[:])
        ins.then_inc(self.turned, 1)

    def part(self, a, r):
        t, half = r // 2, r % 2
        return a[:, 4 * half:4 * half + 4, t * P:(t + 1) * P]

    def high(self, act, b, r, bank):
        act.wait_ge(self.turned, b * self.GROUPS + (r + 1))
        self.nc.scalar.activation(self.part(self.xh, r), bank[:].rearrange("p (k n) -> p k n", k=4), ACT.Copy
                                  ).then_inc(self.hi_done, 1)

    def low(self, dve, b, r, bank):
        dve.wait_ge(self.hi_done, b * self.GROUPS + (r + 1))
        self.nc.vector.tensor_tensor(self.part(self.xl, r), bank[:].rearrange("p (k n) -> p k n", k=4),
                                     f32(self.part(self.xh, r)), ALU.subtract).then_inc(self.lo_done, 1)


class Step:

    def __init__(self, b, g, par, proj=True, attn=True, nxt=True, next_g=None, cross=False, norm=False,
                 steady=True):
        self.b, self.g, self.par = b, g, par
        self.n = b * 8 + g
        self.m = self.n + (-1)
        self.proj, self.attn = proj, attn
        self.nxt = nxt
        self.next_g = g + 1 if next_g is None else next_g
        self.cross = cross
        self.norm = norm
        self.steady = steady
        self.attn_g = 7 if cross else g + (-1)
        self.attn_b = b + (-1) if cross else b


def pipeline(eng, first_block, step):
    def inner(b, steady):
        with eng.Fori(0, 3) as i:
            step(Step(b, i * 2 + 1, 1, steady=steady))
            step(Step(b, i * 2 + 2, 0, steady=steady))

    first_block()
    step(Step(0, 0, 0, attn=False, steady=False))
    with eng.Fori(0, BLOCKS - 1) as b:
        inner(b, True)
        step(Step(b, 7, 1, next_g=0, norm=True))
        step(Step(b + 1, 0, 0, cross=True))
    b = BLOCKS - 1
    inner(b, False)
    step(Step(b, 7, 1, nxt=False, steady=False))
    step(Step(b, 8, 0, proj=False, nxt=False, steady=False))



def self_attention_phase(nc, sems, ident, causal, mix, eps, x_rows, wqkv, wproj, w_nat, w_folded, x1):
    U = 2 + QPG
    PR = TILES * 2
    with ExitStack() as ctx:
        def sb(name, shape, dt=F32):
            return ctx.enter_context(nc.sbuf_tensor(name, shape, dt))

        def bank(name):
            return ctx.enter_context(nc.psum_tensor(name, [P, HALF], F32))

        def sem(name):
            return sems.enter_context(nc.semaphore(name))

        ln = NormBuffers(nc, ctx, sems, "sa_ln", eps)
        acc = sb("sa_acc", [P, TILES, D])
        wraw = sb("sa_wraw", [P, 3, D])
        wh = sb("sa_wh", [P, 3, D], F32R)
        wl = sb("sa_wl", [P, 3, D], F32R)
        praw = sb("sa_praw", [P, QPG, D])
        ph = sb("sa_ph", [P, QPG, D], F32R)
        pl = sb("sa_pl", [P, QPG, D], F32R)
        kT = sb("sa_kT", [P, 2, BT])
        qT = sb("sa_qT", [P, 2, QPG, BT])
        vT = sb("sa_vT", [P, BT])
        v = sb("sa_v", [P, 2, TILES, HD])
        probs = sb("sa_probs", [P, QPG, P])
        probsT = sb("sa_probsT", [P, QPG * P])
        top = sb("sa_top", [P, QPG])
        total = sb("sa_total", [P, QPG])
        inv = sb("sa_inv", [P, QPG])
        oh = sb("sa_oh", [P, QPG * P], F32R)
        ol = sb("sa_ol", [P, QPG * P], F32R)
        nat = sb("sa_nat", [P, D])
        fold = sb("sa_fold", [P, D])

        u_ps = [bank(f"sa_u{i}") for i in range(2)]
        pr_ps = [bank(f"sa_pr{i}") for i in range(2)]
        s_ps, t_ps, o_ps, v_ps = bank("sa_s"), bank("sa_t"), bank("sa_o"), bank("sa_vt")
        turn_ps = [s_ps, t_ps, o_ps, v_ps]

        wraw_loaded = [sem(f"sa_wraw_loaded{i}") for i in range(3)]
        praw_loaded = [sem(f"sa_praw_loaded{i}") for i in range(QPG)]
        acc_loaded = [sem(f"sa_acc_loaded{t}") for t in range(TILES)]
        x1_stored = [sem(f"sa_x1_stored{t}") for t in range(TILES)]
        w_hi = sem("sa_w_hi")
        w_split = sem("sa_w_split")
        p_hi = sem("sa_p_hi")
        p_split = sem("sa_p_split")
        u_done = sem("sa_u_done")
        u_copied = sem("sa_u_copied")
        v_turned = sem("sa_v_turned")
        v_copied = sem("sa_v_copied")
        s_done = sem("sa_s_done")
        s_masked = sem("sa_s_masked")
        s_top = sem("sa_s_top")
        s_shifted = sem("sa_s_shifted")
        exp_done = sem("sa_exp_done")
        total_done = sem("sa_total_done")
        inv_done = sem("sa_inv_done")
        probs_ready = sem("sa_probs_ready")
        probs_turned = sem("sa_probs_turned")
        probsT_ready = sem("sa_probsT_ready")
        o_done = sem("sa_o_done")
        o_hi = sem("sa_o_hi")
        o_split = sem("sa_o_split")
        pr_done = sem("sa_pr_done")
        pr_free = sem("sa_pr_free")
        nat_loaded = sem("sa_nat_loaded")
        folded = sem("sa_folded")
        fold_stored = sem("sa_fold_stored")

        def v_uses(s):
            if not s.attn:
                return 0
            return s.n * 3 + (-2) if s.steady else s.n + 2 * 8 * (BLOCKS - 1)

        block = ctx.enter_context(nc.Block())

        @block.sync
        def _(sp):
            def weights(s, g, n, u):
                sp.wait_ge(w_split, n * U + (u + 1))
                sp.dma_start(wraw[:, u % 3], tile_of(wqkv, g * U + u)).then_inc(wraw_loaded[u % 3], 16)

            def load_x(b):
                for t in range(TILES):
                    sp.dma_start(ln.x[:, t], tile_of(x_rows, b * TILES + t)).then_inc(ln.loaded[t], 16)

            def load_acc(b):
                for t in range(TILES):
                    sp.dma_start(acc[:, t], tile_of(x_rows, b * TILES + t)).then_inc(acc_loaded[t], 16)

            def first_block():
                load_x(0)
                for u in range(3):
                    weights(None, 0, 0, u)

            def step(s):
                if s.steady:
                    sp.wait_ge(folded, s.m * 2 + 2)
                    sp.dma_start(nat[:], tile_of(w_nat, s.m)).then_inc(nat_loaded, 16)
                if s.proj:
                    for u in range(3, U):
                        weights(s, s.g, s.n, u)
                    for h in range(QPG):
                        sp.wait_ge(p_split, s.n * QPG + (h + 1))
                        sp.dma_start(praw[:, h], tile_of(wproj, s.g * QPG + h)).then_inc(praw_loaded[h], 16)
                if s.norm:
                    sp.wait_ge(ln.turned, s.b * ln.GROUPS + ln.GROUPS)
                    load_x(s.b + 1)
                if s.nxt:
                    for u in range(3):
                        weights(s, s.next_g, s.n + 1, u)
                if s.proj and not s.attn:
                    load_acc(0)
                if s.cross:
                    for t in range(TILES):
                        sp.wait_ge(x1_stored[t], s.b * 16)
                    load_acc(s.b)

            pipeline(sp, first_block, step)

        @block.gpsimd
        def _(pool):
            pool.sem_inc(w_split, 3)
            pool.sem_inc(p_split, QPG)

            def weights(n, u):
                pool.wait_ge(w_hi, n * U + (u + 1))
                nc.gpsimd.tensor_tensor(wl[:, u % 3], wraw[:, u % 3], f32(wh[:, u % 3]), ALU.subtract
                                        ).then_inc(w_split, 1)

            def first_block():
                for u in range(3):
                    weights(0, u)

            def step(s):
                if s.attn:
                    for h in range(QPG):
                        pool.wait_ge(p_hi, s.m * QPG + (h + 1))
                        nc.gpsimd.tensor_tensor(pl[:, h], praw[:, h], f32(ph[:, h]), ALU.subtract
                                                ).then_inc(p_split, 1)
                if s.proj:
                    for u in range(3, U):
                        weights(s.n, u)
                if s.nxt:
                    for u in range(3):
                        weights(s.n + 1, u)

            pipeline(pool, first_block, step)

        @block.tensor
        def _(pe):
            pe.sem_inc(pr_done, 1)
            pe.sem_inc(folded, 2)

            def turn_groups(b, rs, banks_used):
                for r in rs:
                    if r >= 4:
                        pe.wait_ge(ln.lo_done, b * ln.GROUPS + (r - 3))
                    ln.turn(pe, b, r, ident, turn_ps[r % 4])

            def first_block():
                turn_groups(0, range(8), False)

            def step(s):
                n, m, mp = s.n, s.m, 1 - s.par
                v0 = v_uses(s)

                def unit(u):
                    if not s.proj:
                        return
                    if u == 0:
                        pe.wait_ge(ln.lo_done, s.b * ln.GROUPS + ln.GROUPS)
                    pe.wait_ge(w_split, n * U + (u + 4))
                    pe.wait_ge(u_copied, n * U + (u + 1))
                    three_passes(nc, u_ps[u % 2][:],
                                 [(wh[:, u % 3, k * P:(k + 1) * P], wl[:, u % 3, k * P:(k + 1) * P],
                                   ln.xh[:, k], ln.xl[:, k]) for k in range(KC)]).then_inc(u_done, 1)

                def turn_v():
                    if not s.proj:
                        return
                    pe.wait_ge(u_copied, n * U + 4)
                    pe.wait_ge(v_copied, v0 + 1)
                    for t in range(TILES):
                        ins = nc.tensor.transpose(v_ps[:, t * P:(t + 1) * P], vT[:, t * P:(t + 1) * P], ident[:])
                    ins.then_inc(v_turned, 1)

                def fold_half(half):
                    if not s.steady:
                        return
                    if half == 0:
                        pe.wait_ge(nat_loaded, m * 16 + 16)
                    pe.wait_ge(v_copied, v0 + (half + 2))
                    mixer = mix[:, 7] if s.cross else mix[:, bass.ds(s.attn_g, 1)].rearrange("p a n -> p (a n)")
                    for k in range(4):
                        ins = nc.tensor.matmul(v_ps[:, k * P:(k + 1) * P],
                                               nat[:, (4 * half + k) * P:(4 * half + k + 1) * P], mixer,
                                               start=True, stop=True)
                    ins.then_inc(folded, 1)

                def scores(t):
                    if not s.attn:
                        return
                    if t == 0:
                        pe.wait_ge(u_copied, n * U + 2)
                        if s.cross:
                            pe.wait_ge(ln.lo_done, s.b * ln.GROUPS + 5)
                    pe.wait_ge(s_masked, m * TILES + (t + 1))
                    for h in range(QPG):
                        ins = nc.tensor.matmul(s_ps[:, h * P:(h + 1) * P], qT[:, mp, h, t * P:(t + 1) * P],
                                               kT[:, mp, t * P:(t + 1) * P], start=True, stop=True)
                    ins.then_inc(s_done, 1)

                def turn_probs(t):
                    if not s.attn:
                        return
                    pe.wait_ge(probs_ready, m * TILES + (t + 1))
                    pe.wait_ge(probsT_ready, m * TILES + (t + 1))
                    for h in range(QPG):
                        ins = nc.tensor.transpose(t_ps[:, h * P:(h + 1) * P], probs[:, h], ident[:])
                    ins.then_inc(probs_turned, 1)

                def mix_values(t):
                    if not s.attn:
                        return
                    if t == 0:
                        pe.wait_ge(v_copied, v0 + 1)
                    pe.wait_ge(probsT_ready, m * TILES + (t + 2))
                    pe.wait_ge(o_split, m * TILES + (t + 1))
                    nc.tensor.matmul(o_ps[:], v[:, mp, t], probsT[:], start=True, stop=True).then_inc(o_done, 1)

                def project(t):
                    if not s.attn:
                        return
                    if t == 0:
                        pe.wait_ge(p_split, m * QPG + 2 * QPG)
                    pe.wait_ge(o_split, m * TILES + (t + 2))
                    for half in range(2):
                        pe.wait_ge(pr_free, m * PR + (2 * t + half + 1))
                        cols = slice(half * HALF, (half + 1) * HALF)
                        ins = three_passes(nc, pr_ps[half][:],
                                           [(oh[:, h * P:(h + 1) * P], ol[:, h * P:(h + 1) * P],
                                             ph[:, h, cols], pl[:, h, cols]) for h in range(QPG)])
                        ins.then_inc(pr_done, 1)

                scores(0)
                unit(0)
                turn_probs(0)
                scores(1)
                unit(1)
                mix_values(0)
                turn_probs(1)
                scores(2)
                unit(2)
                turn_v()
                project(0)
                mix_values(1)
                turn_probs(2)
                scores(3)
                unit(3)
                fold_half(0)
                project(1)
                mix_values(2)
                turn_probs(3)
                unit(4)
                fold_half(1)
                project(2)
                mix_values(3)
                unit(5)
                if s.norm:
                    pe.wait_ge(o_split, m * TILES + (TILES + 1))
                    pe.wait_ge(v_copied, v0 + 4)
                    turn_groups(s.b + 1, range(4), True)
                project(3)
                if s.norm:
                    turn_groups(s.b + 1, range(4, 8), True)

            pipeline(pe, first_block, step)

        @block.scalar
        def _(act):
            act.sem_inc(u_copied, 2)
            act.sem_inc(v_copied, 1)
            act.sem_inc(probsT_ready, 1)
            act.sem_inc(fold_stored, 16)

            def weights(n, u):
                act.wait_ge(wraw_loaded[u % 3], n * 32 + (16 * (u // 3) + 16))
                nc.scalar.activation(wh[:, u % 3], wraw[:, u % 3], ACT.Copy).then_inc(w_hi, 1)

            def first_block():
                for u in range(3):
                    weights(0, u)
                ln.deviations(act, 0)
                for r in range(8):
                    ln.high(act, 0, r, turn_ps[r % 4])

            def step(s):
                n, m = s.n, s.m
                v0 = v_uses(s)
                dst = [kT[:, s.par], vT[:]] + [qT[:, s.par, h] for h in range(QPG)]

                def copy_unit(u):
                    if not s.proj:
                        return
                    act.wait_ge(u_done, n * U + (u + 1))
                    nc.scalar.activation(dst[u], u_ps[u % 2][:], ACT.Copy).then_inc(u_copied, 1)
                    if u < 3:
                        weights(n, u + 3)
                    elif s.nxt:
                        weights(n + 1, u - 3)

                def copy_v():
                    if not s.proj:
                        return
                    act.wait_ge(v_turned, n + 1)
                    nc.scalar.activation(v[:, s.par].rearrange("p t d -> p (t d)"), v_ps[:], ACT.Copy
                                         ).then_inc(v_copied, 1)

                def copy_fold(half):
                    if not s.steady:
                        return
                    act.wait_ge(folded, m * 2 + (half + 3))
                    if half == 0:
                        act.wait_ge(fold_stored, m * 16 + 16)
                    nc.scalar.activation(fold[:, half * HALF:(half + 1) * HALF], v_ps[:], ACT.Copy
                                         ).then_inc(v_copied, 1)

                def store_fold():
                    if not s.steady:
                        return
                    act.wait_ge(v_copied, v0 + 4)
                    act.dma_start(tile_of(w_folded, m), fold[:]).then_inc(fold_stored, 16)

                def out_weights(hs):
                    if not s.attn:
                        return
                    act.wait_ge(pr_done, m * PR + 1)
                    for h in hs:
                        act.wait_ge(praw_loaded[h], n * 16)
                        nc.scalar.activation(ph[:, h], praw[:, h], ACT.Copy).then_inc(p_hi, 1)

                def exps(t):
                    if not s.attn:
                        return
                    act.wait_ge(s_shifted, m * TILES + (t + 1))
                    nc.scalar.activation(probs[:], probs[:], ACT.Exp, scale=SELF_SCALE).then_inc(exp_done, 1)

                def copy_probs(t):
                    if not s.attn:
                        return
                    act.wait_ge(probs_turned, m * TILES + (t + 1))
                    nc.scalar.activation(probsT[:], t_ps[:], ACT.Copy).then_inc(probsT_ready, 1)

                def high_o(t):
                    if not s.attn:
                        return
                    act.wait_ge(o_done, m * TILES + (t + 1))
                    nc.scalar.activation(oh[:], o_ps[:], ACT.Copy).then_inc(o_hi, 1)

                out_weights([0, 1])
                exps(0)
                copy_unit(0)
                copy_probs(0)
                out_weights([2, 3])
                exps(1)
                copy_unit(1)
                high_o(0)
                copy_probs(1)
                exps(2)
                copy_unit(2)
                copy_v()
                high_o(1)
                copy_probs(2)
                exps(3)
                copy_unit(3)
                copy_fold(0)
                high_o(2)
                copy_probs(3)
                copy_unit(4)
                copy_fold(1)
                store_fold()
                high_o(3)
                if s.norm:
                    ln.deviations(act, s.b + 1)
                copy_unit(5)
                if s.norm:
                    for r in range(8):
                        ln.high(act, s.b + 1, r, turn_ps[r % 4])
                if s.cross or not s.proj:
                    for t in range(TILES):
                        act.wait_ge(pr_free, m * PR + (2 * t + 4))
                        act.dma_start(tile_of(x1, s.attn_b * TILES + t), acc[:, t]).then_inc(x1_stored[t], 16)

            pipeline(act, first_block, step)
            for t in range(TILES):
                act.wait_ge(x1_stored[t], 16 * BLOCKS)
            act.wait_ge(fold_stored, 16 * (3 * CH + 1))

        @block.vector
        def _(dve):
            dve.sem_inc(s_masked, 1)
            dve.sem_inc(o_split, 1)
            dve.sem_inc(pr_free, 2)

            def first_block():
                ln.moments(dve, 0)
                ln.normalise(dve, 0)
                for r in range(8):
                    ln.low(dve, 0, r, turn_ps[r % 4])

            def step(s):
                if not s.attn:
                    return
                m = s.m

                def softmax(t):
                    i = m * TILES + (t + 1)
                    dve.wait_ge(s_done, i)
                    nc.vector.tensor_tensor(probs[:], s_ps[:].rearrange("p (h n) -> p h n", h=QPG),
                                            causal[:].unsqueeze(1).broadcast_to([P, QPG, P]), ALU.add
                                            ).then_inc(s_masked, 1)
                    dve.wait_ge(s_masked, i + 1)
                    nc.vector.tensor_reduce(top[:], probs[:], AX.X, ALU.max).then_inc(s_top, 1)
                    dve.wait_ge(s_top, i)
                    nc.vector.tensor_tensor(probs[:], probs[:], top[:].unsqueeze(2).broadcast_to([P, QPG, P]),
                                            ALU.subtract).then_inc(s_shifted, 1)
                    dve.wait_ge(exp_done, i)
                    nc.vector.tensor_reduce(total[:], probs[:], AX.X, ALU.add).then_inc(total_done, 1)
                    dve.wait_ge(total_done, i)
                    nc.vector.reciprocal(inv[:], total[:]).then_inc(inv_done, 1)
                    dve.wait_ge(inv_done, i)
                    nc.vector.tensor_tensor(probs[:], probs[:], inv[:].unsqueeze(2).broadcast_to([P, QPG, P]),
                                            ALU.mult).then_inc(probs_ready, 1)

                def low_o(t):
                    dve.wait_ge(o_hi, m * TILES + (t + 1))
                    nc.vector.tensor_tensor(ol[:], o_ps[:], f32(oh[:]), ALU.subtract).then_inc(o_split, 1)

                def add_projected(t):
                    dve.wait_ge(acc_loaded[t], s.attn_b * 16 + 16)
                    for half in range(2):
                        dve.wait_ge(pr_done, m * PR + (2 * t + half + 2))
                        part = acc[:, t, half * HALF:(half + 1) * HALF]
                        nc.vector.tensor_tensor(part, pr_ps[half][:], part, ALU.add).then_inc(pr_free, 1)

                softmax(0)
                softmax(1)
                low_o(0)
                softmax(2)
                add_projected(0)
                low_o(1)
                softmax(3)
                add_projected(1)
                low_o(2)
                add_projected(2)
                low_o(3)
                if s.norm:
                    ln.moments(dve, s.b + 1)
                    ln.normalise(dve, s.b + 1)
                    for r in range(4):
                        ln.low(dve, s.b + 1, r, turn_ps[r % 4])
                add_projected(3)
                if s.norm:
                    for r in range(4, 8):
                        ln.low(dve, s.b + 1, r, turn_ps[r % 4])

            pipeline(dve, first_block, step)



def cross_attention_phase(nc, sems, ident, slotmask, bias_qkv, eps, x1, ctxT, w_folded, wo, x2):
    PIECE = 2
    PR = TILES * 2
    U = 3
    WHICH = [1, 2, 0]
    DP = 32
    with ExitStack() as ctx:
        def sb(name, shape, dt=F32):
            return ctx.enter_context(nc.sbuf_tensor(name, shape, dt))

        def psum(name, cols=HALF):
            return ctx.enter_context(nc.psum_tensor(name, [P, cols], F32))

        def sem(name):
            return sems.enter_context(nc.semaphore(name))

        ln = NormBuffers(nc, ctx, sems, "ca_ln", eps)
        acc = sb("ca_acc", [P, TILES, D])
        craw = sb("ca_craw", [P, 2, BT])
        ch = sb("ca_ch", [P, KC, BT], F32R)
        cl = sb("ca_cl", [P, KC, BT], F32R)
        wraw = sb("ca_wraw", [P, U, D])
        wh = sb("ca_wh", [P, U, D], F32R)
        wl = sb("ca_wl", [P, U, D], F32R)
        oraw = sb("ca_oraw", [P, D])
        owh = sb("ca_owh", [P, D], F32R)
        owl = sb("ca_owl", [P, D], F32R)
        kh = sb("ca_kh", [P, 2, BT], F32R)
        kl = sb("ca_kl", [P, 2, BT], F32R)
        qh = sb("ca_qh", [P, 2, BT], F32R)
        ql = sb("ca_ql", [P, 2, BT], F32R)
        vT = sb("ca_vT", [P, BT])
        v = sb("ca_v", [P, 2, TILES * SLOTS, DP])
        kmh = sb("ca_kmh", [P, 2, SLOTS, P], F32R)
        kml = sb("ca_kml", [P, 2, SLOTS, P], F32R)
        probs = sb("ca_probs", [P, 2, SLOTS, P])
        probsT = sb("ca_probsT", [P, SLOTS * P])
        bias_now = sb("ca_bias_now", [P, 2, 3])
        top = sb("ca_top", [P, SLOTS])
        inv = sb("ca_inv", [P, SLOTS])
        oT = sb("ca_oT", [P, 2 * P])
        o = sb("ca_o", [P, P])
        oh = sb("ca_oh", [P, P], F32R)
        ol = sb("ca_ol", [P, P], F32R)

        u_ps = [psum(f"ca_u{i}") for i in range(2)]
        s_ps = psum("ca_s", 2 * HALF)
        t_ps = psum("ca_t", 2 * HALF)
        o_ps = psum("ca_o_ps")
        x_ps = psum("ca_x")

        acc_loaded = [sem(f"ca_acc_loaded{t}") for t in range(TILES)]
        craw_loaded = [sem(f"ca_craw_loaded{i}") for i in range(2)]
        c_hi = sem("ca_c_hi")
        c_split = sem("ca_c_split")
        wraw_loaded = [sem(f"ca_wraw_loaded{u}") for u in range(U)]
        w_hi = sem("ca_w_hi")
        w_split = sem("ca_w_split")
        oraw_loaded = sem("ca_oraw_loaded")
        ow_hi = sem("ca_ow_hi")
        ow_split = sem("ca_ow_split")
        u_done = sem("ca_u_done")
        u_hi = sem("ca_u_hi")
        u_free = sem("ca_u_free")
        bias_ready = sem("ca_bias_ready")
        v_set = sem("ca_v_set")
        v_turned = sem("ca_v_turned")
        v_placed = sem("ca_v_placed")
        km_ready = sem("ca_km_ready")
        s_done = sem("ca_s_done")
        s_top = sem("ca_s_top")
        s_shifted = sem("ca_s_shifted")
        probs_ready = sem("ca_probs_ready")
        probs_turned = sem("ca_probs_turned")
        probsT_ready = sem("ca_probsT_ready")
        pv_done = sem("ca_pv_done")
        oT_ready = sem("ca_oT_ready")
        oT_turned = sem("ca_oT_turned")
        inv_done = sem("ca_inv_done")
        o_ready = sem("ca_o_ready")
        o_turned = sem("ca_o_turned")
        o_hi = sem("ca_o_hi")
        o_split = sem("ca_o_split")
        pr_done = sem("ca_pr_done")
        x_free = sem("ca_x_free")
        x2_stored = [sem(f"ca_x2_stored{t}") for t in range(TILES)]

        x1_by_i = x1.rearrange("t p n -> (t p) n").rearrange("(j i) n -> i j n", i=SEQ)

        block = ctx.enter_context(nc.Block())

        def turns(s):
            return s.cross or not s.attn

        @block.sync
        def _(sp):
            def weights(g, n, u):
                sp.wait_ge(w_split, n * U + (u + 1))
                sp.dma_start(wraw[:, u], tile_of(w_folded, g + WHICH[u] * CH)).then_inc(wraw_loaded[u], 16)

            def load(b, dst, sem_of_tile):
                for t in range(TILES):
                    sp.dma_start(dst[:, t], tile_of(x1_by_i, b * TILES + t)).then_inc(sem_of_tile[t], 16)

            def load_context(b, ks):
                for k in ks:
                    sp.wait_ge(c_split, b * KC + (k + 1))
                    sp.dma_start(craw[:, k % 2], tile_of(ctxT, b * KC + k)).then_inc(craw_loaded[k % 2], 16)

            def first_block():
                weights(0, 0, 0)
                load_context(0, range(KC))
                load(0, ln.x, ln.loaded)
                weights(0, 0, 1)
                weights(0, 0, 2)

            def step(s):
                if s.attn:
                    sp.wait_ge(ow_split, s.n)
                    sp.dma_start(oraw[:], tile_of(wo, s.attn_g)).then_inc(oraw_loaded, 16)
                if s.norm:
                    sp.wait_ge(ln.turned, s.b * ln.GROUPS + ln.GROUPS)
                    load(s.b + 1, ln.x, ln.loaded)
                    load_context(s.b + 1, range(2))
                if s.nxt:
                    for u in range(U):
                        weights(s.next_g, s.n + 1, u)
                if s.norm:
                    load_context(s.b + 1, range(2, KC))
                if not s.attn:
                    load(0, acc, acc_loaded)
                if s.cross:
                    for t in range(TILES):
                        sp.wait_ge(x2_stored[t], s.b * 16)
                    load(s.b, acc, acc_loaded)

            pipeline(sp, first_block, step)

        @block.gpsimd
        def _(pool):
            pool.sem_inc(w_split, 3)
            pool.sem_inc(ow_split, 1)
            nc.gpsimd.memset(v[:], 0.0).then_inc(v_set, 1)
            pool.wait_ge(v_set, 1)
            nc.gpsimd.memset(v[:, :, :, DK:VW], 1.0).then_inc(v_set, 1)

            def weights(n, u):
                pool.wait_ge(w_hi, n * U + (u + 1))
                nc.gpsimd.tensor_tensor(wl[:, u], wraw[:, u], f32(wh[:, u]), ALU.subtract).then_inc(w_split, 1)

            def masked_k(n, par, t):
                pool.wait_ge(s_done, n * TILES + (t + 1))
                mask = slotmask[:].unsqueeze(2).broadcast_to([P, SLOTS, P])
                for dst, src in ((kmh, kh), (kml, kl)):
                    ins = nc.gpsimd.tensor_tensor(
                        dst[:, t % 2], f32(src[:, par, t * P:(t + 1) * P]).unsqueeze(1).broadcast_to([P, SLOTS, P]),
                        mask, ALU.mult)
                ins.then_inc(km_ready, 1)

            def first_block():
                for u in range(U):
                    weights(0, u)

            def step(s):
                if s.attn:
                    pool.wait_ge(ow_hi, s.n)
                    nc.gpsimd.tensor_tensor(owl[:], oraw[:], f32(owh[:]), ALU.subtract).then_inc(ow_split, 1)
                    masked_k(s.m, 1 - s.par, 2)
                    masked_k(s.m, 1 - s.par, 3)
                if s.nxt:
                    weights(s.n + 1, 0)
                if s.proj:
                    pool.wait_ge(u_free, s.n * U + 3)
                    masked_k(s.n, s.par, 0)
                if s.nxt:
                    weights(s.n + 1, 1)
                if s.proj:
                    masked_k(s.n, s.par, 1)
                if s.nxt:
                    weights(s.n + 1, 2)

            pipeline(pool, first_block, step)

        @block.tensor
        def _(pe):
            pe.sem_inc(s_done, 2)
            pe.sem_inc(pr_done, 1)

            def first_block():
                pass

            def step(s):
                n, m, mp = s.n, s.m, 1 - s.par

                def piece(i):
                    if not s.proj:
                        return
                    u, q = i // 4, i % 4
                    if q == 0:
                        pe.wait_ge(w_split, n * U + (u + 4))
                        if u == 2 and turns(s):
                            pe.wait_ge(ln.lo_done, s.b * ln.GROUPS + ln.GROUPS)
                        pe.wait_ge(u_free, n * U + (u + 1))
                    if u == 0 and turns(s):
                        pe.wait_ge(c_split, s.b * KC + (q * PIECE + PIECE + 2))
                    bh, bl = (ln.xh, ln.xl) if u == 2 else (ch, cl)
                    ins = three_passes(nc, u_ps[(s.par * U + u) % 2][:],
                                       [(wh[:, u, k * P:(k + 1) * P], wl[:, u, k * P:(k + 1) * P],
                                         bh[:, k], bl[:, k]) for k in range(q * PIECE, (q + 1) * PIECE)],
                                       first=q == 0, last=q == 3)
                    if q == 3:
                        ins.then_inc(u_done, 1)

                def turn_x(r):
                    if not turns(s):
                        return
                    if r:
                        pe.wait_ge(ln.lo_done, s.b * ln.GROUPS + r)
                    elif s.attn:
                        pe.wait_ge(x_free, m * PR + 1)
                    ln.turn(pe, s.b, r, ident, x_ps)

                def turn_v():
                    if not s.proj:
                        return
                    pe.wait_ge(u_free, n * U + 4)
                    if s.attn:
                        pe.wait_ge(probsT_ready, m * TILES + 4)
                    for t in range(TILES):
                        ins = nc.tensor.transpose(t_ps[:, t * P:(t + 1) * P], vT[:, t * P:(t + 1) * P], ident[:])
                    ins.then_inc(v_turned, 1)

                def scores(t):
                    if not s.attn:
                        return
                    if t == 0:
                        pe.wait_ge(u_free, n * U + 2)
                    pe.wait_ge(km_ready, m * TILES + (t + 1))
                    pe.wait_ge(s_shifted, m * TILES + (t + 1))
                    for half in range(2):
                        sl = slice(4 * half, 4 * half + 4)
                        ins = three_passes(nc, s_ps[:, half * HALF:(half + 1) * HALF],
                                           [(qh[:, mp, t * P:(t + 1) * P], ql[:, mp, t * P:(t + 1) * P],
                                             kmh[:, t % 2, sl], kml[:, t % 2, sl])])
                    ins.then_inc(s_done, 1)

                def turn_probs(t):
                    if not s.attn:
                        return
                    if t == 0:
                        pe.wait_ge(v_placed, n)
                    if t == 3 and s.proj:
                        pe.wait_ge(v_placed, n + 1)
                    pe.wait_ge(probs_ready, m * TILES + (t + 1))
                    pe.wait_ge(probsT_ready, m * TILES + (t + 1))
                    for j in range(SLOTS):
                        ins = nc.tensor.transpose(t_ps[:, j * P:(j + 1) * P], probs[:, t % 2, j], ident[:])
                    ins.then_inc(probs_turned, 1)

                def mix_values(t):
                    if not s.attn:
                        return
                    pe.wait_ge(probsT_ready, m * TILES + (t + 2))
                    pe.wait_ge(o_split, m * TILES + (t + 1))
                    for j in range(SLOTS):
                        rows = slice(DP * (j % 4), DP * (j % 4 + 1))
                        ins = nc.tensor.matmul(o_ps[rows, (j // 4) * P:(j // 4 + 1) * P],
                                               v[:, mp, t * SLOTS + j], probsT[:, j * P:(j + 1) * P],
                                               start=True, stop=True)
                    ins.then_inc(pv_done, 1)

                def turn_oT(t):
                    if not s.attn:
                        return
                    pe.wait_ge(oT_ready, m * TILES + (t + 1))
                    for a in range(2):
                        ins = nc.tensor.transpose(o_ps[:, (2 + a) * P:(3 + a) * P], oT[:, a * P:(a + 1) * P],
                                                  ident[:])
                    ins.then_inc(oT_turned, 1)

                def turn_o(t):
                    if not s.attn:
                        return
                    pe.wait_ge(o_ready, m * TILES + (t + 1))
                    nc.tensor.transpose(o_ps[:, 0:P], o[:], ident[:]).then_inc(o_turned, 1)

                def project(t, half):
                    if not s.attn:
                        return
                    if t == 0 and half == 0:
                        pe.wait_ge(ow_split, m + 2)
                        if s.cross:
                            pe.wait_ge(ln.lo_done, s.b * ln.GROUPS + ln.GROUPS)
                    if half == 0:
                        pe.wait_ge(o_split, m * TILES + (t + 2))
                    pe.wait_ge(x_free, m * PR + (2 * t + half + 1))
                    cols = slice(half * HALF, (half + 1) * HALF)
                    three_passes(nc, x_ps[:], [(oh[:], ol[:], owh[:, cols], owl[:, cols])]).then_inc(pr_done, 1)

                scores(0)
                turn_x(0)
                piece(0)
                turn_x(1)
                piece(1)
                scores(1)
                turn_x(2)
                piece(2)
                turn_probs(0)
                turn_x(3)
                piece(3)
                scores(2)
                turn_x(4)
                piece(4)
                mix_values(0)
                turn_probs(1)
                turn_x(5)
                piece(5)
                turn_oT(0)
                scores(3)
                turn_x(6)
                piece(6)
                turn_o(0)
                mix_values(1)
                turn_probs(2)
                turn_x(7)
                project(0, 0)
                piece(7)
                turn_oT(1)
                project(0, 1)
                piece(8)
                turn_o(1)
                turn_v()
                mix_values(2)
                project(1, 0)
                piece(9)
                turn_oT(2)
                turn_probs(3)
                project(1, 1)
                piece(10)
                turn_o(2)
                piece(11)
                mix_values(3)
                project(2, 0)
                turn_oT(3)
                project(2, 1)
                turn_o(3)
                project(3, 0)
                project(3, 1)

            pipeline(pe, first_block, step)

        @block.scalar
        def _(act):
            act.sem_inc(probsT_ready, 1)

            def weights(n, u):
                act.wait_ge(wraw_loaded[u], n * 16 + 16)
                nc.scalar.activation(wh[:, u], wraw[:, u], ACT.Copy).then_inc(w_hi, 1)

            def context_high(b, ks):
                for k in ks:
                    act.wait_ge(craw_loaded[k % 2], b * (8 * KC) + (16 * (k // 2) + 16))
                    nc.scalar.activation(ch[:, k], craw[:, k % 2], ACT.Copy).then_inc(c_hi, 1)

            def first_block():
                weights(0, 0)
                context_high(0, range(KC))
                weights(0, 1)
                weights(0, 2)
                ln.deviations(act, 0)

            def step(s):
                n, m = s.n, s.m

                def set_bias():
                    if not s.proj:
                        return
                    src = bias_qkv[:, s.g] if isinstance(s.g, int) else bias_qkv[:, bass.ds(s.g, 1)].rearrange("p a w -> p (a w)")
                    nc.scalar.activation(bias_now[:, s.par], src, ACT.Copy).then_inc(bias_ready, 1)

                def high_unit(u, dst):
                    if not s.proj:
                        return
                    act.wait_ge(bias_ready, n + 1)
                    act.wait_ge(u_done, n * U + (u + 1))
                    w = WHICH[u]
                    nc.scalar.activation(dst[:, s.par], u_ps[(s.par * U + u) % 2][:], ACT.Identity,
                                         bias=bias_now[:, s.par, w:w + 1]).then_inc(u_hi, 1)

                def next_weights(u):
                    if s.nxt:
                        act.wait_ge(u_done, n * U + (u + 1))
                        weights(n + 1, u)

                def out_weights():
                    if not s.attn:
                        return
                    act.wait_ge(pr_done, m * PR + 1)
                    act.wait_ge(oraw_loaded, n * 16)
                    nc.scalar.activation(owh[:], oraw[:], ACT.Copy).then_inc(ow_hi, 1)

                def exps(t):
                    if not s.attn:
                        return
                    act.wait_ge(s_shifted, m * TILES + (t + 2))
                    nc.scalar.activation(probs[:, t % 2], probs[:, t % 2], ACT.Exp, scale=CROSS_SCALE
                                         ).then_inc(probs_ready, 1)

                def copy_probs(t):
                    if not s.attn:
                        return
                    act.wait_ge(probs_turned, m * TILES + (t + 1))
                    nc.scalar.activation(probsT[:], t_ps[:], ACT.Copy).then_inc(probsT_ready, 1)

                def copy_oT(t):
                    if not s.attn:
                        return
                    act.wait_ge(pv_done, m * TILES + (t + 1))
                    nc.scalar.activation(oT[:], o_ps[:, 0:2 * P], ACT.Copy).then_inc(oT_ready, 1)

                def high_o(t):
                    if not s.attn:
                        return
                    act.wait_ge(o_turned, m * TILES + (t + 1))
                    nc.scalar.activation(oh[:], o_ps[:, 0:P], ACT.Copy).then_inc(o_hi, 1)

                def high_x(*rs):
                    if turns(s):
                        for r in rs:
                            ln.high(act, s.b, r, x_ps)

                set_bias()
                high_x(0)
                out_weights()
                exps(0)
                high_x(1, 2)
                exps(1)
                copy_probs(0)
                high_x(3)
                high_unit(0, kh)
                next_weights(0)
                high_x(4)
                copy_probs(1)
                copy_oT(0)
                high_x(5)
                exps(2)
                high_x(6)
                high_o(0)
                copy_probs(2)
                high_x(7)
                copy_oT(1)
                exps(3)
                next_weights(1)
                high_o(1)
                copy_oT(2)
                if s.norm:
                    act.wait_ge(u_done, n * U + 2)
                    context_high(s.b + 1, range(4))
                copy_probs(3)
                high_o(2)
                if s.norm:
                    ln.deviations(act, s.b + 1)
                    context_high(s.b + 1, range(4, KC))
                copy_oT(3)
                high_unit(2, qh)
                high_o(3)
                next_weights(2)
                if s.cross or not s.proj:
                    for t in range(TILES):
                        act.wait_ge(x_free, m * PR + (2 * t + 3))
                        act.dma_start(tile_of(x2, s.attn_b * TILES + t), acc[:, t]).then_inc(x2_stored[t], 16)

            pipeline(act, first_block, step)
            for t in range(TILES):
                act.wait_ge(x2_stored[t], 16 * BLOCKS)

        @block.vector
        def _(dve):
            dve.sem_inc(c_split, 2)
            dve.sem_inc(u_free, 2)
            dve.sem_inc(s_shifted, 1)
            dve.sem_inc(o_split, 1)
            dve.sem_inc(x_free, 1)

            def context_low(b, ks):
                for k in ks:
                    dve.wait_ge(c_hi, b * KC + (k + 1))
                    nc.vector.tensor_tensor(cl[:, k], craw[:, k % 2], f32(ch[:, k]), ALU.subtract
                                            ).then_inc(c_split, 1)

            def first_block():
                context_low(0, range(KC))
                ln.moments(dve, 0)
                ln.normalise(dve, 0)

            def step(s):
                n, m = s.n, s.m

                def low_unit(u, dst, hi, number):
                    if not s.proj:
                        return
                    dve.wait_ge(u_hi, n * 2 + number)
                    w = WHICH[u]
                    nc.vector.scalar_tensor_tensor(dst[:, s.par], u_ps[(s.par * U + u) % 2][:],
                                                   bias_now[:, s.par, w:w + 1], f32(hi[:, s.par]),
                                                   ALU.add, ALU.subtract).then_inc(u_free, 1)

                def copy_vT():
                    if not s.proj:
                        return
                    dve.wait_ge(u_done, n * U + 2)
                    nc.vector.tensor_scalar(vT[:], u_ps[(s.par * U + 1) % 2][:], bias_now[:, s.par, 2:3], None,
                                            ALU.add).then_inc(u_free, 1)

                def place_v():
                    if not s.proj:
                        return
                    dve.wait_ge(v_set, 2)
                    dve.wait_ge(v_turned, n + 1)
                    nc.vector.tensor_copy(v[:, s.par, :, 0:DK], t_ps[:, 0:BT].rearrange("p (s d) -> p s d", d=DK)
                                          ).then_inc(v_placed, 1)

                def shift(t):
                    if not s.attn:
                        return
                    sv = s_ps[:].rearrange("p (s n) -> p s n", s=SLOTS)
                    dve.wait_ge(s_done, m * TILES + (t + 3))
                    nc.vector.tensor_reduce(top[:], sv, AX.X, ALU.max).then_inc(s_top, 1)
                    dve.wait_ge(s_top, m * TILES + (t + 1))
                    nc.vector.tensor_tensor(probs[:, t % 2], sv, top[:].unsqueeze(2).broadcast_to([P, SLOTS, P]),
                                            ALU.subtract).then_inc(s_shifted, 1)

                def scale_o(t):
                    if not s.attn:
                        return
                    ov = o_ps[:, 2 * P:4 * P].rearrange("p (s w) -> p s w", w=DP)
                    dve.wait_ge(oT_turned, m * TILES + (t + 1))
                    nc.vector.reciprocal(inv[:], ov[:, :, DK]).then_inc(inv_done, 1)
                    dve.wait_ge(inv_done, m * TILES + (t + 1))
                    nc.vector.tensor_tensor(o[:].rearrange("p (s d) -> p s d", d=DK), ov[:, :, 0:DK],
                                            inv[:].unsqueeze(2).broadcast_to([P, SLOTS, DK]), ALU.mult
                                            ).then_inc(o_ready, 1)

                def low_o(t):
                    if not s.attn:
                        return
                    dve.wait_ge(o_hi, m * TILES + (t + 1))
                    nc.vector.tensor_tensor(ol[:], o_ps[:, 0:P], f32(oh[:]), ALU.subtract).then_inc(o_split, 1)

                def add_projected(t, half):
                    if not s.attn:
                        return
                    if half == 0:
                        dve.wait_ge(acc_loaded[t], s.attn_b * 16 + 16)
                    dve.wait_ge(pr_done, m * PR + (2 * t + half + 2))
                    part = acc[:, t, half * HALF:(half + 1) * HALF]
                    nc.vector.tensor_tensor(part, x_ps[:], part, ALU.add).then_inc(x_free, 1)

                def low_x(*rs):
                    if turns(s):
                        for r in rs:
                            ln.low(dve, s.b, r, x_ps)

                shift(0)
                low_x(0, 1)
                shift(1)
                low_x(2, 3)
                low_unit(0, kl, kh, 1)
                shift(2)
                low_x(4, 5)
                scale_o(0)
                shift(3)
                low_x(6)
                low_o(0)
                low_x(7)
                add_projected(0, 0)
                copy_vT()
                scale_o(1)
                add_projected(0, 1)
                low_o(1)
                place_v()
                add_projected(1, 0)
                scale_o(2)
                add_projected(1, 1)
                if s.norm:
                    ln.moments(dve, s.b + 1)
                    context_low(s.b + 1, range(4))
                low_o(2)
                if s.norm:
                    ln.normalise(dve, s.b + 1)
                    context_low(s.b + 1, range(4, KC))
                add_projected(2, 0)
                scale_o(3)
                low_unit(2, ql, qh, 2)
                add_projected(2, 1)
                low_o(3)
                add_projected(3, 0)
                add_projected(3, 1)

            pipeline(dve, first_block, step)



def ffn_phase(nc, sems, ident, eps, x2, bo, vh, uT, s_all, alpha, beta, u_rT, vh_r, s_r, d_r, r_mat, bias,
              out):
    with ExitStack() as ctx:
        def sb(name, shape, dt=F32):
            return ctx.enter_context(nc.sbuf_tensor(name, shape, dt))

        def sem(name):
            return sems.enter_context(nc.semaphore(name))

        bo_sb = sb("ff_bo", [P, D])
        ln = NormBuffers(nc, ctx, sems, "ff_ln", eps, offset=bo_sb)
        acc = sb("ff_acc", [P, TILES, D])
        vh_sb = sb("ff_vh", [P, KC, D])
        uT_sb = sb("ff_uT", [P, KC, D])
        s_sb = sb("ff_s", [P, KC])
        ab = sb("ff_ab", [R_TOP, 2])
        small = sb("ff_small", [R_INT, 2])
        urT_sb = sb("ff_urT", [R_INT, D])
        vhr_sb = sb("ff_vhr", [R_INT, D])
        r_sb = sb("ff_r", [R_INT, R_INT])
        delta = sb("ff_delta", [R_INT, D])
        bias_sb = sb("ff_bias", [P, D])
        weh = sb("ff_weh", [P, KC, D], F32R)
        wel = sb("ff_wel", [P, KC, D], F32R)
        banks = [ctx.enter_context(nc.psum_tensor(f"ff_ps{i}", [P, HALF], F32)) for i in range(8)]
        turn_ps, y_ps = banks[0:4], banks[4:8]

        small_loaded = sem("ff_small_loaded")
        biases_loaded = sem("ff_biases_loaded")
        factors_loaded = [sem(f"ff_factors_loaded{k}") for k in range(KC)]
        acc_loaded = [sem(f"ff_acc_loaded{t}") for t in range(TILES)]
        s_steps = sem("ff_s_steps")
        u_scaled = sem("ff_u_scaled")
        delta_mm = sem("ff_delta_mm")
        delta_ready = sem("ff_delta_ready")
        we_done = sem("ff_we_done")
        we_hi = sem("ff_we_hi")
        we_split = sem("ff_we_split")
        biases_summed = sem("ff_biases_summed")
        acc_ready = sem("ff_acc_ready")
        y_done = sem("ff_y_done")
        y_free = sem("ff_y_free")
        stored = [sem(f"ff_stored{t}") for t in range(TILES)]
        NWE = 2 * KC
        YB = 2 * TILES

        block = ctx.enter_context(nc.Block())

        @block.sync
        def _(sp):
            sp.dma_start(s_sb[:], s_all).then_inc(small_loaded, 16)
            sp.dma_start(ab[:, 0:1], alpha).then_inc(small_loaded, 16)
            sp.dma_start(ab[:, 1:2], beta).then_inc(small_loaded, 16)
            sp.dma_start(small[:, 0:1], s_r).then_inc(small_loaded, 16)
            sp.dma_start(small[:, 1:2], d_r).then_inc(small_loaded, 16)
            sp.dma_start(urT_sb[:], u_rT).then_inc(small_loaded, 16)
            sp.dma_start(vhr_sb[:], vh_r).then_inc(small_loaded, 16)
            sp.dma_start(r_sb[:], r_mat).then_inc(small_loaded, 16)
            for k in range(KC):
                sp.dma_start(uT_sb[:, k], uT[k]).then_inc(factors_loaded[k], 16)
                sp.dma_start(vh_sb[:, k], vh[k]).then_inc(factors_loaded[k], 16)
            sp.dma_start(bo_sb[:], bo).then_inc(biases_loaded, 16)
            sp.dma_start(bias_sb[:], bias).then_inc(biases_loaded, 16)
            for t in range(TILES):
                sp.dma_start(ln.x[:, t], x2[t]).then_inc(ln.loaded[t], 16)

            def load_acc(b, t):
                sp.wait_ge(stored[t], b * 16 + 16)
                sp.dma_start(acc[:, t], tile_of(x2, b * TILES + t)).then_inc(acc_loaded[t], 16)

            def load_next_x(b, t):
                sp.wait_ge(ln.turned, b * ln.GROUPS + (2 * t + 2))
                sp.dma_start(ln.x[:, t], tile_of(x2, b * TILES + (TILES + t))).then_inc(ln.loaded[t], 16)

            with sp.Fori(0, BLOCKS - 1) as b:
                load_acc(b, 0)
                load_acc(b, 1)
                load_next_x(b, 0)
                load_next_x(b, 1)
                load_acc(b, 2)
                load_next_x(b, 2)
                load_next_x(b, 3)
                load_acc(b, 3)
            for t in range(TILES):
                load_acc(BLOCKS - 1, t)

        @block.tensor
        def _(pe):
            pe.wait_ge(s_steps, 5)
            for half in range(2):
                ins = nc.tensor.matmul(banks[half][0:R_INT, :], r_sb[:], urT_sb[:, half * HALF:(half + 1) * HALF],
                                       start=True, stop=True)
            ins.then_inc(delta_mm, 1)
            pe.wait_ge(delta_ready, 1)
            for first in range(0, NWE, 8):
                for k in range(KC + 1):
                    if first == 0 and k < KC:
                        pe.wait_ge(u_scaled, k + 1)
                    for w in range(first, first + 8):
                        ic, half = w // 2, w % 2
                        cols = slice(half * HALF, (half + 1) * HALF)
                        if k == 0 and first:
                            pe.wait_ge(we_split, w - 7)
                        if k < KC:
                            nc.tensor.matmul(banks[w % 8][:], vh_sb[:, k, ic * P:(ic + 1) * P],
                                             uT_sb[:, k, cols], start=(k == 0), stop=False)
                        else:
                            nc.tensor.matmul(banks[w % 8][:], vhr_sb[:, ic * P:(ic + 1) * P], delta[:, cols],
                                             start=False, stop=True).then_inc(we_done, 1)

            def turn(b, *rs):
                for r in rs:
                    if r >= 4:
                        pe.wait_ge(ln.lo_done, b * ln.GROUPS + (r - 3))
                    ln.turn(pe, b, r, ident, turn_ps[r % 4])

            def project(b, t):
                pe.wait_ge(ln.lo_done, b * ln.GROUPS + (2 * t + 2))
                for half in range(2):
                    use = 2 * t + half
                    pe.wait_ge(y_free, b * YB + (use + 1))
                    cols = slice(half * HALF, (half + 1) * HALF)
                    three_passes(nc, y_ps[use % 4][:],
                                 [(ln.xh[:, k, t * P:(t + 1) * P], ln.xl[:, k, t * P:(t + 1) * P],
                                   weh[:, k, cols], wel[:, k, cols]) for k in range(KC)]).then_inc(y_done, 1)

            pe.wait_ge(we_split, NWE - 4)
            turn(0, *range(8))
            pe.wait_ge(we_split, NWE)
            with pe.Fori(0, BLOCKS - 1) as b:
                project(b, 0)
                project(b, 1)
                pe.wait_ge(ln.lo_done, b * ln.GROUPS + ln.GROUPS)
                turn(b + 1, 0, 1)
                project(b, 2)
                turn(b + 1, 2, 3)
                project(b, 3)
                turn(b + 1, 4, 5, 6, 7)
            for t in range(TILES):
                project(BLOCKS - 1, t)

        @block.scalar
        def _(act):
            for t in range(TILES):
                act.sem_inc(stored[t], 16)

            def high_we(w):
                act.wait_ge(we_done, w + 1)
                nc.scalar.activation(weh[:, w // 2, (w % 2) * HALF:(w % 2 + 1) * HALF], banks[w % 8][:],
                                     ACT.Copy).then_inc(we_hi, 1)

            def high(b, *rs):
                for r in rs:
                    ln.high(act, b, r, turn_ps[r % 4])

            def store(b, *ts):
                for t in ts:
                    act.wait_ge(y_free, b * YB + (2 * t + 2 + 4))
                    act.dma_start(tile_of(out, b * TILES + t), acc[:, t]).then_inc(stored[t], 16)

            for w in range(8):
                high_we(w)
            ln.deviations(act, 0)
            for w in range(8, NWE):
                high_we(w)
            high(0, *range(8))
            with act.Fori(0, BLOCKS - 1) as b:
                ln.deviations(act, b + 1)
                high(b + 1, 0, 1)
                store(b, 0, 1)
                high(b + 1, 2, 3)
                store(b, 2)
                high(b + 1, 4, 5, 6, 7)
                store(b, 3)
            store(BLOCKS - 1, *range(TILES))
            for t in range(TILES):
                act.wait_ge(stored[t], 16 + 16 * BLOCKS)

        @block.vector
        def _(dve):
            dve.sem_inc(y_free, 4)
            dve.wait_ge(small_loaded, 8 * 16)
            top = s_sb[0:R_TOP, 0:1]
            nc.vector.tensor_scalar(top, top, ab[:, 0:1], ab[:, 1:2], ALU.mult, ALU.add).then_inc(s_steps, 1)
            dve.wait_ge(s_steps, 1)
            nc.vector.tensor_scalar(top, top, 0.0, None, ALU.max).then_inc(s_steps, 1)
            nc.vector.tensor_scalar(small[:, 1:2], small[:, 1:2], 0.0, None, ALU.max).then_inc(s_steps, 1)
            dve.wait_ge(s_steps, 3)
            nc.vector.tensor_scalar(urT_sb[:], urT_sb[:], small[:, 0:1], None, ALU.mult).then_inc(s_steps, 1)
            dve.wait_ge(s_steps, 4)
            nc.vector.tensor_scalar(urT_sb[:], urT_sb[:], small[:, 1:2], None, ALU.mult).then_inc(s_steps, 1)
            dve.wait_ge(delta_mm, 1)
            for half in range(2):
                ins = nc.vector.tensor_copy(delta[:, half * HALF:(half + 1) * HALF], banks[half][0:R_INT, :])
            ins.then_inc(delta_ready, 1)
            for k in range(KC):
                dve.wait_ge(factors_loaded[k], 32)
                nc.vector.tensor_scalar(uT_sb[:, k], uT_sb[:, k], s_sb[:, k:k + 1], None, ALU.mult
                                        ).then_inc(u_scaled, 1)

            def low_we(w):
                dve.wait_ge(we_hi, w + 1)
                part = (slice(None), w // 2, slice((w % 2) * HALF, (w % 2 + 1) * HALF))
                nc.vector.tensor_tensor(wel[part], banks[w % 8][:], f32(weh[part]), ALU.subtract
                                        ).then_inc(we_split, 1)

            def low(b, *rs):
                for r in rs:
                    ln.low(dve, b, r, turn_ps[r % 4])

            def add_biases(b, *ts):
                for t in ts:
                    dve.wait_ge(acc_loaded[t], b * 16 + 16)
                    nc.vector.tensor_tensor(acc[:, t], acc[:, t], bias_sb[:], ALU.add).then_inc(acc_ready, 1)

            def add_products(b, *ts):
                for t in ts:
                    dve.wait_ge(acc_ready, b * TILES + (t + 1))
                    for half in range(2):
                        use = 2 * t + half
                        dve.wait_ge(y_done, b * YB + (use + 1))
                        part = acc[:, t, half * HALF:(half + 1) * HALF]
                        nc.vector.tensor_tensor(part, y_ps[use % 4][:], part, ALU.add).then_inc(y_free, 1)

            dve.wait_ge(biases_loaded, 32)
            nc.vector.tensor_tensor(bias_sb[:], bias_sb[:], bo_sb[:], ALU.add).then_inc(biases_summed, 1)
            for w in range(8):
                low_we(w)
            ln.moments(dve, 0)
            ln.normalise(dve, 0)
            for w in range(8, NWE):
                low_we(w)
            low(0, *range(8))
            dve.wait_ge(biases_summed, 1)
            nc.vector.memset(ln.idle[:], 0.0)
            with dve.Fori(0, BLOCKS - 1) as b:
                add_biases(b, 0, 1)
                ln.moments(dve, b + 1)
                ln.normalise(dve, b + 1)
                add_products(b, 0, 1)
                low(b + 1, 0, 1)
                add_biases(b, 2, 3)
                add_products(b, 2)
                low(b + 1, 2, 3)
                add_products(b, 3)
                low(b + 1, 4, 5, 6, 7)
            add_biases(BLOCKS - 1, *range(TILES))
            add_products(BLOCKS - 1, *range(TILES))


def decoder_layer(nc, a, out):
    x1 = nc.dram_tensor("x1", (TOKENS // P, P, D), F32, kind="Internal").ap()
    x2 = nc.dram_tensor("x2", (TOKENS // P, P, D), F32, kind="Internal").ap()
    w_folded = nc.dram_tensor("w_folded", (3 * CH, P, D), F32, kind="Internal").ap()
    with ExitStack() as sems, ExitStack() as ctx:
        def sb(name, shape, stack=ctx):
            return stack.enter_context(nc.sbuf_tensor(name, shape, F32))

        ident = sb("ident", [P, P])
        slotmask = sb("slotmask", [P, SLOTS])
        bias_qkv = sb("bias_qkv", [P, CH, 3])
        eps = sb("eps", [P, 1])
        with ExitStack() as first_phases:
            causal = sb("causal", [P, P], first_phases)
            mix = sb("mix", [P, CH, P], first_phases)
            constants_phase(nc, sems, ident, causal, slotmask, mix, bias_qkv, eps, a["b_nat"],
                            a["inter_rows"], a["amp_col"])
            self_attention_phase(nc, sems, ident, causal, mix, eps, a["x_rows"], a["wqkv"], a["wproj"],
                                 a["w_nat"], w_folded, x1)
        cross_attention_phase(nc, sems, ident, slotmask, bias_qkv, eps, x1, a["ctxT"], w_folded, a["wo"], x2)
        ffn_phase(nc, sems, ident, eps, x2, a["bo"], a["vh"], a["uT"], a["s_all"], a["alpha"], a["beta"],
                  a["u_rT"], a["vh_r"], a["s_r"], a["d_r"], a["r_mat"], a["ffn_bias"], out)


def layouts(i):
    c = np.ascontiguousarray
    g = {}
    g["x_rows"] = c(np.transpose(i["x"], (1, 0, 2))).reshape(TOKENS // P, P, D)
    w = i["L0_attn_weight_qkv"].reshape(KVH, QPG + 2, HD, KC, P)[:, [QPG, QPG + 1] + list(range(QPG))]
    g["wqkv"] = c(np.transpose(w, (0, 1, 4, 3, 2))).reshape(KVH * (QPG + 2), P, D)
    g["wproj"] = c(i["L0_attn_weight_proj"].T).reshape(KVH * QPG, P, D)
    g["w_nat"] = c(np.concatenate([i["L0_xattn_W" + n] for n in "qkv"])).reshape(3 * CH, P, D)
    g["b_nat"] = c(np.stack([i["L0_xattn_b" + n].reshape(CH, P) for n in "qkv"], 2).transpose(1, 0, 2))
    inter = np.repeat(i["L0_xattn_interference"][:, None], DK, axis=1).reshape(CH, P, MS)
    g["inter_rows"] = c(np.transpose(inter, (1, 0, 2)))
    g["amp_col"] = c(np.broadcast_to(i["L0_xattn_amp"].reshape(1, 1), (P, 1)))
    ctx = np.transpose(i["ctx_4096"].reshape(BLOCKS, BT, KC, P), (0, 2, 3, 1))
    g["ctxT"] = c(ctx).reshape(BLOCKS * KC, P, BT)
    wo = i["L0_xattn_Wo"].T.reshape(CH, 2, DK, MS, D)
    g["wo"] = c(np.transpose(wo, (0, 1, 3, 2, 4))).reshape(CH, P, D)
    g["bo"] = c(np.broadcast_to(i["L0_xattn_bo"][None], (P, D)))
    g["vh"] = c(np.concatenate([i["L0_ffn_Vh_top"], i["L0_ffn_Vh_tail"]])).reshape(KC, P, D)
    g["uT"] = c(np.concatenate([i["L0_ffn_U_top"].T, i["L0_ffn_U_tail"].T])).reshape(KC, P, D)
    g["s_all"] = c(np.concatenate([i["L0_ffn_S_top"], i["L0_ffn_S_tail"]]).reshape(KC, P).T)
    g["alpha"] = c(i["L0_ffn_alpha"].reshape(R_TOP, 1))
    g["beta"] = c(i["L0_ffn_beta"].reshape(R_TOP, 1))
    g["u_rT"] = c(i["L0_ffn_U_tail_r"].T)
    g["vh_r"] = c(i["L0_ffn_Vh_tail_r"])
    g["s_r"] = c(i["L0_ffn_S_tail_r"].reshape(R_INT, 1))
    g["d_r"] = c(i["L0_ffn_D"].reshape(R_INT, 1))
    g["r_mat"] = c(i["L0_ffn_R"])
    g["ffn_bias"] = c(np.broadcast_to(i["L0_ffn_bias"][None], (P, D)))
    return g


def kernel(**inputs):
    import concourse.bacc as bacc
    from concourse.bass_utils import run_bass_kernel_spmd

    given = layouts({name: np.asarray(a) for name, a in inputs.items()})
    nc = bacc.Bacc("TRN2", target_bir_lowering=False, num_devices=1, dynamic_dma_scratch_size=1024)
    aps = {name: nc.dram_tensor(f"in_{name}", a.shape, F32, kind="ExternalInput").ap()
           for name, a in given.items()}
    out = nc.dram_tensor("out_x", (TOKENS // P, P, D), F32, kind="ExternalOutput").ap()
    decoder_layer(nc, aps, out)
    r = run_bass_kernel_spmd(nc, [{f"in_{name}": a for name, a in given.items()}], core_ids=[0])
    return r.results[0]["out_x"].reshape(SEQ, TOKENS // SEQ, D)
```

```python
import numpy as np
import concourse.bass as bass
from concourse import mybir
from contextlib import ExitStack

F32 = mybir.dt.float32
F32R = mybir.dt.float32r
ALU = mybir.AluOpType
ACT = mybir.ActivationFunctionType
AX = mybir.AxisListType

P = 128
D = 1024
KC = D // P
HALF = 512
TOKENS = 2048
TILES = 4
BT = TILES * P
BLOCKS = TOKENS // BT
EPS = 1e-5
MASKED = -1e30

SEQ = 16
KVH = 8
QPG = 4
HD = 128
SELF_SCALE = 1.0 / HD ** 0.5

CH = D // P
SLOTS = 8
DK = 16
MS = 4
CROSS_SCALE = 1.0 / DK ** 0.5

R_TOP = 64
R_INT = 4


def f32(ap):
    return ap.bitcast(F32)


def three_passes(nc, out, parts, first=True, last=True):
    for i, (ah, al, bh, bl) in enumerate(parts):
        nc.tensor.matmul(out, ah, bh, start=(first and i == 0), stop=False)
        nc.tensor.matmul(out, ah, bl, start=False, stop=False)
        ins = nc.tensor.matmul(out, al, bh, start=False, stop=(last and i == len(parts) - 1))
    return ins


def tile_of(array, index):
    return array[bass.ds(index, 1)].rearrange("a p n -> (a p) n")



def constants_phase(nc, sems, ident, causal, pairmask, mix, bias_qkv, eps, b_nat, inter_rows, amp_col):
    with ExitStack() as ctx:
        def sb(name, shape, dt=F32):
            return ctx.enter_context(nc.sbuf_tensor(name, shape, dt))

        def sem(name):
            return sems.enter_context(nc.semaphore(name))

        inter = sb("inter", [P, CH, MS])
        amp = sb("amp", [P, 1])
        amp01 = sb("amp01", [P, 1])
        same_hd = sb("same_hd", [P, 2 * DK])
        same_m = sb("same_m", [P, MS])
        mix_rows = sb("mix_rows", [P, CH, MS])
        bias_raw = sb("bias_raw", [P, CH, 3])
        slotmask = sb("slotmask", [P, SLOTS])
        bias_ps = ctx.enter_context(nc.psum_tensor("bias_ps", [P, HALF], F32))

        small_loaded = sem("set_small_loaded")
        masks_built = sem("set_masks_built")
        mix_steps = sem("set_mix_steps")
        bias_mixed = sem("set_bias_mixed")

        block = ctx.enter_context(nc.Block())

        @block.sync
        def _(sp):
            sp.dma_start(inter[:], inter_rows).then_inc(small_loaded, 16)
            sp.dma_start(amp[:], amp_col).then_inc(small_loaded, 16)
            sp.dma_start(bias_raw[:], b_nat).then_inc(small_loaded, 16)

        @block.gpsimd
        def _(pool):
            pool.memset(ident[:], 0.0).then_inc(masks_built, 1)
            pool.memset(causal[:], 0.0).then_inc(masks_built, 1)
            pool.memset(same_hd[:], 1.0).then_inc(masks_built, 1)
            pool.memset(slotmask[:], 1.0).then_inc(masks_built, 1)
            pool.wait_ge(masks_built, 4)
            pool.affine_select(out=ident[:], in_=ident[:], compare_op=ALU.not_equal, fill=1.0, base=0,
                               pattern=[[-1, P]], channel_multiplier=1).then_inc(masks_built, 1)
            pool.affine_select(out=causal[:], in_=causal[:], compare_op=ALU.is_ge, fill=MASKED, base=0,
                               pattern=[[-1, P]], channel_multiplier=1).then_inc(masks_built, 1)
            pool.affine_select(out=same_hd[:], in_=same_hd[:], compare_op=ALU.is_ge, fill=0.0, base=0,
                               pattern=[[-MS, 2 * DK]], channel_multiplier=1).then_inc(masks_built, 1)
            pool.affine_select(out=slotmask[:], in_=slotmask[:], compare_op=ALU.is_ge, fill=0.0, base=0,
                               pattern=[[-DK, SLOTS]], channel_multiplier=1).then_inc(masks_built, 1)
            pool.wait_ge(masks_built, 8)
            cv = causal[:].rearrange("p (j i) -> p j i", i=SEQ)
            pool.affine_select(out=cv, in_=cv, compare_op=ALU.is_ge, fill=MASKED, base=SEQ - 1,
                               pattern=[[SEQ, P // SEQ], [0, SEQ]], channel_multiplier=-1).then_inc(masks_built, 1)
            pool.affine_select(out=same_hd[:], in_=same_hd[:], compare_op=ALU.is_ge, fill=0.0, base=MS - 1,
                               pattern=[[MS, 2 * DK]], channel_multiplier=-1).then_inc(masks_built, 1)
            pool.affine_select(out=slotmask[:], in_=slotmask[:], compare_op=ALU.is_ge, fill=0.0, base=DK - 1,
                               pattern=[[DK, SLOTS]], channel_multiplier=-1).then_inc(masks_built, 1)

        @block.vector
        def _(dve):
            nc.vector.memset(eps[:], EPS).then_inc(mix_steps, 1)
            dve.wait_ge(masks_built, 11)
            nc.vector.tensor_reduce(same_m[:], ident[:].rearrange("p (k j) -> p j k", j=MS), AX.X,
                                    ALU.add).then_inc(mix_steps, 1)
            nc.vector.tensor_reduce(pairmask[:], slotmask[:].rearrange("p (r w) -> p w r", w=2), AX.X,
                                    ALU.add).then_inc(mix_steps, 1)
            dve.wait_ge(small_loaded, 48)
            nc.vector.tensor_scalar(amp01[:], amp[:], 0.1, None, ALU.mult).then_inc(mix_steps, 1)
            dve.wait_ge(mix_steps, 4)
            for c in range(CH):
                ins = nc.vector.scalar_tensor_tensor(mix_rows[:, c], inter[:, c], amp01[:], same_m[:],
                                                     ALU.mult, ALU.add)
            ins.then_inc(mix_steps, 1)
            dve.wait_ge(mix_steps, 5)
            hd = same_hd[:].rearrange("p (h d) -> p h d", h=2)
            mv = mix[:].rearrange("p c (h j d) -> p c h j d", h=2, j=MS)
            for c in range(CH):
                for h in range(2):
                    ins = nc.vector.tensor_tensor(
                        mv[:, c, h], hd[:, h].unsqueeze(1).broadcast_to([P, MS, DK]),
                        mix_rows[:, c].unsqueeze(2).broadcast_to([P, MS, DK]), ALU.mult)
            ins.then_inc(mix_steps, 1)
            dve.wait_ge(bias_mixed, 1)
            nc.vector.tensor_copy(bias_qkv[:].rearrange("p c w -> p (c w)"),
                                  bias_ps[:, 0:CH * 3])

        @block.tensor
        def _(pe):
            pe.wait_ge(mix_steps, 6)
            pe.wait_ge(small_loaded, 48)
            for c in range(CH):
                ins = nc.tensor.matmul(bias_ps[:, c * 3:c * 3 + 3], mix[:, c], bias_raw[:, c],
                                       start=True, stop=True)
            ins.then_inc(bias_mixed, 1)



class NormBuffers:
    GROUPS = 2 * TILES

    def __init__(self, nc, ctx, sems, tag, eps, offset=None):
        self.nc, self.eps, self.offset = nc, eps, offset

        def sb(name, shape, dt=F32):
            return ctx.enter_context(nc.sbuf_tensor(f"{tag}_{name}", shape, dt))

        def sem(name):
            return sems.enter_context(nc.semaphore(f"{tag}_{name}"))

        self.x = sb("x", [P, TILES, D])
        self.stats = sb("stats", [P, TILES, 12])
        self.mv = sb("mv", [P, TILES, 2])
        self.std = sb("std", [P, TILES])
        self.idle = sb("idle", [P, 1])
        self.rstd = sb("rstd", [P, TILES])
        self.xh = sb("xh", [P, KC, BT], F32R)
        self.xl = sb("xl", [P, KC, BT], F32R)
        self.loaded = [sem(f"x_loaded{t}") for t in range(TILES)]
        self.offset_added = sem("offset_added") if offset is not None else None
        self.stats_done = sem("stats_done")
        self.moments_done = sem("moments_done")
        self.std_done = sem("std_done")
        self.rstd_done = sem("rstd_done")
        self.normal = sem("normal")
        self.turned = sem("turned")
        self.hi_done = sem("hi_done")
        self.lo_done = sem("lo_done")

    def moments(self, dve, b, tiles=range(TILES)):
        nc = self.nc
        for t in tiles:
            dve.wait_ge(self.loaded[t], b * 16 + 16)
            if self.offset is not None:
                nc.vector.tensor_tensor(self.x[:, t], self.x[:, t], self.offset[:], ALU.add
                                        ).then_inc(self.offset_added, 1)
                dve.wait_ge(self.offset_added, b * TILES + (t + 1))
            nc.vector.bn_stats(self.stats[:, t, 0:6], self.x[:, t, 0:HALF])
            nc.vector.bn_stats(self.stats[:, t, 6:12], self.x[:, t, HALF:D]).then_inc(self.stats_done, 1)
            dve.wait_ge(self.stats_done, b * TILES + (t + 1))
            nc.vector.memset(self.idle[:], 0.0)
            nc.vector.bn_aggr(self.mv[:, t], self.stats[:, t]).then_inc(self.moments_done, 1)

    def deviations(self, act, b):
        act.wait_ge(self.moments_done, b * TILES + TILES)
        self.nc.scalar.activation(self.std[:], self.mv[:, :, 1], ACT.Sqrt, bias=self.eps[:]
                                  ).then_inc(self.std_done, 1)

    def normalise(self, dve, b):
        nc = self.nc
        dve.wait_ge(self.std_done, b + 1)
        nc.vector.reciprocal(self.rstd[:], self.std[:]).then_inc(self.rstd_done, 1)
        dve.wait_ge(self.rstd_done, b + 1)
        for t in range(TILES):
            nc.vector.tensor_scalar(self.x[:, t], self.x[:, t], self.mv[:, t, 0:1], self.rstd[:, t:t + 1],
                                    ALU.subtract, ALU.mult).then_inc(self.normal, 1)

    def turn(self, pe, b, r, ident, bank):
        t, half = r // 2, r % 2
        pe.wait_ge(self.normal, b * TILES + (t + 1))
        for k in range(4):
            ins = self.nc.tensor.transpose(bank[:, k * P:(k + 1) * P],
                                           self.x[:, t, (4 * half + k) * P:(4 * half + k + 1) * P], ident[:])
        ins.then_inc(self.turned, 1)

    def part(self, a, r):
        t, half = r // 2, r % 2
        return a[:, 4 * half:4 * half + 4, t * P:(t + 1) * P]

    def high(self, act, b, r, bank):
        act.wait_ge(self.turned, b * self.GROUPS + (r + 1))
        self.nc.scalar.activation(self.part(self.xh, r), bank[:].rearrange("p (k n) -> p k n", k=4), ACT.Copy
                                  ).then_inc(self.hi_done, 1)

    def low(self, dve, b, r, bank):
        dve.wait_ge(self.hi_done, b * self.GROUPS + (r + 1))
        self.nc.vector.tensor_tensor(self.part(self.xl, r), bank[:].rearrange("p (k n) -> p k n", k=4),
                                     f32(self.part(self.xh, r)), ALU.subtract).then_inc(self.lo_done, 1)


class Step:

    def __init__(self, b, g, par, proj=True, attn=True, nxt=True, next_g=None, cross=False, norm=False,
                 steady=True):
        self.b, self.g, self.par = b, g, par
        self.n = b * 8 + g
        self.m = self.n + (-1)
        self.proj, self.attn = proj, attn
        self.nxt = nxt
        self.next_g = g + 1 if next_g is None else next_g
        self.cross = cross
        self.norm = norm
        self.steady = steady
        self.attn_g = 7 if cross else g + (-1)
        self.attn_b = b + (-1) if cross else b


def pipeline(eng, first_block, step):
    def inner(b, steady):
        with eng.Fori(0, 3) as i:
            step(Step(b, i * 2 + 1, 1, steady=steady))
            step(Step(b, i * 2 + 2, 0, steady=steady))

    first_block()
    step(Step(0, 0, 0, attn=False, steady=False))
    with eng.Fori(0, BLOCKS - 1) as b:
        inner(b, True)
        step(Step(b, 7, 1, next_g=0, norm=True))
        step(Step(b + 1, 0, 0, cross=True))
    b = BLOCKS - 1
    inner(b, False)
    step(Step(b, 7, 1, nxt=False, steady=False))
    step(Step(b, 8, 0, proj=False, nxt=False, steady=False))



def self_attention_phase(nc, sems, ident, causal, mix, eps, x_rows, wqkv, wproj, w_nat, w_folded, x1):
    U = 2 + QPG
    PR = TILES * 2
    with ExitStack() as ctx:
        def sb(name, shape, dt=F32):
            return ctx.enter_context(nc.sbuf_tensor(name, shape, dt))

        def bank(name):
            return ctx.enter_context(nc.psum_tensor(name, [P, HALF], F32))

        def sem(name):
            return sems.enter_context(nc.semaphore(name))

        ln = NormBuffers(nc, ctx, sems, "sa_ln", eps)
        acc = sb("sa_acc", [P, TILES, D])
        wraw = sb("sa_wraw", [P, 3, D])
        wh = sb("sa_wh", [P, 3, D], F32R)
        wl = sb("sa_wl", [P, 3, D], F32R)
        praw = sb("sa_praw", [P, QPG, D])
        ph = sb("sa_ph", [P, QPG, D], F32R)
        pl = sb("sa_pl", [P, QPG, D], F32R)
        kT = sb("sa_kT", [P, 2, BT])
        qT = sb("sa_qT", [P, 2, QPG, BT])
        vT = sb("sa_vT", [P, BT])
        vh = sb("sa_vh", [P, 2, TILES, HD], F32R)
        vl = sb("sa_vl", [P, 2, TILES, HD], F32R)
        probs = sb("sa_probs", [P, QPG, P])
        probsTh = sb("sa_probsTh", [P, QPG * P], F32R)
        probsTl = sb("sa_probsTl", [P, QPG * P], F32R)
        top = sb("sa_top", [P, QPG])
        total = sb("sa_total", [P, QPG])
        inv = sb("sa_inv", [P, QPG])
        oh = sb("sa_oh", [P, QPG * P], F32R)
        ol = sb("sa_ol", [P, QPG * P], F32R)
        nat = sb("sa_nat", [P, D])
        fold = sb("sa_fold", [P, D])

        u_ps = [bank(f"sa_u{i}") for i in range(2)]
        pr_ps = [bank(f"sa_pr{i}") for i in range(2)]
        s_ps, t_ps, o_ps, v_ps = bank("sa_s"), bank("sa_t"), bank("sa_o"), bank("sa_vt")
        turn_ps = [s_ps, t_ps, o_ps, v_ps]

        wraw_loaded = [sem(f"sa_wraw_loaded{i}") for i in range(3)]
        praw_loaded = [sem(f"sa_praw_loaded{i}") for i in range(QPG)]
        acc_loaded = [sem(f"sa_acc_loaded{t}") for t in range(TILES)]
        x1_stored = [sem(f"sa_x1_stored{t}") for t in range(TILES)]
        w_hi = sem("sa_w_hi")
        w_split = sem("sa_w_split")
        p_hi = sem("sa_p_hi")
        p_split = sem("sa_p_split")
        u_done = sem("sa_u_done")
        u_copied = sem("sa_u_copied")
        v_turned = sem("sa_v_turned")
        v_hi = sem("sa_v_hi")
        v_copied = sem("sa_v_copied")
        s_done = sem("sa_s_done")
        s_masked = sem("sa_s_masked")
        s_top = sem("sa_s_top")
        s_shifted = sem("sa_s_shifted")
        exp_done = sem("sa_exp_done")
        total_done = sem("sa_total_done")
        inv_done = sem("sa_inv_done")
        probs_ready = sem("sa_probs_ready")
        probs_turned = sem("sa_probs_turned")
        probsT_hi = sem("sa_probsT_hi")
        probsT_ready = sem("sa_probsT_ready")
        o_done = sem("sa_o_done")
        o_hi = sem("sa_o_hi")
        o_split = sem("sa_o_split")
        pr_done = sem("sa_pr_done")
        pr_free = sem("sa_pr_free")
        nat_loaded = sem("sa_nat_loaded")
        folded = sem("sa_folded")
        fold_stored = sem("sa_fold_stored")

        def v_uses(s):
            if not s.attn:
                return 0
            return s.n * 3 + (-2) if s.steady else s.n + 2 * 8 * (BLOCKS - 1)

        block = ctx.enter_context(nc.Block())

        @block.sync
        def _(sp):
            def weights(g, n, u):
                sp.wait_ge(w_split, n * U + (u + 1))
                sp.dma_start(wraw[:, u % 3], tile_of(wqkv, g * U + u)).then_inc(wraw_loaded[u % 3], 16)

            def load_x(b):
                for t in range(TILES):
                    sp.dma_start(ln.x[:, t], tile_of(x_rows, b * TILES + t)).then_inc(ln.loaded[t], 16)

            def load_acc(b):
                for t in range(TILES):
                    sp.dma_start(acc[:, t], tile_of(x_rows, b * TILES + t)).then_inc(acc_loaded[t], 16)

            def first_block():
                load_x(0)
                for u in range(U):
                    weights(0, 0, u)

            def step(s):
                if s.steady:
                    sp.wait_ge(folded, s.m * 2 + 2)
                    sp.dma_start(nat[:], tile_of(w_nat, s.m)).then_inc(nat_loaded, 16)
                if s.proj:
                    for h in range(QPG):
                        sp.wait_ge(p_split, s.n * QPG + (h + 1))
                        sp.dma_start(praw[:, h], tile_of(wproj, s.g * QPG + h)).then_inc(praw_loaded[h], 16)
                if s.norm:
                    sp.wait_ge(ln.turned, s.b * ln.GROUPS + ln.GROUPS)
                    load_x(s.b + 1)
                if s.nxt:
                    for u in range(U):
                        weights(s.next_g, s.n + 1, u)
                if s.proj and not s.attn:
                    load_acc(0)
                if s.cross or not s.proj:
                    for t in range(TILES):
                        sp.wait_ge(pr_free, s.m * PR + (2 * t + 4))
                        sp.dma_start(tile_of(x1, s.attn_b * TILES + t), acc[:, t]).then_inc(x1_stored[t], 16)
                if s.cross:
                    for t in range(TILES):
                        sp.wait_ge(x1_stored[t], s.b * 16)
                        sp.dma_start(acc[:, t], tile_of(x_rows, s.b * TILES + t)).then_inc(acc_loaded[t], 16)

            pipeline(sp, first_block, step)
            for t in range(TILES):
                sp.wait_ge(x1_stored[t], 16 * BLOCKS)

        @block.gpsimd
        def _(pool):
            pool.sem_inc(w_split, 3)
            pool.sem_inc(p_split, QPG)

            def weights(n, u):
                pool.wait_ge(w_hi, n * U + (u + 1))
                nc.gpsimd.tensor_tensor(wl[:, u % 3], wraw[:, u % 3], f32(wh[:, u % 3]), ALU.subtract
                                        ).then_inc(w_split, 1)

            def first_block():
                for u in range(3):
                    weights(0, u)

            def step(s):
                if s.attn:
                    for h in range(QPG):
                        pool.wait_ge(p_hi, s.m * QPG + (h + 1))
                        nc.gpsimd.tensor_tensor(pl[:, h], praw[:, h], f32(ph[:, h]), ALU.subtract
                                                ).then_inc(p_split, 1)
                if s.proj:
                    for u in range(3, U):
                        weights(s.n, u)
                if s.nxt:
                    for u in range(3):
                        weights(s.n + 1, u)

            pipeline(pool, first_block, step)

        @block.tensor
        def _(pe):
            pe.sem_inc(pr_done, 1)
            pe.sem_inc(folded, 2)

            def turn_groups(b, rs):
                for r in rs:
                    if r >= 4:
                        pe.wait_ge(ln.lo_done, b * ln.GROUPS + (r - 3))
                    ln.turn(pe, b, r, ident, turn_ps[r % 4])

            def first_block():
                turn_groups(0, range(8))

            def step(s):
                n, m, mp = s.n, s.m, 1 - s.par
                v0 = v_uses(s)

                def unit(u):
                    if not s.proj:
                        return
                    if u == 0:
                        pe.wait_ge(ln.lo_done, s.b * ln.GROUPS + ln.GROUPS)
                    pe.wait_ge(w_split, n * U + (u + 4))
                    pe.wait_ge(u_copied, n * U + (u + 1))
                    three_passes(nc, u_ps[u % 2][:],
                                 [(wh[:, u % 3, k * P:(k + 1) * P], wl[:, u % 3, k * P:(k + 1) * P],
                                   ln.xh[:, k], ln.xl[:, k]) for k in range(KC)]).then_inc(u_done, 1)

                def turn_v():
                    if not s.proj:
                        return
                    pe.wait_ge(u_copied, n * U + 4)
                    pe.wait_ge(v_copied, v0 + 1)
                    for t in range(TILES):
                        ins = nc.tensor.transpose(v_ps[:, t * P:(t + 1) * P], vT[:, t * P:(t + 1) * P], ident[:])
                    ins.then_inc(v_turned, 1)

                def fold_half(half):
                    if not s.steady:
                        return
                    if half == 0:
                        pe.wait_ge(nat_loaded, m * 16 + 16)
                    pe.wait_ge(v_copied, v0 + (half + 2))
                    mixer = mix[:, 7] if s.cross else mix[:, bass.ds(s.attn_g, 1)].rearrange("p a n -> p (a n)")
                    for k in range(4):
                        ins = nc.tensor.matmul(v_ps[:, k * P:(k + 1) * P],
                                               nat[:, (4 * half + k) * P:(4 * half + k + 1) * P], mixer,
                                               start=True, stop=True)
                    ins.then_inc(folded, 1)

                def scores(t):
                    if not s.attn:
                        return
                    if t == 0:
                        pe.wait_ge(u_copied, n * U + 2)
                        if s.cross:
                            pe.wait_ge(ln.lo_done, s.b * ln.GROUPS + 5)
                    pe.wait_ge(s_masked, m * TILES + (t + 1))
                    for h in range(QPG):
                        ins = nc.tensor.matmul(s_ps[:, h * P:(h + 1) * P], qT[:, mp, h, t * P:(t + 1) * P],
                                               kT[:, mp, t * P:(t + 1) * P], start=True, stop=True)
                    ins.then_inc(s_done, 1)

                def turn_probs(t):
                    if not s.attn:
                        return
                    pe.wait_ge(probs_ready, m * TILES + (t + 1))
                    pe.wait_ge(probsT_ready, m * TILES + (t + 1))
                    for h in range(QPG):
                        ins = nc.tensor.transpose(t_ps[:, h * P:(h + 1) * P], probs[:, h], ident[:])
                    ins.then_inc(probs_turned, 1)

                def mix_values(t):
                    if not s.attn:
                        return
                    if t == 0:
                        pe.wait_ge(v_copied, v0 + 1)
                    pe.wait_ge(probsT_ready, m * TILES + (t + 2))
                    pe.wait_ge(o_split, m * TILES + (t + 1))
                    three_passes(nc, o_ps[:], [(vh[:, mp, t], vl[:, mp, t], probsTh[:], probsTl[:])]
                                 ).then_inc(o_done, 1)

                def project(t):
                    if not s.attn:
                        return
                    if t == 0:
                        pe.wait_ge(p_split, m * QPG + 2 * QPG)
                    pe.wait_ge(o_split, m * TILES + (t + 2))
                    for half in range(2):
                        pe.wait_ge(pr_free, m * PR + (2 * t + half + 1))
                        cols = slice(half * HALF, (half + 1) * HALF)
                        ins = three_passes(nc, pr_ps[half][:],
                                           [(oh[:, h * P:(h + 1) * P], ol[:, h * P:(h + 1) * P],
                                             ph[:, h, cols], pl[:, h, cols]) for h in range(QPG)])
                        ins.then_inc(pr_done, 1)

                scores(0)
                unit(0)
                turn_probs(0)
                scores(1)
                unit(1)
                mix_values(0)
                turn_probs(1)
                scores(2)
                unit(2)
                turn_v()
                project(0)
                mix_values(1)
                turn_probs(2)
                scores(3)
                unit(3)
                fold_half(0)
                project(1)
                mix_values(2)
                turn_probs(3)
                unit(4)
                fold_half(1)
                project(2)
                mix_values(3)
                unit(5)
                if s.norm:
                    pe.wait_ge(o_split, m * TILES + (TILES + 1))
                    pe.wait_ge(v_copied, v0 + 4)
                    turn_groups(s.b + 1, range(4))
                project(3)
                if s.norm:
                    turn_groups(s.b + 1, range(4, 8))

            pipeline(pe, first_block, step)

        @block.scalar
        def _(act):
            act.sem_inc(u_copied, 2)
            act.sem_inc(fold_stored, 16)

            def weights(n, u):
                act.wait_ge(wraw_loaded[u % 3], n * 32 + (16 * (u // 3) + 16))
                nc.scalar.activation(wh[:, u % 3], wraw[:, u % 3], ACT.Copy).then_inc(w_hi, 1)

            def first_block():
                for u in range(3):
                    weights(0, u)
                ln.deviations(act, 0)
                for r in range(8):
                    ln.high(act, 0, r, turn_ps[r % 4])

            def step(s):
                n, m = s.n, s.m
                v0 = v_uses(s)
                dst = [kT[:, s.par], vT[:]] + [qT[:, s.par, h] for h in range(QPG)]

                def copy_unit(u):
                    if not s.proj:
                        return
                    act.wait_ge(u_done, n * U + (u + 1))
                    nc.scalar.activation(dst[u], u_ps[u % 2][:], ACT.Copy).then_inc(u_copied, 1)
                    if u < 3:
                        weights(n, u + 3)
                    elif s.nxt:
                        weights(n + 1, u - 3)

                def copy_v():
                    if not s.proj:
                        return
                    act.wait_ge(v_turned, n + 1)
                    nc.scalar.activation(vh[:, s.par].rearrange("p t d -> p (t d)"), v_ps[:], ACT.Copy
                                         ).then_inc(v_hi, 1)

                def copy_fold(half):
                    if not s.steady:
                        return
                    act.wait_ge(folded, m * 2 + (half + 3))
                    if half == 0:
                        act.wait_ge(fold_stored, m * 16 + 16)
                    nc.scalar.activation(fold[:, half * HALF:(half + 1) * HALF], v_ps[:], ACT.Copy
                                         ).then_inc(v_copied, 1)

                def store_fold():
                    if not s.steady:
                        return
                    act.wait_ge(v_copied, v0 + 4)
                    act.dma_start(tile_of(w_folded, m), fold[:]).then_inc(fold_stored, 16)

                def out_weights(hs):
                    if not s.attn:
                        return
                    act.wait_ge(pr_done, m * PR + 1)
                    for h in hs:
                        act.wait_ge(praw_loaded[h], n * 16)
                        nc.scalar.activation(ph[:, h], praw[:, h], ACT.Copy).then_inc(p_hi, 1)

                def exps(t):
                    if not s.attn:
                        return
                    act.wait_ge(s_shifted, m * TILES + (t + 1))
                    nc.scalar.activation(probs[:], probs[:], ACT.Exp, scale=SELF_SCALE).then_inc(exp_done, 1)

                def copy_probs(t):
                    if not s.attn:
                        return
                    act.wait_ge(probs_turned, m * TILES + (t + 1))
                    nc.scalar.activation(probsTh[:], t_ps[:], ACT.Copy).then_inc(probsT_hi, 1)

                def high_o(t):
                    if not s.attn:
                        return
                    act.wait_ge(o_done, m * TILES + (t + 1))
                    nc.scalar.activation(oh[:], o_ps[:], ACT.Copy).then_inc(o_hi, 1)

                out_weights([0, 1])
                exps(0)
                copy_unit(0)
                copy_probs(0)
                out_weights([2, 3])
                exps(1)
                copy_unit(1)
                high_o(0)
                copy_probs(1)
                exps(2)
                copy_unit(2)
                copy_v()
                high_o(1)
                copy_probs(2)
                exps(3)
                copy_unit(3)
                copy_fold(0)
                high_o(2)
                copy_probs(3)
                if s.norm:
                    ln.deviations(act, s.b + 1)
                copy_unit(4)
                copy_fold(1)
                store_fold()
                high_o(3)
                copy_unit(5)
                if s.norm:
                    for r in range(8):
                        ln.high(act, s.b + 1, r, turn_ps[r % 4])

            pipeline(act, first_block, step)
            act.wait_ge(fold_stored, 16 * (3 * CH + 1))

        @block.vector
        def _(dve):
            dve.sem_inc(v_copied, 1)
            dve.sem_inc(probsT_ready, 1)
            dve.sem_inc(s_masked, 1)
            dve.sem_inc(o_split, 1)
            dve.sem_inc(pr_free, 2)

            def first_block():
                ln.moments(dve, 0)
                ln.normalise(dve, 0)
                for r in range(8):
                    ln.low(dve, 0, r, turn_ps[r % 4])

            def step(s):
                m = s.m

                def low_v():
                    if not s.proj:
                        return
                    dve.wait_ge(v_hi, s.n + 1)
                    nc.vector.tensor_tensor(vl[:, s.par].rearrange("p t d -> p (t d)"), v_ps[:],
                                            f32(vh[:, s.par]).rearrange("p t d -> p (t d)"), ALU.subtract
                                            ).then_inc(v_copied, 1)

                if not s.attn:
                    low_v()
                    return

                def softmax(t):
                    i = m * TILES + (t + 1)
                    dve.wait_ge(s_done, i)
                    nc.vector.tensor_tensor(probs[:], s_ps[:].rearrange("p (h n) -> p h n", h=QPG),
                                            causal[:].unsqueeze(1).broadcast_to([P, QPG, P]), ALU.add
                                            ).then_inc(s_masked, 1)
                    dve.wait_ge(s_masked, i + 1)
                    nc.vector.tensor_reduce(top[:], probs[:], AX.X, ALU.max).then_inc(s_top, 1)
                    dve.wait_ge(s_top, i)
                    nc.vector.tensor_tensor(probs[:], probs[:], top[:].unsqueeze(2).broadcast_to([P, QPG, P]),
                                            ALU.subtract).then_inc(s_shifted, 1)
                    dve.wait_ge(exp_done, i)
                    nc.vector.tensor_reduce(total[:], probs[:], AX.X, ALU.add).then_inc(total_done, 1)
                    dve.wait_ge(total_done, i)
                    nc.vector.reciprocal(inv[:], total[:]).then_inc(inv_done, 1)
                    dve.wait_ge(inv_done, i)
                    nc.vector.tensor_tensor(probs[:], probs[:], inv[:].unsqueeze(2).broadcast_to([P, QPG, P]),
                                            ALU.mult).then_inc(probs_ready, 1)

                def low_probs(t):
                    dve.wait_ge(probsT_hi, m * TILES + (t + 1))
                    nc.vector.tensor_tensor(probsTl[:], t_ps[:], f32(probsTh[:]), ALU.subtract
                                            ).then_inc(probsT_ready, 1)

                def low_o(t):
                    dve.wait_ge(o_hi, m * TILES + (t + 1))
                    nc.vector.tensor_tensor(ol[:], o_ps[:], f32(oh[:]), ALU.subtract).then_inc(o_split, 1)

                def add_projected(t):
                    dve.wait_ge(acc_loaded[t], s.attn_b * 16 + 16)
                    for half in range(2):
                        dve.wait_ge(pr_done, m * PR + (2 * t + half + 2))
                        part = acc[:, t, half * HALF:(half + 1) * HALF]
                        nc.vector.tensor_tensor(part, pr_ps[half][:], part, ALU.add).then_inc(pr_free, 1)

                def next_moments(t):
                    if s.norm:
                        ln.moments(dve, s.b + 1, [t])

                softmax(0)
                low_probs(0)
                softmax(1)
                low_o(0)
                low_probs(1)
                softmax(2)
                low_v()
                add_projected(0)
                next_moments(0)
                low_o(1)
                low_probs(2)
                softmax(3)
                next_moments(1)
                add_projected(1)
                next_moments(2)
                low_o(2)
                low_probs(3)
                next_moments(3)
                add_projected(2)
                if s.norm:
                    ln.normalise(dve, s.b + 1)
                low_o(3)
                if s.norm:
                    for r in range(4):
                        ln.low(dve, s.b + 1, r, turn_ps[r % 4])
                add_projected(3)
                if s.norm:
                    for r in range(4, 8):
                        ln.low(dve, s.b + 1, r, turn_ps[r % 4])

            pipeline(dve, first_block, step)



def cross_attention_phase(nc, sems, ident, pairmask, bias_qkv, eps, x1, ctxT, w_folded, wo, x2):
    PR = TILES * 2
    U = 3
    WHICH = [1, 0, 2]
    PAIRS = SLOTS // 2
    PC = P // PAIRS
    PARTS = 3
    CRAW = 4
    STACK = 16 * PARTS * PAIRS
    OUT, VALUE, KEY, QUERY = range(4)
    ITEMS = 4
    DP = 32
    with ExitStack() as ctx:
        def sb(name, shape, dt=F32):
            return ctx.enter_context(nc.sbuf_tensor(name, shape, dt))

        def psum(name, cols=HALF):
            return ctx.enter_context(nc.psum_tensor(name, [P, cols], F32))

        def sem(name):
            return sems.enter_context(nc.semaphore(name))

        ln = NormBuffers(nc, ctx, sems, "ca_ln", eps)
        acc = sb("ca_acc", [P, TILES, D])
        ch = sb("ca_ch", [P, KC, BT], F32R)
        cl = sb("ca_cl", [P, KC, BT], F32R)
        craw = sb("ca_craw", [P, CRAW, BT])
        wraw = sb("ca_wraw", [P, 2, D])
        wh = sb("ca_wh", [P, U, D], F32R)
        wl = sb("ca_wl", [P, U, D], F32R)
        owh = sb("ca_owh", [P, D], F32R)
        owl = sb("ca_owl", [P, D], F32R)
        kh = sb("ca_kh", [P, BT], F32R)
        kl = sb("ca_kl", [P, BT], F32R)
        qh = sb("ca_qh", [P, BT], F32R)
        ql = sb("ca_ql", [P, BT], F32R)
        kmh = sb("ca_kmh", [P, 2, BT], F32R)
        kml = sb("ca_kml", [P, 2, BT], F32R)
        kstack = sb("ca_kstack", [PARTS * PC, 2, PAIRS, 2, BT], F32R)
        qstack = sb("ca_qstack", [PARTS * PC, PAIRS, BT], F32R)
        vT = sb("ca_vT", [P, BT])
        v = sb("ca_v", [P, TILES * SLOTS, DP])
        probs = sb("ca_probs", [P, 2, SLOTS, P])
        probsT = sb("ca_probsT", [P, SLOTS * P])
        bias_now = sb("ca_bias_now", [P, 2, 3])
        top = sb("ca_top", [P, SLOTS])
        inv = sb("ca_inv", [P, SLOTS])
        oT = sb("ca_oT", [P, 2 * P])
        o = sb("ca_o", [P, P])
        oh = sb("ca_oh", [P, P], F32R)
        ol = sb("ca_ol", [P, P], F32R)

        u_ps = [psum(f"ca_u{i}") for i in range(2)]
        s_ps = psum("ca_s", 2 * HALF)
        t_ps = psum("ca_t", 2 * HALF)
        o_ps = psum("ca_o_ps")
        x_ps = psum("ca_x")
        turn_ps = [x_ps, o_ps]

        acc_loaded = [sem(f"ca_acc_loaded{t}") for t in range(TILES)]
        craw_loaded = [sem(f"ca_craw_loaded{i}") for i in range(CRAW)]
        c_hi = sem("ca_c_hi")
        c_used = sem("ca_c_used")
        c_split = sem("ca_c_split")
        wraw_loaded = [sem(f"ca_wraw_loaded{i}") for i in range(2)]
        w_hi = sem("ca_w_hi")
        w_split = sem("ca_w_split")
        u_done = sem("ca_u_done")
        u_hi = sem("ca_u_hi")
        u_free = sem("ca_u_free")
        bias_ready = sem("ca_bias_ready")
        v_set = sem("ca_v_set")
        v_turned = sem("ca_v_turned")
        v_placed = sem("ca_v_placed")
        km_ready = sem("ca_km_ready")
        k_stacked = sem("ca_k_stacked")
        q_stacked = sem("ca_q_stacked")
        s_done = sem("ca_s_done")
        s_top = sem("ca_s_top")
        s_shifted = sem("ca_s_shifted")
        probs_ready = sem("ca_probs_ready")
        probs_turned = sem("ca_probs_turned")
        probsT_ready = sem("ca_probsT_ready")
        pv_done = sem("ca_pv_done")
        oT_ready = sem("ca_oT_ready")
        oT_turned = sem("ca_oT_turned")
        inv_done = sem("ca_inv_done")
        o_ready = sem("ca_o_ready")
        o_turned = sem("ca_o_turned")
        o_hi = sem("ca_o_hi")
        o_split = sem("ca_o_split")
        pr_done = sem("ca_pr_done")
        x_free = sem("ca_x_free")
        x2_stored = [sem(f"ca_x2_stored{t}") for t in range(TILES)]

        x1_by_i = x1.rearrange("t p n -> (t p) n").rearrange("(j i) n -> i j n", i=SEQ)

        block = ctx.enter_context(nc.Block())

        high_weights = {OUT: owh[:], VALUE: wh[:, 2], KEY: wh[:, 0], QUERY: wh[:, 1]}
        low_weights = {OUT: owl[:], VALUE: wl[:, 2], KEY: wl[:, 0], QUERY: wl[:, 1]}

        def splits(n, item, skipped=0):
            return n * ITEMS + (item + 3 - skipped)

        def pr_bank(t, half):
            return o_ps if (t, half) == (TILES - 1, 1) else x_ps

        def turns(s):
            return s.cross or not s.attn

        @block.sync
        def _(sp):
            def weights(n, item, g, skipped=0):
                if not (isinstance(n, int) and n < 0):
                    sp.wait_ge(w_split, splits(n, item + (-2), skipped))
                src = {OUT: wo, VALUE: w_folded, KEY: w_folded, QUERY: w_folded}[item]
                first = {OUT: 0, VALUE: 2 * CH, KEY: CH, QUERY: 0}[item]
                sp.dma_start(wraw[:, item % 2], tile_of(src, g + first)).then_inc(wraw_loaded[item % 2], 16)

            def load(b, dst, sem_of_tile):
                for t in range(TILES):
                    sp.dma_start(dst[:, t], tile_of(x1_by_i, b * TILES + t)).then_inc(sem_of_tile[t], 16)

            def load_context(b, ks):
                for k in ks:
                    sp.wait_ge(c_split, b * KC + (k + 1))
                    sp.dma_start(craw[:, k % CRAW], tile_of(ctxT, b * KC + k)
                                 ).then_inc(craw_loaded[k % CRAW], 16)

            def stack(dst, a, part, stacked):
                for r in range(PAIRS):
                    sp.dma_start(f32(dst[a * PC:(a + 1) * PC, r]), f32(part[r * PC:(r + 1) * PC])
                                 ).then_inc(stacked, 16)

            def first_block():
                weights(-1, KEY, 0)
                load_context(0, range(CRAW))
                load(0, ln.x, ln.loaded)
                weights(-1, QUERY, 0)
                load_context(0, range(CRAW, KC))
                weights(0, OUT, 0)
                weights(0, VALUE, 0)

            def step(s):
                if s.norm:
                    sp.wait_ge(ln.turned, s.b * ln.GROUPS + ln.GROUPS)
                    load(s.b + 1, ln.x, ln.loaded)
                    load_context(s.b + 1, range(CRAW))
                if s.nxt:
                    weights(s.n, KEY, s.next_g)
                    weights(s.n, QUERY, s.next_g)
                if not s.attn:
                    load(0, acc, acc_loaded)
                if s.proj:
                    sp.wait_ge(km_ready, s.n * 2 + 1)
                    stack(kstack[:, s.par], 0, kmh, k_stacked)
                    stack(kstack[:, s.par], 2, kmh, k_stacked)
                    sp.wait_ge(km_ready, s.n * 2 + 2)
                    stack(kstack[:, s.par], 1, kml, k_stacked)
                    weights(s.n + 1, OUT, s.g, 0 if s.nxt else 2)
                    sp.wait_ge(u_hi, s.n * 2 + 2)
                    if s.attn:
                        sp.wait_ge(s_done, s.m * TILES + TILES)
                    stack(qstack, 0, qh, q_stacked)
                    stack(qstack, 1, qh, q_stacked)
                    sp.wait_ge(u_free, s.n * U + 4)
                    stack(qstack, 2, ql, q_stacked)
                    if s.nxt:
                        weights(s.n + 1, VALUE, s.next_g)
                if s.norm:
                    load_context(s.b + 1, range(CRAW, KC))
                if s.cross or not s.proj:
                    for t in range(TILES):
                        sp.wait_ge(x_free, s.m * PR + (2 * t + 3))
                        sp.dma_start(tile_of(x2, s.attn_b * TILES + t), acc[:, t]).then_inc(x2_stored[t], 16)
                if s.cross:
                    for t in range(TILES):
                        sp.wait_ge(x2_stored[t], s.b * 16)
                        sp.dma_start(acc[:, t], tile_of(x1_by_i, s.b * TILES + t)).then_inc(acc_loaded[t], 16)

            pipeline(sp, first_block, step)
            for t in range(TILES):
                sp.wait_ge(x2_stored[t], 16 * BLOCKS)

        @block.gpsimd
        def _(pool):
            pool.sem_inc(c_split, CRAW)
            nc.gpsimd.memset(v[:], 0.0).then_inc(v_set, 1)
            pool.wait_ge(v_set, 1)
            nc.gpsimd.memset(v[:, :, DK:DK + 1], 1.0).then_inc(v_set, 1)

            def weights(n, item, skipped=0):
                pool.wait_ge(w_hi, splits(n, item, skipped))
                nc.gpsimd.tensor_tensor(low_weights[item], wraw[:, item % 2], f32(high_weights[item]), ALU.subtract
                                        ).then_inc(w_split, 1)

            def context_low(b):
                for k in range(KC):
                    pool.wait_ge(c_hi, b * KC + (k + 1))
                    nc.gpsimd.tensor_tensor(cl[:, k], craw[:, k % CRAW], f32(ch[:, k]), ALU.subtract
                                            ).then_inc(c_split, 1)

            def mask_k(s):
                pool.wait_ge(u_free, s.n * U + 3)
                if s.attn:
                    pool.wait_ge(k_stacked, s.n * STACK)
                mask = pairmask[:].unsqueeze(2).broadcast_to([P, 2, BT])
                for dst, src in ((kmh, kh), (kml, kl)):
                    nc.gpsimd.tensor_tensor(
                        dst[:], f32(src[:]).unsqueeze(1).broadcast_to([P, 2, BT]), mask, ALU.mult
                    ).then_inc(km_ready, 1)

            def first_block():
                weights(-1, KEY)
                context_low(0)
                weights(-1, QUERY)

            def step(s):
                weights(s.n, OUT, 0 if s.proj else 2)
                if s.proj:
                    weights(s.n, VALUE)
                    mask_k(s)
                if s.nxt:
                    weights(s.n, KEY)
                    weights(s.n, QUERY)
                if s.norm:
                    context_low(s.b + 1)

            pipeline(pool, first_block, step)

        @block.tensor
        def _(pe):
            pe.sem_inc(pr_done, 1)

            def first_block():
                pass

            def step(s):
                n, m = s.n, s.m

                def pieces(*numbers):
                    for i in numbers if s.proj else ():
                        u, k = i // KC, i % KC
                        if k == 0:
                            pe.wait_ge(w_split, [splits(n, KEY - ITEMS), splits(n, QUERY - ITEMS), splits(n, VALUE)][u])
                            if u == 1 and turns(s):
                                pe.wait_ge(ln.lo_done, s.b * ln.GROUPS + ln.GROUPS)
                            pe.wait_ge(u_free, n * U + (u + 1))
                        if u == 0 and turns(s):
                            pe.wait_ge(c_split, s.b * KC + (k + 1 + CRAW))
                        bh, bl = (ln.xh, ln.xl) if u == 1 else (ch, cl)
                        ins = three_passes(nc, u_ps[(s.par * U + u) % 2][:],
                                           [(wh[:, u, k * P:(k + 1) * P], wl[:, u, k * P:(k + 1) * P],
                                             bh[:, k], bl[:, k])], first=k == 0, last=k == KC - 1)
                        if k == KC - 1:
                            ins.then_inc(u_done, 1)
                        elif s.norm and u == 2:
                            ins.then_inc(c_used, 1)

                def turn_x(r):
                    if not turns(s):
                        return
                    if r >= 2:
                        pe.wait_ge(ln.lo_done, s.b * ln.GROUPS + (r - 1))
                    elif s.attn:
                        pe.wait_ge(x_free, m * PR + r)
                    ln.turn(pe, s.b, r, ident, turn_ps[r % 2])

                def turn_v():
                    if not s.attn:
                        return
                    pe.wait_ge(u_free, n * U + 2)
                    pe.wait_ge(probsT_ready, m * TILES + 1)
                    for t in range(TILES):
                        ins = nc.tensor.transpose(t_ps[:, t * P:(t + 1) * P], vT[:, t * P:(t + 1) * P], ident[:])
                    ins.then_inc(v_turned, 1)

                def scores(t):
                    if not s.attn:
                        return
                    if t == 0:
                        pe.wait_ge(k_stacked, n * STACK)
                        pe.wait_ge(q_stacked, n * STACK)
                    pe.wait_ge(s_shifted, m * TILES + (t + 1))
                    for r in range(PAIRS):
                        ins = nc.tensor.matmul(s_ps[:, r * 2 * P:(r + 1) * 2 * P], qstack[:, r, t * P:(t + 1) * P],
                                               kstack[:, 1 - s.par, r, :, t * P:(t + 1) * P], start=True, stop=True)
                    ins.then_inc(s_done, 1)

                def turn_probs(t):
                    if not s.attn:
                        return
                    if t == 0:
                        pe.wait_ge(v_placed, n)
                    pe.wait_ge(probs_ready, m * TILES + (t + 1))
                    pe.wait_ge(probsT_ready, m * TILES + (t + 1))
                    for j in range(SLOTS):
                        ins = nc.tensor.transpose(t_ps[:, j * P:(j + 1) * P], probs[:, t % 2, j], ident[:])
                    ins.then_inc(probs_turned, 1)

                def mix_values(t):
                    if not s.attn:
                        return
                    if t == 0:
                        pe.wait_ge(x_free, m * PR + 1)
                        if s.cross:
                            pe.wait_ge(ln.lo_done, s.b * ln.GROUPS + ln.GROUPS)
                    pe.wait_ge(probsT_ready, m * TILES + (t + 2))
                    pe.wait_ge(o_split, m * TILES + (t + 1))
                    for j in range(SLOTS):
                        rows = slice(DP * (j % 4), DP * (j % 4 + 1))
                        ins = nc.tensor.matmul(o_ps[rows, (j // 4) * P:(j // 4 + 1) * P],
                                               v[:, t * SLOTS + j], probsT[:, j * P:(j + 1) * P],
                                               start=True, stop=True)
                    ins.then_inc(pv_done, 1)

                def turn_oT(t):
                    if not s.attn:
                        return
                    pe.wait_ge(oT_ready, m * TILES + (t + 1))
                    for a in range(2):
                        ins = nc.tensor.transpose(o_ps[:, (2 + a) * P:(3 + a) * P], oT[:, a * P:(a + 1) * P],
                                                  ident[:])
                    ins.then_inc(oT_turned, 1)

                def turn_o(t):
                    if not s.attn:
                        return
                    pe.wait_ge(o_ready, m * TILES + (t + 1))
                    nc.tensor.transpose(o_ps[:, 0:P], o[:], ident[:]).then_inc(o_turned, 1)

                def project(t, half):
                    if not s.attn:
                        return
                    if t == 0 and half == 0:
                        pe.wait_ge(w_split, splits(n, OUT, 0 if s.proj else 2))
                    if half == 0:
                        pe.wait_ge(o_split, m * TILES + (t + 2))
                    if (t, half) != (TILES - 1, 1):
                        pe.wait_ge(x_free, m * PR + (2 * t + half + 1))
                    cols = slice(half * HALF, (half + 1) * HALF)
                    three_passes(nc, pr_bank(t, half)[:], [(oh[:], ol[:], owh[:, cols], owl[:, cols])]
                                 ).then_inc(pr_done, 1)

                if not s.attn:
                    pieces(0, 1, 2, 3)
                    for r in range(ln.GROUPS):
                        turn_x(r)
                        if r < 4:
                            pieces(4 + r)
                    pieces(*range(KC, U * KC))
                    return
                if s.cross:
                    turn_x(0)
                    turn_x(1)
                    pieces(0)
                    turn_x(2)
                    pieces(1)
                    turn_x(3)
                    scores(0)
                else:
                    scores(0)
                    pieces(0, 1)
                turn_v()
                pieces(2)
                turn_x(4)
                pieces(3)
                turn_x(5)
                pieces(4)
                turn_x(6)
                turn_probs(0)
                pieces(5)
                turn_x(7)
                for t in range(1, TILES):
                    first = 5 * t + 1
                    scores(t)
                    mix_values(t - 1)
                    pieces(first)
                    turn_oT(t - 1)
                    pieces(first + 1, first + 2)
                    turn_o(t - 1)
                    pieces(first + 3, first + 4)
                    project(t - 1, 0)
                    turn_probs(t)
                    project(t - 1, 1)
                mix_values(3)
                pieces(21)
                turn_oT(3)
                pieces(22)
                turn_o(3)
                pieces(23)
                project(3, 0)
                project(3, 1)

            pipeline(pe, first_block, step)

        @block.scalar
        def _(act):
            act.sem_inc(probsT_ready, 1)

            def weights(n, item, skipped=0):
                act.wait_ge(wraw_loaded[item % 2], n * 32 + (16 * (item // 2) + 32 - 8 * skipped))
                nc.scalar.activation(high_weights[item], wraw[:, item % 2], ACT.Copy).then_inc(w_hi, 1)

            def context_high(b, ks):
                for k in ks:
                    act.wait_ge(craw_loaded[k % CRAW], b * (16 * KC // CRAW) + (16 * (k // CRAW) + 16))
                    nc.scalar.activation(ch[:, k], craw[:, k % CRAW], ACT.Copy).then_inc(c_hi, 1)

            def first_block():
                weights(-1, KEY)
                context_high(0, range(KC))
                weights(-1, QUERY)
                ln.deviations(act, 0)

            def step(s):
                n, m = s.n, s.m

                def set_bias():
                    if not s.proj:
                        return
                    src = bias_qkv[:, s.g] if isinstance(s.g, int) else bias_qkv[:, bass.ds(s.g, 1)].rearrange("p a w -> p (a w)")
                    nc.scalar.activation(bias_now[:, s.par], src, ACT.Copy).then_inc(bias_ready, 1)

                def high_unit(u, dst, used, count):
                    if not s.proj:
                        return
                    if s.attn:
                        act.wait_ge(used, count)
                    act.wait_ge(bias_ready, n + 1)
                    act.wait_ge(u_done, n * U + (u + 1))
                    w = WHICH[u]
                    nc.scalar.activation(dst[:], u_ps[(s.par * U + u) % 2][:], ACT.Identity,
                                         bias=bias_now[:, s.par, w:w + 1]).then_inc(u_hi, 1)

                def out_weights():
                    if s.attn:
                        act.wait_ge(pr_done, m * PR + 1)
                    weights(n, OUT, 0 if s.proj else 2)

                def value_weights():
                    if s.proj:
                        if s.attn:
                            act.wait_ge(u_done, n * U)
                        weights(n, VALUE)

                def next_weights(item, u):
                    if s.nxt:
                        act.wait_ge(u_done, n * U + (u + 1))
                        weights(n, item)

                def exps(t):
                    if not s.attn:
                        return
                    act.wait_ge(s_shifted, m * TILES + (t + 2))
                    nc.scalar.activation(probs[:, t % 2], probs[:, t % 2], ACT.Exp, scale=CROSS_SCALE
                                         ).then_inc(probs_ready, 1)

                def copy_probs(t):
                    if not s.attn:
                        return
                    act.wait_ge(probs_turned, m * TILES + (t + 1))
                    nc.scalar.activation(probsT[:], t_ps[:], ACT.Copy).then_inc(probsT_ready, 1)

                def copy_oT(t):
                    if not s.attn:
                        return
                    act.wait_ge(pv_done, m * TILES + (t + 1))
                    nc.scalar.activation(oT[:], o_ps[:, 0:2 * P], ACT.Copy).then_inc(oT_ready, 1)

                def high_o(t):
                    if not s.attn:
                        return
                    act.wait_ge(o_turned, m * TILES + (t + 1))
                    nc.scalar.activation(oh[:], o_ps[:, 0:P], ACT.Copy).then_inc(o_hi, 1)

                def high_x(*rs):
                    if turns(s):
                        for r in rs:
                            ln.high(act, s.b, r, turn_ps[r % 2])

                def next_context(*ks):
                    if s.norm:
                        for k in ks:
                            if k < KC - 1:
                                act.wait_ge(c_used, s.b * (KC - 1) + (k + 1))
                            else:
                                act.wait_ge(u_done, n * U + 3)
                            context_high(s.b + 1, [k])

                set_bias()
                high_x(0, 1, 2, 3)
                exps(0)
                high_x(4, 5)
                out_weights()
                high_x(6)
                copy_probs(0)
                high_x(7)
                copy_oT(0)
                value_weights()
                high_o(0)
                high_unit(0, kh, km_ready, n * 2)
                exps(1)
                next_weights(KEY, 0)
                copy_probs(1)
                copy_oT(1)
                high_o(1)
                exps(2)
                high_unit(1, qh, q_stacked, n * STACK)
                copy_probs(2)
                next_weights(QUERY, 1)
                copy_oT(2)
                high_o(2)
                exps(3)
                if s.norm:
                    ln.deviations(act, s.b + 1)
                next_context(0, 1)
                copy_probs(3)
                next_context(2)
                copy_oT(3)
                next_context(3)
                high_o(3)
                next_context(4, 5, 6, 7)

            pipeline(act, first_block, step)

        @block.vector
        def _(dve):
            dve.sem_inc(u_free, 2)
            dve.sem_inc(s_shifted, 1)
            dve.sem_inc(o_split, 1)
            dve.sem_inc(x_free, 1)

            def first_block():
                ln.moments(dve, 0)
                ln.normalise(dve, 0)

            def step(s):
                n, m = s.n, s.m

                def low_unit(u, dst, hi, number):
                    if not s.proj:
                        return
                    dve.wait_ge(u_hi, n * 2 + number)
                    w = WHICH[u]
                    nc.vector.scalar_tensor_tensor(dst[:], u_ps[(s.par * U + u) % 2][:],
                                                   bias_now[:, s.par, w:w + 1], f32(hi[:]),
                                                   ALU.add, ALU.subtract).then_inc(u_free, 1)

                def copy_vT():
                    if not s.proj:
                        return
                    dve.wait_ge(u_done, n * U + 3)
                    nc.vector.tensor_scalar(vT[:], u_ps[(s.par * U + 2) % 2][:], bias_now[:, s.par, 2:3], None,
                                            ALU.add).then_inc(u_free, 1)

                def place_v():
                    if not s.attn:
                        return
                    dve.wait_ge(v_set, 2)
                    dve.wait_ge(v_turned, n)
                    nc.vector.tensor_copy(v[:, :, 0:DK], t_ps[:, 0:BT].rearrange("p (s d) -> p s d", d=DK)
                                          ).then_inc(v_placed, 1)

                def tops(t):
                    if not s.attn:
                        return
                    dve.wait_ge(s_done, m * TILES + (t + 1))
                    nc.vector.tensor_reduce(top[:], s_ps[:].rearrange("p (s n) -> p s n", s=SLOTS), AX.X,
                                            ALU.max).then_inc(s_top, 1)

                def shift(t):
                    if not s.attn:
                        return
                    dve.wait_ge(s_top, m * TILES + (t + 1))
                    nc.vector.tensor_tensor(probs[:, t % 2], s_ps[:].rearrange("p (s n) -> p s n", s=SLOTS),
                                            top[:].unsqueeze(2).broadcast_to([P, SLOTS, P]), ALU.subtract
                                            ).then_inc(s_shifted, 1)

                def scale_o(t):
                    if not s.attn:
                        return
                    ov = o_ps[:, 2 * P:4 * P].rearrange("p (s w) -> p s w", w=DP)
                    dve.wait_ge(oT_turned, m * TILES + (t + 1))
                    nc.vector.reciprocal(inv[:], ov[:, :, DK]).then_inc(inv_done, 1)
                    dve.wait_ge(inv_done, m * TILES + (t + 1))
                    nc.vector.tensor_tensor(o[:].rearrange("p (s d) -> p s d", d=DK), ov[:, :, 0:DK],
                                            inv[:].unsqueeze(2).broadcast_to([P, SLOTS, DK]), ALU.mult
                                            ).then_inc(o_ready, 1)

                def low_o(t):
                    if not s.attn:
                        return
                    dve.wait_ge(o_hi, m * TILES + (t + 1))
                    nc.vector.tensor_tensor(ol[:], o_ps[:, 0:P], f32(oh[:]), ALU.subtract).then_inc(o_split, 1)

                def add_projected(t, half):
                    if not s.attn:
                        return
                    if half == 0:
                        dve.wait_ge(acc_loaded[t], s.attn_b * 16 + 16)
                    dve.wait_ge(pr_done, m * PR + (2 * t + half + 2))
                    part = acc[:, t, half * HALF:(half + 1) * HALF]
                    nc.vector.tensor_tensor(part, pr_bank(t, half)[:], part, ALU.add).then_inc(x_free, 1)

                def low_x(*rs):
                    if turns(s):
                        for r in rs:
                            ln.low(dve, s.b, r, turn_ps[r % 2])

                def next_moments(*ts):
                    if s.norm:
                        ln.moments(dve, s.b + 1, ts)

                low_x(0, 1, 2, 3)
                tops(0)
                shift(0)
                place_v()
                low_x(4, 5, 6, 7)
                next_moments(0, 1)
                tops(1)
                scale_o(0)
                shift(1)
                low_o(0)
                low_unit(0, kl, kh, 1)
                add_projected(0, 0)
                add_projected(0, 1)
                tops(2)
                scale_o(1)
                shift(2)
                low_o(1)
                next_moments(2)
                add_projected(1, 0)
                add_projected(1, 1)
                tops(3)
                scale_o(2)
                shift(3)
                low_o(2)
                next_moments(3)
                add_projected(2, 0)
                low_unit(1, ql, qh, 2)
                add_projected(2, 1)
                if s.norm:
                    ln.normalise(dve, s.b + 1)
                scale_o(3)
                low_o(3)
                copy_vT()
                add_projected(3, 0)
                add_projected(3, 1)

            pipeline(dve, first_block, step)



def ffn_phase(nc, sems, ident, eps, x2, bo, vh, uT, s_all, alpha, beta, u_rT, vh_r, s_r, d_r, r_mat, bias,
              out):
    with ExitStack() as ctx:
        def sb(name, shape, dt=F32):
            return ctx.enter_context(nc.sbuf_tensor(name, shape, dt))

        def sem(name):
            return sems.enter_context(nc.semaphore(name))

        bo_sb = sb("ff_bo", [P, D])
        ln = NormBuffers(nc, ctx, sems, "ff_ln", eps, offset=bo_sb)
        acc = sb("ff_acc", [P, TILES, D])
        vh_sb = sb("ff_vh", [P, KC, D])
        uT_sb = sb("ff_uT", [P, KC, D])
        s_sb = sb("ff_s", [P, KC])
        ab = sb("ff_ab", [R_TOP, 2])
        small = sb("ff_small", [R_INT, 2])
        urT_sb = sb("ff_urT", [R_INT, D])
        vhr_sb = sb("ff_vhr", [R_INT, D])
        r_sb = sb("ff_r", [R_INT, R_INT])
        delta = sb("ff_delta", [R_INT, D])
        bias_sb = sb("ff_bias", [P, D])
        weh = sb("ff_weh", [P, KC, D], F32R)
        wel = sb("ff_wel", [P, KC, D], F32R)
        banks = [ctx.enter_context(nc.psum_tensor(f"ff_ps{i}", [P, HALF], F32)) for i in range(8)]
        turn_ps, y_ps = banks[0:4], banks[4:8]

        small_loaded = sem("ff_small_loaded")
        biases_loaded = sem("ff_biases_loaded")
        factors_loaded = [sem(f"ff_factors_loaded{i}") for i in range(KC // 2)]
        acc_loaded = [sem(f"ff_acc_loaded{t}") for t in range(TILES)]
        s_steps = sem("ff_s_steps")
        u_scaled = sem("ff_u_scaled")
        delta_mm = sem("ff_delta_mm")
        delta_ready = sem("ff_delta_ready")
        we_done = sem("ff_we_done")
        we_hi = sem("ff_we_hi")
        we_split = sem("ff_we_split")
        biases_summed = sem("ff_biases_summed")
        acc_ready = sem("ff_acc_ready")
        y_done = sem("ff_y_done")
        y_free = sem("ff_y_free")
        stored = [sem(f"ff_stored{t}") for t in range(TILES)]
        NWE = 2 * KC
        YB = 2 * TILES

        block = ctx.enter_context(nc.Block())

        @block.sync
        def _(sp):
            sp.dma_start(s_sb[:], s_all).then_inc(small_loaded, 16)
            sp.dma_start(ab[:, 0:1], alpha).then_inc(small_loaded, 16)
            sp.dma_start(ab[:, 1:2], beta).then_inc(small_loaded, 16)
            sp.dma_start(small[:, 0:1], s_r).then_inc(small_loaded, 16)
            sp.dma_start(small[:, 1:2], d_r).then_inc(small_loaded, 16)
            sp.dma_start(urT_sb[:], u_rT).then_inc(small_loaded, 16)
            sp.dma_start(vhr_sb[:], vh_r).then_inc(small_loaded, 16)
            sp.dma_start(r_sb[:], r_mat).then_inc(small_loaded, 16)
            for k in range(KC):
                sp.dma_start(uT_sb[:, k], uT[k]).then_inc(factors_loaded[k // 2], 16)
                sp.dma_start(vh_sb[:, k], vh[k]).then_inc(factors_loaded[k // 2], 16)
            sp.dma_start(bo_sb[:], bo).then_inc(biases_loaded, 16)
            sp.dma_start(bias_sb[:], bias).then_inc(biases_loaded, 16)
            for t in range(TILES):
                sp.dma_start(ln.x[:, t], x2[t]).then_inc(ln.loaded[t], 16)

            def load_acc(b, t):
                sp.wait_ge(stored[t], b * 16 + 16)
                sp.dma_start(acc[:, t], tile_of(x2, b * TILES + t)).then_inc(acc_loaded[t], 16)

            def load_next_x(b, t):
                sp.wait_ge(ln.turned, b * ln.GROUPS + (2 * t + 2))
                sp.dma_start(ln.x[:, t], tile_of(x2, b * TILES + (TILES + t))).then_inc(ln.loaded[t], 16)

            with sp.Fori(0, BLOCKS - 1) as b:
                load_acc(b, 0)
                load_acc(b, 1)
                load_next_x(b, 0)
                load_next_x(b, 1)
                load_acc(b, 2)
                load_next_x(b, 2)
                load_next_x(b, 3)
                load_acc(b, 3)
            for t in range(TILES):
                load_acc(BLOCKS - 1, t)

        @block.tensor
        def _(pe):
            pe.wait_ge(s_steps, 5)
            for half in range(2):
                ins = nc.tensor.matmul(banks[half][0:R_INT, :], r_sb[:], urT_sb[:, half * HALF:(half + 1) * HALF],
                                       start=True, stop=True)
            ins.then_inc(delta_mm, 1)
            pe.wait_ge(delta_ready, 1)
            for first in range(0, NWE, 8):
                for k in range(KC + 1):
                    if first == 0 and k < KC:
                        pe.wait_ge(u_scaled, k + 1)
                    for w in range(first, first + 8):
                        ic, half = w // 2, w % 2
                        cols = slice(half * HALF, (half + 1) * HALF)
                        if k == 0 and first:
                            pe.wait_ge(we_split, w - 7)
                        if k < KC:
                            nc.tensor.matmul(banks[w % 8][:], vh_sb[:, k, ic * P:(ic + 1) * P],
                                             uT_sb[:, k, cols], start=(k == 0), stop=False)
                        else:
                            nc.tensor.matmul(banks[w % 8][:], vhr_sb[:, ic * P:(ic + 1) * P], delta[:, cols],
                                             start=False, stop=True).then_inc(we_done, 1)

            def turn(b, *rs):
                for r in rs:
                    if r >= 4:
                        pe.wait_ge(ln.lo_done, b * ln.GROUPS + (r - 3))
                    ln.turn(pe, b, r, ident, turn_ps[r % 4])

            def project(b, t):
                pe.wait_ge(ln.lo_done, b * ln.GROUPS + (2 * t + 2))
                for half in range(2):
                    use = 2 * t + half
                    pe.wait_ge(y_free, b * YB + (use + 1))
                    cols = slice(half * HALF, (half + 1) * HALF)
                    three_passes(nc, y_ps[use % 4][:],
                                 [(ln.xh[:, k, t * P:(t + 1) * P], ln.xl[:, k, t * P:(t + 1) * P],
                                   weh[:, k, cols], wel[:, k, cols]) for k in range(KC)]).then_inc(y_done, 1)

            pe.wait_ge(we_split, NWE - 4)
            turn(0, *range(8))
            pe.wait_ge(we_split, NWE)
            with pe.Fori(0, BLOCKS - 1) as b:
                project(b, 0)
                project(b, 1)
                pe.wait_ge(ln.lo_done, b * ln.GROUPS + ln.GROUPS)
                turn(b + 1, 0, 1)
                project(b, 2)
                turn(b + 1, 2, 3)
                project(b, 3)
                turn(b + 1, 4, 5, 6, 7)
            for t in range(TILES):
                project(BLOCKS - 1, t)

        @block.scalar
        def _(act):
            for t in range(TILES):
                act.sem_inc(stored[t], 16)

            def high_we(w):
                act.wait_ge(we_done, w + 1)
                nc.scalar.activation(weh[:, w // 2, (w % 2) * HALF:(w % 2 + 1) * HALF], banks[w % 8][:],
                                     ACT.Copy).then_inc(we_hi, 1)

            def high(b, *rs):
                for r in rs:
                    ln.high(act, b, r, turn_ps[r % 4])

            def store(b, *ts):
                for t in ts:
                    act.wait_ge(y_free, b * YB + (2 * t + 2 + 4))
                    act.dma_start(tile_of(out, b * TILES + t), acc[:, t]).then_inc(stored[t], 16)

            for w in range(8):
                high_we(w)
            ln.deviations(act, 0)
            for w in range(8, NWE):
                high_we(w)
            high(0, *range(8))
            with act.Fori(0, BLOCKS - 1) as b:
                ln.deviations(act, b + 1)
                high(b + 1, 0, 1)
                store(b, 0, 1)
                high(b + 1, 2, 3)
                store(b, 2)
                high(b + 1, 4, 5, 6, 7)
                store(b, 3)
            store(BLOCKS - 1, *range(TILES))
            for t in range(TILES):
                act.wait_ge(stored[t], 16 + 16 * BLOCKS)

        @block.vector
        def _(dve):
            dve.sem_inc(y_free, 4)
            dve.wait_ge(small_loaded, 8 * 16)
            top = s_sb[0:R_TOP, 0:1]
            nc.vector.tensor_scalar(top, top, ab[:, 0:1], ab[:, 1:2], ALU.mult, ALU.add).then_inc(s_steps, 1)
            dve.wait_ge(s_steps, 1)
            nc.vector.tensor_scalar(top, top, 0.0, None, ALU.max).then_inc(s_steps, 1)
            nc.vector.tensor_scalar(small[:, 1:2], small[:, 1:2], 0.0, None, ALU.max).then_inc(s_steps, 1)
            dve.wait_ge(s_steps, 3)
            nc.vector.tensor_scalar(urT_sb[:], urT_sb[:], small[:, 0:1], None, ALU.mult).then_inc(s_steps, 1)
            dve.wait_ge(s_steps, 4)
            nc.vector.tensor_scalar(urT_sb[:], urT_sb[:], small[:, 1:2], None, ALU.mult).then_inc(s_steps, 1)
            dve.wait_ge(delta_mm, 1)
            for half in range(2):
                ins = nc.vector.tensor_copy(delta[:, half * HALF:(half + 1) * HALF], banks[half][0:R_INT, :])
            ins.then_inc(delta_ready, 1)
            for k in range(KC):
                if k % 2 == 0:
                    dve.wait_ge(factors_loaded[k // 2], 64)
                nc.vector.tensor_scalar(uT_sb[:, k], uT_sb[:, k], s_sb[:, k:k + 1], None, ALU.mult
                                        ).then_inc(u_scaled, 1)

            def low_we(w):
                dve.wait_ge(we_hi, w + 1)
                part = (slice(None), w // 2, slice((w % 2) * HALF, (w % 2 + 1) * HALF))
                nc.vector.tensor_tensor(wel[part], banks[w % 8][:], f32(weh[part]), ALU.subtract
                                        ).then_inc(we_split, 1)

            def low(b, *rs):
                for r in rs:
                    ln.low(dve, b, r, turn_ps[r % 4])

            def add_biases(b, *ts):
                for t in ts:
                    dve.wait_ge(acc_loaded[t], b * 16 + 16)
                    nc.vector.tensor_tensor(acc[:, t], acc[:, t], bias_sb[:], ALU.add).then_inc(acc_ready, 1)

            def add_products(b, *ts):
                for t in ts:
                    dve.wait_ge(acc_ready, b * TILES + (t + 1))
                    for half in range(2):
                        use = 2 * t + half
                        dve.wait_ge(y_done, b * YB + (use + 1))
                        part = acc[:, t, half * HALF:(half + 1) * HALF]
                        nc.vector.tensor_tensor(part, y_ps[use % 4][:], part, ALU.add).then_inc(y_free, 1)

            dve.wait_ge(biases_loaded, 32)
            nc.vector.tensor_tensor(bias_sb[:], bias_sb[:], bo_sb[:], ALU.add).then_inc(biases_summed, 1)
            for w in range(8):
                low_we(w)
            ln.moments(dve, 0)
            ln.normalise(dve, 0)
            for w in range(8, NWE):
                low_we(w)
            low(0, *range(8))
            dve.wait_ge(biases_summed, 1)
            nc.vector.memset(ln.idle[:], 0.0)
            with dve.Fori(0, BLOCKS - 1) as b:
                add_biases(b, 0, 1)
                ln.moments(dve, b + 1)
                ln.normalise(dve, b + 1)
                add_products(b, 0, 1)
                low(b + 1, 0, 1)
                add_biases(b, 2, 3)
                add_products(b, 2)
                low(b + 1, 2, 3)
                add_products(b, 3)
                low(b + 1, 4, 5, 6, 7)
            add_biases(BLOCKS - 1, *range(TILES))
            add_products(BLOCKS - 1, *range(TILES))


def decoder_layer(nc, a, out):
    x1 = nc.dram_tensor("x1", (TOKENS // P, P, D), F32, kind="Internal").ap()
    x2 = nc.dram_tensor("x2", (TOKENS // P, P, D), F32, kind="Internal").ap()
    w_folded = nc.dram_tensor("w_folded", (3 * CH, P, D), F32, kind="Internal").ap()
    with ExitStack() as sems, ExitStack() as ctx:
        def sb(name, shape, stack=ctx):
            return stack.enter_context(nc.sbuf_tensor(name, shape, F32))

        ident = sb("ident", [P, P])
        pairmask = sb("pairmask", [P, 2])
        bias_qkv = sb("bias_qkv", [P, CH, 3])
        eps = sb("eps", [P, 1])
        with ExitStack() as first_phases:
            causal = sb("causal", [P, P], first_phases)
            mix = sb("mix", [P, CH, P], first_phases)
            constants_phase(nc, sems, ident, causal, pairmask, mix, bias_qkv, eps, a["b_nat"],
                            a["inter_rows"], a["amp_col"])
            self_attention_phase(nc, sems, ident, causal, mix, eps, a["x_rows"], a["wqkv"], a["wproj"],
                                 a["w_nat"], w_folded, x1)
        cross_attention_phase(nc, sems, ident, pairmask, bias_qkv, eps, x1, a["ctxT"], w_folded, a["wo"], x2)
        ffn_phase(nc, sems, ident, eps, x2, a["bo"], a["vh"], a["uT"], a["s_all"], a["alpha"], a["beta"],
                  a["u_rT"], a["vh_r"], a["s_r"], a["d_r"], a["r_mat"], a["ffn_bias"], out)


def layouts(i):
    c = np.ascontiguousarray
    g = {}
    g["x_rows"] = c(np.transpose(i["x"], (1, 0, 2))).reshape(TOKENS // P, P, D)
    w = i["L0_attn_weight_qkv"].reshape(KVH, QPG + 2, HD, KC, P)[:, [QPG, QPG + 1] + list(range(QPG))]
    g["wqkv"] = c(np.transpose(w, (0, 1, 4, 3, 2))).reshape(KVH * (QPG + 2), P, D)
    g["wproj"] = c(i["L0_attn_weight_proj"].T).reshape(KVH * QPG, P, D)
    g["w_nat"] = c(np.concatenate([i["L0_xattn_W" + n] for n in "qkv"])).reshape(3 * CH, P, D)
    g["b_nat"] = c(np.stack([i["L0_xattn_b" + n].reshape(CH, P) for n in "qkv"], 2).transpose(1, 0, 2))
    inter = np.repeat(i["L0_xattn_interference"][:, None], DK, axis=1).reshape(CH, P, MS)
    g["inter_rows"] = c(np.transpose(inter, (1, 0, 2)))
    g["amp_col"] = c(np.broadcast_to(i["L0_xattn_amp"].reshape(1, 1), (P, 1)))
    ctx = np.transpose(i["ctx_4096"].reshape(BLOCKS, BT, KC, P), (0, 2, 3, 1))
    g["ctxT"] = c(ctx).reshape(BLOCKS * KC, P, BT)
    wo = i["L0_xattn_Wo"].T.reshape(CH, 2, DK, MS, D)
    g["wo"] = c(np.transpose(wo, (0, 1, 3, 2, 4))).reshape(CH, P, D)
    g["bo"] = c(np.broadcast_to(i["L0_xattn_bo"][None], (P, D)))
    g["vh"] = c(np.concatenate([i["L0_ffn_Vh_top"], i["L0_ffn_Vh_tail"]])).reshape(KC, P, D)
    g["uT"] = c(np.concatenate([i["L0_ffn_U_top"].T, i["L0_ffn_U_tail"].T])).reshape(KC, P, D)
    g["s_all"] = c(np.concatenate([i["L0_ffn_S_top"], i["L0_ffn_S_tail"]]).reshape(KC, P).T)
    g["alpha"] = c(i["L0_ffn_alpha"].reshape(R_TOP, 1))
    g["beta"] = c(i["L0_ffn_beta"].reshape(R_TOP, 1))
    g["u_rT"] = c(i["L0_ffn_U_tail_r"].T)
    g["vh_r"] = c(i["L0_ffn_Vh_tail_r"])
    g["s_r"] = c(i["L0_ffn_S_tail_r"].reshape(R_INT, 1))
    g["d_r"] = c(i["L0_ffn_D"].reshape(R_INT, 1))
    g["r_mat"] = c(i["L0_ffn_R"])
    g["ffn_bias"] = c(np.broadcast_to(i["L0_ffn_bias"][None], (P, D)))
    return g


def kernel(**inputs):
    import concourse.bacc as bacc
    from concourse.bass_utils import run_bass_kernel_spmd

    given = layouts({name: np.asarray(a) for name, a in inputs.items()})
    nc = bacc.Bacc("TRN2", target_bir_lowering=False, num_devices=1, dynamic_dma_scratch_size=1024)
    aps = {name: nc.dram_tensor(f"in_{name}", a.shape, F32, kind="ExternalInput").ap()
           for name, a in given.items()}
    out = nc.dram_tensor("out_x", (TOKENS // P, P, D), F32, kind="ExternalOutput").ap()
    decoder_layer(nc, aps, out)
    r = run_bass_kernel_spmd(nc, [{f"in_{name}": a for name, a in given.items()}], core_ids=[0])
    return r.results[0]["out_x"].reshape(SEQ, TOKENS // SEQ, D)
```
